# Optimizing a Trainium2 kernel written in Bass

```python
import numpy as np
import jax
import jax.numpy as jnp

def _softmax(x, axis=-1):
    return jax.nn.softmax(x, axis=axis)
def _gelu(x):
    return jax.nn.gelu(x, approximate=True)
def _silu(x):
    return jax.nn.silu(x)
def _sigmoid(x):
    return jax.nn.sigmoid(x)
def _layernorm(x, axis=-1, eps=1e-5):
    m = jnp.mean(x, axis=axis, keepdims=True)
    v = jnp.var(x, axis=axis, keepdims=True)
    return (x - m) / jnp.sqrt(v + eps)
def _scatter_add(tgt, idx, src, axis=0):
    return tgt.at[idx].add(src)
def _segment_sum(src, seg, n):
    return jax.ops.segment_sum(src, seg, n)

kernel_name = 'mk_vit_tower_postln_d1_tok_img256_181cae'

def setup_inputs(seed: int = 0):
    np.random.seed(seed)
    _w = jnp.asarray
    def _rec_inputs():
        import jax
        import jax.numpy as jnp
        _rk = jax.random.key(seed)
        x = (-0.000125008 + 0.999885 * jax.random.normal(jax.random.fold_in(_rk, 1), (32, 256, 64, 64), jnp.float32))
        return x
    x = _rec_inputs()
    def _L0_tok_setup():
        import jax, jax.numpy as jnp
        import numpy as np
        B, C, H, W = (32, 256, 64, 64)
        STRIDE, HEADS = (4, 8)

        def _ln(x, w, b):
            mu = x.mean(-1, keepdims=True)
            var = ((x - mu) ** 2).mean(-1, keepdims=True)
            return (x - mu) * jax.lax.rsqrt(var + 1e-05) * w + b
        key = jax.random.key(seed)
        ks = jax.random.split(key, 4)
        return {'features': jax.random.normal(ks[0], (B, C, H, W), dtype=jnp.float32), 'ln_q_w': jnp.ones((C,), jnp.float32), 'ln_q_b': jnp.zeros((C,), jnp.float32), 'Wq': jax.random.normal(ks[1], (C, C), dtype=jnp.float32) * 0.02, 'ln_kv_w': jnp.ones((C,), jnp.float32), 'ln_kv_b': jnp.zeros((C,), jnp.float32), 'Wkv': jax.random.normal(ks[2], (2 * C, C), dtype=jnp.float32) * 0.02, 'proj_w': jax.random.normal(ks[3], (C, C), dtype=jnp.float32) * 0.02, 'proj_b': jnp.zeros((C,), jnp.float32), 'conv_stride': STRIDE, 'num_heads': HEADS}
    _L0_tok_all = _L0_tok_setup()
    _L0_tok_in = {k: v for k, v in _L0_tok_all.items() if k in ('ln_q_w', 'ln_q_b', 'Wq', 'ln_kv_w', 'ln_kv_b', 'Wkv', 'proj_w', 'proj_b', )}
    del _L0_tok_all

    def _L0_attn_setup():
        import jax, jax.numpy as jnp
        import numpy as np
        H, D = (8, 32)
        EPS = 1e-05
        key = jax.random.key(seed)
        ks = jax.random.split(key, 4)
        B, N, C = (2, 2048, 256)
        inner = H * D
        return {'node_features': jax.random.normal(ks[0], (B, N, C), jnp.float32), 'ln_gamma': jnp.ones((C,), jnp.float32), 'ln_beta': jnp.zeros((C,), jnp.float32), 'W_qkv': jax.random.normal(ks[1], (3 * inner, C), jnp.float32) * 0.02, 'W_gate': jax.random.normal(ks[2], (inner, C), jnp.float32) * 0.02, 'b_gate': jnp.ones((inner,), jnp.float32), 'W_final': jax.random.normal(ks[3], (C, inner), jnp.float32) * 0.02, 'b_final': jnp.zeros((C,), jnp.float32)}
    _L0_attn_all = _L0_attn_setup()
    _L0_attn_in = {k: v for k, v in _L0_attn_all.items() if k in ('ln_gamma', 'ln_beta', 'W_qkv', 'W_gate', 'b_gate', 'W_final', 'b_final', )}
    del _L0_attn_all

    def _L0_ffn_setup():
        import jax, jax.numpy as jnp
        import numpy as np
        E, D, H, TOP_K = (6, 256, 256, 2)
        ROUTER_H = D // 2
        key = jax.random.key(seed)
        ks = jax.random.split(key, 12)
        s = 1.0 / np.sqrt(D)
        sh = 1.0 / np.sqrt(H)
        sr = 1.0 / np.sqrt(ROUTER_H)
        return {'features': jax.random.normal(ks[0], (8, 4096, D), dtype=jnp.float32), 'router_w1': jax.random.uniform(ks[1], (D, ROUTER_H), jnp.float32, -s, s), 'router_b1': jnp.zeros((ROUTER_H,), jnp.float32), 'router_w2': jax.random.uniform(ks[2], (ROUTER_H, E), jnp.float32, -sr, sr), 'router_b2': jnp.zeros((E,), jnp.float32), 'expert_w1': jax.random.uniform(ks[3], (E, D, H), jnp.float32, -s, s), 'expert_b1': jnp.zeros((E, H), jnp.float32), 'expert_w2': jax.random.uniform(ks[4], (E, H, H), jnp.float32, -sh, sh), 'expert_b2': jnp.zeros((E, H), jnp.float32), 'expert_w3': jax.random.uniform(ks[5], (E, H, D), jnp.float32, -sh, sh), 'expert_b3': jnp.zeros((E, D), jnp.float32)}
    _L0_ffn_all = _L0_ffn_setup()
    _L0_ffn_in = {k: v for k, v in _L0_ffn_all.items() if k in ('router_w1', 'router_b1', 'router_w2', 'router_b2', 'expert_w1', 'expert_b1', 'expert_w2', 'expert_b2', 'expert_w3', 'expert_b3', )}
    del _L0_ffn_all

    return {
        "x": x,
        "L0_tok_ln_q_w": _L0_tok_in["ln_q_w"],
        "L0_tok_ln_q_b": _L0_tok_in["ln_q_b"],
        "L0_tok_Wq": _L0_tok_in["Wq"],
        "L0_tok_ln_kv_w": _L0_tok_in["ln_kv_w"],
        "L0_tok_ln_kv_b": _L0_tok_in["ln_kv_b"],
        "L0_tok_Wkv": _L0_tok_in["Wkv"],
        "L0_tok_proj_w": _L0_tok_in["proj_w"],
        "L0_tok_proj_b": _L0_tok_in["proj_b"],
        "L0_attn_ln_gamma": _L0_attn_in["ln_gamma"],
        "L0_attn_ln_beta": _L0_attn_in["ln_beta"],
        "L0_attn_W_qkv": _L0_attn_in["W_qkv"],
        "L0_attn_W_gate": _L0_attn_in["W_gate"],
        "L0_attn_b_gate": _L0_attn_in["b_gate"],
        "L0_attn_W_final": _L0_attn_in["W_final"],
        "L0_attn_b_final": _L0_attn_in["b_final"],
        "L0_ffn_router_w1": _L0_ffn_in["router_w1"],
        "L0_ffn_router_b1": _L0_ffn_in["router_b1"],
        "L0_ffn_router_w2": _L0_ffn_in["router_w2"],
        "L0_ffn_router_b2": _L0_ffn_in["router_b2"],
        "L0_ffn_expert_w1": _L0_ffn_in["expert_w1"],
        "L0_ffn_expert_b1": _L0_ffn_in["expert_b1"],
        "L0_ffn_expert_w2": _L0_ffn_in["expert_w2"],
        "L0_ffn_expert_b2": _L0_ffn_in["expert_b2"],
        "L0_ffn_expert_w3": _L0_ffn_in["expert_w3"],
        "L0_ffn_expert_b3": _L0_ffn_in["expert_b3"],
    }

def reference(x, L0_tok_ln_q_w, L0_tok_ln_q_b, L0_tok_Wq, L0_tok_ln_kv_w, L0_tok_ln_kv_b, L0_tok_Wkv, L0_tok_proj_w, L0_tok_proj_b, L0_attn_ln_gamma, L0_attn_ln_beta, L0_attn_W_qkv, L0_attn_W_gate, L0_attn_b_gate, L0_attn_W_final, L0_attn_b_final, L0_ffn_router_w1, L0_ffn_router_b1, L0_ffn_router_w2, L0_ffn_router_b2, L0_ffn_expert_w1, L0_ffn_expert_b1, L0_ffn_expert_w2, L0_ffn_expert_b2, L0_ffn_expert_w3, L0_ffn_expert_b3):
    import jax
    import jax.numpy as jnp
    def _L0_tok_ref(features, ln_q_w, ln_q_b, Wq, ln_kv_w, ln_kv_b, Wkv, proj_w, proj_b, conv_stride, num_heads):
        import jax, jax.numpy as jnp
        import numpy as np
        B, C, H, W = (32, 256, 64, 64)
        STRIDE, HEADS = (4, 8)

        def _ln(x, w, b):
            mu = x.mean(-1, keepdims=True)
            var = ((x - mu) ** 2).mean(-1, keepdims=True)
            return (x - mu) * jax.lax.rsqrt(var + 1e-05) * w + b
        s = conv_stride
        b, c, hh, ww = features.shape
        h, w = (hh // s, ww // s)
        hw, n, d = (h * w, s * s, c // num_heads)
        scale = c ** (-0.5)
        x = features.reshape(b, c, h, s, w, s)
        reduce_feats = x.mean((3, 5)).reshape(b, c, hw).transpose(0, 2, 1)
        unf = x.transpose(0, 1, 2, 4, 3, 5).reshape(b, c, hw, n).transpose(0, 2, 3, 1)
        q = _ln(reduce_feats, ln_q_w, ln_q_b) @ Wq.T
        q = q.reshape(b, hw, num_heads, d).transpose(0, 2, 1, 3)
        kv = _ln(unf, ln_kv_w, ln_kv_b) @ Wkv.T
        kv = kv.reshape(b, hw, n, 2, num_heads, d).transpose(3, 0, 4, 1, 2, 5)
        k, v = (kv[0], kv[1])
        attn = jax.nn.softmax(jnp.einsum('bhpd,bhpnd->bhpn', q * scale, k), axis=-1)
        aggre = jnp.einsum('bhpn,bhpnd->bhpd', attn, v)
        aggre = aggre.transpose(0, 2, 1, 3).reshape(b, hw, c)
        return reduce_feats + aggre @ proj_w.T + proj_b

    def _L0_attn_ref(node_features, ln_gamma, ln_beta, W_qkv, W_gate, b_gate, W_final, b_final):
        import jax, jax.numpy as jnp
        import numpy as np
        H, D = (8, 32)
        EPS = 1e-05
        x = node_features
        B, N, _ = x.shape
        mu = jnp.mean(x, axis=-1, keepdims=True)
        var = jnp.mean(jnp.square(x - mu), axis=-1, keepdims=True)
        normed = (x - mu) / jnp.sqrt(var + EPS) * ln_gamma + ln_beta
        qkv = normed @ W_qkv.T
        q, k, v = jnp.split(qkv, 3, axis=-1)

        def to_heads(t):
            return t.reshape(B, N, H, D).transpose(0, 2, 1, 3)
        q, k, v = (to_heads(q), to_heads(k), to_heads(v))
        gate = jax.nn.sigmoid(to_heads(x @ W_gate.T + b_gate))
        scores = jnp.einsum('bhid,bhjd->bhij', q, k) * D ** (-0.5)
        attn = jax.nn.softmax(scores, axis=-1)
        out = jnp.einsum('bhij,bhid->bhjd', attn, v) * gate
        out = out.transpose(0, 2, 1, 3).reshape(B, N, H * D)
        return x + out @ W_final.T + b_final

    def _L0_ffn_ref(features, router_w1, router_b1, router_w2, router_b2, expert_w1, expert_b1, expert_w2, expert_b2, expert_w3, expert_b3):
        import jax, jax.numpy as jnp
        import numpy as np
        E, D, H, TOP_K = (6, 256, 256, 2)
        ROUTER_H = D // 2
        rh = jax.nn.relu(features @ router_w1 + router_b1)
        expert_logits = jax.nn.softmax(rh @ router_w2 + router_b2, axis=-1)
        top_w, top_i = jax.lax.top_k(expert_logits, TOP_K)
        routing_weights = jax.nn.softmax(top_w, axis=-1)
        h1 = jax.nn.relu(jnp.einsum('bsd,edh->bseh', features, expert_w1) + expert_b1)
        h2 = jax.nn.relu(jnp.einsum('bseh,ehf->bsef', h1, expert_w2) + expert_b2)
        expert_out = jnp.einsum('bsef,efo->bseo', h2, expert_w3) + expert_b3
        sel = jnp.take_along_axis(expert_out, top_i[:, :, :, None], axis=2)
        combined = jnp.sum(sel * routing_weights[..., None], axis=2)
        return combined

    h = _L0_tok_ref(x, L0_tok_ln_q_w, L0_tok_ln_q_b, L0_tok_Wq, L0_tok_ln_kv_w, L0_tok_ln_kv_b, L0_tok_Wkv, L0_tok_proj_w, L0_tok_proj_b, 4, 8)
    h = _layernorm(h + _L0_attn_ref(h, L0_attn_ln_gamma, L0_attn_ln_beta, L0_attn_W_qkv, L0_attn_W_gate, L0_attn_b_gate, L0_attn_W_final, L0_attn_b_final), axis=-1)
    h = _layernorm(h + _L0_ffn_ref(h, L0_ffn_router_w1, L0_ffn_router_b1, L0_ffn_router_w2, L0_ffn_router_b2, L0_ffn_expert_w1, L0_ffn_expert_b1, L0_ffn_expert_w2, L0_ffn_expert_b2, L0_ffn_expert_w3, L0_ffn_expert_b3), axis=-1)
    return h


_drawn_inputs = setup_inputs


def setup_inputs(seed=0):
    import zlib

    import numpy as np

    out = dict(_drawn_inputs(seed))
    spreads = {'L0_tok_ln_q_w': (1.0, 0.6),
     'L0_tok_ln_q_b': (0.0, 0.8),
     'L0_tok_ln_kv_w': (1.0, 0.6),
     'L0_tok_ln_kv_b': (0.0, 0.1),
     'L0_tok_proj_b': (0.0, 0.1),
     'L0_attn_ln_gamma': (1.0, 0.6),
     'L0_attn_ln_beta': (0.0, 0.442),
     'L0_attn_b_gate': (1.0, 0.6),
     'L0_attn_b_final': (0.0, 0.1),
     'L0_ffn_router_b1': (0.0, 0.1),
     'L0_ffn_router_b2': (0.0, 0.1),
     'L0_ffn_expert_b1': (0.0, 0.705),
     'L0_ffn_expert_b2': (0.0, 0.293),
     'L0_ffn_expert_b3': (0.0, 0.1)}
    factors = {'L0_tok_Wq': 8.0, 'L0_attn_W_gate': 8.0}
    for name, (base, spread) in spreads.items():
        noise = np.random.default_rng([zlib.crc32(name.encode()), seed]).standard_normal(out[name].shape)
        drawn = base * np.exp(spread * noise) if base else spread * noise
        out[name] = jnp.asarray(drawn.astype(out[name].dtype))
    for name, factor in factors.items():
        out[name] = (out[name] * factor).astype(out[name].dtype)
    return out
```

```python
from contextlib import ExitStack

import concourse.bass as bass
from concourse import mybir

F32 = mybir.dt.float32
ALU = mybir.AluOpType
ACT = mybir.ActivationFunctionType
AX = mybir.AxisListType

P = 128
STRIDE = 4
HEADS = 8
EPS = 1e-5
EXPERTS = 6
VECS = ["L0_tok_ln_q_w", "L0_tok_ln_q_b", "L0_tok_ln_kv_w", "L0_tok_ln_kv_b", "L0_tok_proj_b",
        "L0_attn_ln_gamma", "L0_attn_ln_beta", "L0_attn_b_gate", "L0_attn_b_final"]
QW, QB, KVW, KVB, PB, GAMMA, BETA, BGATE, BFINAL = range(len(VECS))


def build(nc, x, wq_t, wkv, proj_t, wqkv_t, wgate_t, wfinal_t, vecs, ident_in, masks_in,
          rw1, rb1, rw2, rb2, ew1, eb1, ew2, eb2, ew3, eb3, out):
    NB, C, LOC, N2 = x.shape
    CH = C // P
    PIX = LOC * N2
    LH = LOC // P
    D = C // HEADS
    HPC = P // D
    GROUPS = PIX // P
    LPG = LOC // GROUPS
    QUARTERS = 4
    GPQ = GROUPS // QUARTERS
    PAIRS = GROUPS // 2
    SH = LPG * HEADS
    assert C == 256 and LOC == 256 and GROUPS == 32 and SH == 64 and NB >= 3

    h1_dram = nc.dram_tensor("h1_scratch", (NB * LOC, C), F32, kind="Internal").ap()

    def at(index, per, n):
        return index * per + n

    def wait(eng, sem, value):
        if not (isinstance(value, int) and value <= 0):
            eng.wait_ge(sem, value)

    class Steps:
        def __init__(self, eng, signal, per):
            self.eng, self.counted, self.per = eng, signal, per

        def start(self, index):
            self.index, self.n = index, 0

        def __call__(self, ins):
            self.n += 1
            ins.then_inc(self.counted, 1)
            self.eng.wait_ge(self.counted, at(self.index, self.per, self.n))

        def finish(self):
            assert self.n == self.per, self.n

    def layer_stats(dve, src, n, tmp, mean_var, step, signal):
        for l in range(n):
            last = dve.bn_stats(tmp[:, l, 0:6], src[:, l, :])
        step(last)
        diff, squares = tmp[:, 0:n, 6], tmp[:, 0:n, 7]
        dve.tensor_tensor(squares, tmp[:, 0:n, 2], tmp[:, 0:n, 5], ALU.add)
        step(dve.tensor_tensor(diff, tmp[:, 0:n, 1], tmp[:, 0:n, 4], ALU.subtract))
        dve.scalar_tensor_tensor(mean_var[:, :, 0], diff, 0.5, tmp[:, 0:n, 4], ALU.mult, ALU.add)
        step(dve.scalar_tensor_tensor(mean_var[:, :, 1], diff, C / 4.0, diff, ALU.mult, ALU.mult))
        step(dve.tensor_tensor(squares, squares, mean_var[:, :, 1], ALU.add))
        dve.tensor_scalar(mean_var[:, :, 1], squares, 1.0 / C, EPS, ALU.mult, ALU.add).then_inc(signal, 1)

    with ExitStack() as whole:
        def sem(name):
            return whole.enter_context(nc.semaphore(name))

        setup_loads = sem("setup_loads")
        x_loaded = [sem(f"x_loaded{q}") for q in range(QUARTERS)]
        h1_stored = sem("h1_stored")
        su_v, su_p, su_a = sem("setup_vector"), sem("setup_tensor"), sem("setup_scalar")
        setup_done = sem("setup_done")
        feats_summed = sem("feats_summed")
        r_turned, r_taken, r_var, r_rstd = sem("r_turned"), sem("r_taken"), sem("r_var"), sem("r_rstd")
        rb_ready = sem("rb_ready")
        qn_ready, qn_turned, qn_taken = sem("qn_ready"), sem("qn_turned"), sem("qn_taken")
        q_made, q_taken = sem("q_made"), sem("q_taken")
        g_made, g_taken_act, g_taken_dve = sem("g_made"), sem("g_taken_act"), sem("g_taken_dve")
        xt_made, xt_taken, stats_done = sem("xt_made"), sem("xt_taken"), sem("stats_done")
        s_made, s_taken = sem("s_made"), sem("s_taken")
        pix_var, pix_rstd = sem("pix_var"), sem("pix_rstd")
        e_ready, e_turned, e_shifted, e_exped = sem("e_ready"), sem("e_turned"), sem("e_shifted"), sem("e_exped")
        p_ready, p_turned, p_taken, p_spread = sem("p_ready"), sem("p_turned"), sem("p_taken"), sem("p_spread")
        z_made, z_taken_act, z_taken_dve = sem("z_made"), sem("z_taken_act"), sem("z_taken_dve")
        agg_made, agg_taken = sem("agg_made"), sem("agg_taken")
        proj_made, h0_ready = sem("proj_made"), sem("h0_ready")
        t_chain = sem("tokenizer_vector_steps")
        h0_var, h0_rstd, h0_twice = sem("h0_var"), sem("h0_rstd"), sem("h0_twice")
        pool_t_chain = sem("tokenizer_pool_steps")
        h_turned, h_taken = sem("h_turned"), sem("h_taken")
        n_ready, n_turned, n_taken = sem("n_ready"), sem("n_turned"), sem("n_taken")
        aq_made, aq_taken, ak_made, ak_taken = sem("aq_made"), sem("aq_taken"), sem("ak_made"), sem("ak_taken")
        av_made, av_taken = sem("av_made"), sem("av_taken")
        gate_made, gate_exped, gate_ready = sem("gate_made"), sem("gate_exped"), sem("gate_ready")
        as_made, as_max, as_exped = sem("as_made"), sem("as_max"), sem("as_exped")
        vs_ready = sem("vs_ready")
        ao_made, ao_taken = sem("ao_made"), sem("ao_taken")
        fin_made, u_var, u_rstd, h1_ready = sem("fin_made"), sem("u_var"), sem("u_rstd"), sem("h1_ready")
        a_chain = sem("attention_vector_steps")

        banks = [whole.enter_context(nc.psum_tensor(f"bank{i}", [P, 512], F32)) for i in range(8)]

        def sb(stack, name, *shape):
            return stack.enter_context(nc.sbuf_tensor(name, [P, *shape], F32))

        ident = sb(whole, "ident", P)
        halves = sb(whole, "minus_half", GROUPS)

        def halved(bank):
            return banks[bank][:, :].rearrange("p (a b) -> p a b", a=2)

        with ExitStack() as one:
            X = sb(one, "x_image", CH, PIX)
            XT = sb(one, "x_turned", GROUPS, C)
            G = sb(one, "score_weights", CH, LOC, HEADS)
            A = sb(one, "attn_spread", GROUPS, LPG, HEADS)
            Z = sb(one, "pooled_pixels", CH, HEADS, LOC)
            WQ, WKm, WVm = sb(one, "wq", CH, C), sb(one, "wk_masked", HEADS, C), sb(one, "wv_masked", CH, HEADS, P)
            PW, WA = sb(one, "w_proj", CH, C), sb(one, "w_qkv", CH, 3 * C)
            WG, WF = sb(one, "w_gate", CH, C), sb(one, "w_final", CH, C)
            pixmask = sb(one, "pixel_token_mask", SH)
            headmask = sb(one, "head_mask", HPC)
            qscale = sb(one, "head_mask_scaled", HPC)
            vcol = sb(one, "vectors_cols", len(VECS), CH)
            pb_row, vb_row, bf_row = sb(one, "proj_b_row", C), sb(one, "v_bias_row", C), sb(one, "b_final_row", C)
            bq_col, bqm, bk_col, nbg = sb(one, "bq_col", CH), sb(one, "bq_masked", HEADS), sb(one, "bk_col", CH), sb(one, "gate_b_negated", CH)
            R = sb(one, "feats", CH, LOC)
            RT, RTB = sb(one, "feats_turned", LH, C), sb(one, "feats_plus_bias", LH, C)
            QNT, QN, Q = sb(one, "qn_tokens", LH, C), sb(one, "qn", CH, LOC), sb(one, "q", CH, LOC)
            bnt, mv, rstd2 = sb(one, "bn_tmp", LH, 8), sb(one, "mean_var", LH, 2), sb(one, "rstd2", LH)
            st, vt, RS = sb(one, "bn_pixels", GROUPS, 6), sb(one, "var_pixels", 2, GROUPS), sb(one, "rstd_pixels", GROUPS)
            SM, E = sb(one, "scores_masked", GPQ, SH), sb(one, "scores", GROUPS, HEADS)
            mx, den = sb(one, "softmax_max", 2 * LPG), sb(one, "softmax_sum", 2 * LPG)
            PE_, PR = sb(one, "softmax_exp", 2 * LPG, N2), sb(one, "attn_scaled", GROUPS, HEADS)
            AG = QN
            H0, H2 = sb(one, "h0", LH, C), sb(one, "h0_twice_b", LH, C)
            amv, arstd = sb(one, "mean_var_attn", LH, 2), sb(one, "rstd_attn", LH)
            NH, NT, HT = sb(one, "normed", LH, C), sb(one, "normed_turned", CH, LOC), sb(one, "h0_turned", CH, LOC)
            QM, K = sb(one, "q_masked", HEADS, LOC), sb(one, "k", CH, LOC)
            V, VS = sb(one, "v", LH, HEADS, D), sb(one, "v_scaled_masked", LH, HEADS, P)
            GT = sb(one, "gate", CH, LOC)
            EX = sb(one, "attn_exp", HEADS, LH, LOC)
            nmax, esum = sb(one, "minus_max", HEADS, LH), sb(one, "exp_sum", HEADS, LH)
            O, U = GT, H2
            H1 = sb(one, "h1", LH, C)
            bmv, brstd = sb(one, "mean_var_out", LH, 2), sb(one, "rstd_out", LH)

            def stage(start, width, chunks=CH):
                return XT[:, :, :].rearrange("p a b -> p (a b)")[:, start:start + chunks * width].rearrange(
                    "p (c w) -> p c w", c=chunks)

            raw_wq, raw_wk, raw_wv = stage(0, C), stage(512, C), stage(1024, C)
            raw_wqkv = stage(1536, 3 * C)
            row_w, row_b = stage(3072, C, 1)[:, 0, :], stage(3328, C, 1)[:, 0, :]
            beta_wide, bv_wide = stage(3584, P), stage(3840, P)
            wtmp = stage(4096, C)
            wmean = stage(4608, 1)
            bv_col = stage(4612, 1)
            ones = stage(4736, P, 1)[:, 0, :]
            pb_raw = stage(4864, C, 1)[:, 0, :]

            x_img = x.rearrange("b (c p) l n -> b p c (l n)", p=P)
            h1_img = h1_dram.rearrange("(b h p) c -> b p h c", h=LH, p=P)
            QP = PIX // QUARTERS

            def halves_of(w):
                return w.rearrange("(c p) n -> p c n", p=P)

            block = one.enter_context(nc.Block())

            @block.sync
            def _(sp):
                def load_quarter(t, q):
                    wait(sp, s_made, at(t, QUARTERS, q + 1 - QUARTERS))
                    wait(sp, feats_summed, at(t, 1, 0))
                    sp.dma_start(X[:, :, q * QP:(q + 1) * QP],
                                 x_img[t, :, :, q * QP:(q + 1) * QP]).then_inc(x_loaded[q], 16)

                def store_h1(a):
                    wait(sp, h1_ready, at(a, 1, 1))
                    sp.dma_start(h1_img[a], H1[:, :, :]).then_inc(h1_stored, 16)

                setup = [
                    (raw_wq, halves_of(wq_t)), (raw_wk, halves_of(wkv[0:C, :])), (raw_wv, halves_of(wkv[C:2 * C, :])),
                    (raw_wqkv, halves_of(wqkv_t)), (PW[:, :, :], halves_of(proj_t)), (WG[:, :, :], halves_of(wgate_t)),
                    (WF[:, :, :], halves_of(wfinal_t)), (ident[:, :], ident_in),
                    (pixmask[:, :], masks_in[:, 0:SH]), (headmask[:, :], masks_in[:, SH:SH + HPC]),
                    (row_w, vecs[KVW, :].partition_broadcast(P)), (row_b, vecs[KVB, :].partition_broadcast(P)),
                    (pb_raw, vecs[PB, :].partition_broadcast(P)), (bf_row[:, :], vecs[BFINAL, :].partition_broadcast(P)),
                ]
                for dst, src in setup:
                    sp.dma_start(dst, src).then_inc(setup_loads, 16)
                with nc.allow_non_contiguous_dma(reason="a few hundred values, once"):
                    for v in range(len(VECS)):
                        sp.dma_start(vcol[:, v, :], vecs[v, :].rearrange("(c p) -> p c", p=P),
                                     allow_slow_non_contiguous=True).then_inc(setup_loads, 16)
                for q in range(QUARTERS):
                    load_quarter(0, q)
                for q in range(QUARTERS):
                    load_quarter(1, q)
                for q in range(QUARTERS):
                    load_quarter(2, q)
                store_h1(0)
                with sp.Fori(3, NB) as t:
                    for q in range(QUARTERS):
                        load_quarter(t, q)
                    store_h1(t - 2)
                store_h1(NB - 2)
                store_h1(NB - 1)
                sp.wait_ge(h1_stored, 16 * NB)

            SETUP_LOADS = 16 * (14 + len(VECS))

            @block.tensor
            def _(pe):
                mm = pe.matmul

                pe.wait_ge(setup_loads, SETUP_LOADS)
                for m in range(CH):
                    for c in range(CH):
                        mm(banks[0][:, m:m + 1], raw_wq[:, c, m * P:(m + 1) * P], vcol[:, QB, c:c + 1],
                           start=(c == 0), stop=(c == CH - 1)).then_inc(su_p, 1)
                for m in range(2 * CH):
                    for c in range(CH):
                        mm(banks[1][:, m:m + 1], raw_wqkv[:, c, m * P:(m + 1) * P], vcol[:, BETA, c:c + 1],
                           start=(c == 0), stop=(c == CH - 1)).then_inc(su_p, 1)
                pe.wait_ge(su_v, 9)
                for c in range(CH):
                    mm(banks[2][:, 0:C], beta_wide[:, c, :], raw_wqkv[:, c, 2 * C:3 * C],
                       start=(c == 0), stop=(c == CH - 1)).then_inc(su_p, 1)
                for c in range(CH):
                    mm(banks[3][:, 0:C], bv_wide[:, c, :], PW[:, c, :],
                       start=(c == 0), stop=(c == CH - 1)).then_inc(su_p, 1)
                pe.wait_ge(su_v, 15)
                for c in range(CH):
                    for m in range(CH):
                        pe.transpose(halved(4)[:, c, m * P:(m + 1) * P], wtmp[:, m, c * P:(c + 1) * P],
                                     ident[:, :]).then_inc(su_p, 1)
                pe.wait_ge(setup_done, 1)

                def turn_feats(t):
                    wait(pe, feats_summed, at(t, 1, 1))
                    wait(pe, h0_ready, at(t, 1, 0))
                    for l in range(LH):
                        for c in range(CH):
                            last = pe.transpose(halved(4)[:, l, c * P:(c + 1) * P], R[:, c, l * P:(l + 1) * P], ident[:, :])
                    last.then_inc(r_turned, 1)

                def turn_qn(t):
                    wait(pe, qn_ready, at(t, 1, 1))
                    for c in range(CH):
                        for l in range(LH):
                            last = pe.transpose(halved(4)[:, c, l * P:(l + 1) * P], QNT[:, l, c * P:(c + 1) * P], ident[:, :])
                    last.then_inc(qn_turned, 1)

                def make_q(t):
                    wait(pe, qn_taken, at(t, 1, 1))
                    for m in range(CH):
                        for c in range(CH):
                            last = mm(halved(4)[:, m, :], WQ[:, c, m * P:(m + 1) * P], QN[:, c, :],
                                      start=(c == 0), stop=(c == CH - 1))
                    last.then_inc(q_made, 1)

                def make_g(t):
                    wait(pe, q_taken, at(t, 2, 2))
                    for i in range(HEADS):
                        pair, c = i // CH, i % CH
                        if i >= 2:
                            wait(pe, (g_taken_act, g_taken_dve)[i % 2], at(t, HEADS // 2, i // 2))
                        else:
                            wait(pe, (z_taken_act, z_taken_dve)[i % 2], at(t, HEADS // 2, 0))
                        for j in range(2):
                            h = 2 * pair + j
                            last = mm(halved(i % 2)[:, j, :], WKm[:, h, c * P:(c + 1) * P], Q[:, h // HPC, :],
                                      start=True, stop=True)
                        last.then_inc(g_made, 1)

                def pixels(c, g):
                    return X[:, c, g * P:(g + 1) * P]

                def turn_pair(t, p):
                    if p % (PAIRS // QUARTERS) == 0:
                        q = p // (PAIRS // QUARTERS)
                        wait(pe, x_loaded[q], at(t, 16, 16))
                    if p >= 2:
                        wait(pe, xt_taken, at(t, PAIRS, p - 1))
                    elif p == 0:
                        wait(pe, g_taken_act, at(t, HEADS // 2, HEADS // 2))
                        wait(pe, g_taken_dve, at(t, HEADS // 2, HEADS // 2))
                    for j in range(2):
                        for c in range(CH):
                            last = pe.transpose(halved(p % 2)[:, j, c * P:(c + 1) * P], pixels(c, 2 * p + j), ident[:, :])
                    last.then_inc(xt_made, 1)

                def score_pair(t, p):
                    ppq = PAIRS // QUARTERS
                    q = p // ppq
                    if p % ppq == 0:
                        wait(pe, s_taken, at(t, QUARTERS, q - 1))
                    for j in range(2):
                        g = 2 * p + j
                        for c in range(CH):
                            last = mm(banks[2 + q % 2][:, (g % GPQ) * SH:(g % GPQ + 1) * SH], pixels(c, g),
                                      G[:, c, g * LPG:(g + 1) * LPG, :], start=(c == 0), stop=(c == CH - 1))
                    if p % ppq == ppq - 1:
                        last.then_inc(s_made, 1)

                def turn_scores(t):
                    wait(pe, e_ready, at(t, 1, 1))
                    Ev = E[:, :, :].rearrange("p (u g) h -> p u (g h)", u=2)
                    for u in range(2):
                        last = pe.transpose(banks[4][:, u * P:(u + 1) * P], Ev[:, u, :], ident[:, :])
                    last.then_inc(e_turned, 1)

                def turn_probs(t):
                    wait(pe, p_ready, at(t, 1, 1))
                    for u in range(2):
                        last = pe.transpose(banks[4][:, u * P:(u + 1) * P], PE_[:, u * LPG:(u + 1) * LPG, :], ident[:, :])
                    last.then_inc(p_turned, 1)

                def pool_pixels(t):
                    for i in range(2 * QUARTERS):
                        q, c = i // CH, i % CH
                        if c == 0:
                            wait(pe, p_spread, at(t, QUARTERS, q + 1))
                        if i >= 2:
                            wait(pe, (z_taken_act, z_taken_dve)[i % 2], at(t, QUARTERS, i // 2))
                        elif i == 0:
                            wait(pe, xt_taken, at(t, PAIRS, PAIRS))
                        for g in range(q * GPQ, (q + 1) * GPQ):
                            last = mm(banks[i % 2][:, (g % GPQ) * SH:(g % GPQ + 1) * SH], XT[:, g, c * P:(c + 1) * P],
                                      A[:, g, :, :], start=True, stop=True)
                        last.then_inc(z_made, 1)

                def aggregate(t):
                    wait(pe, z_taken_act, at(t, QUARTERS, QUARTERS))
                    wait(pe, z_taken_dve, at(t, QUARTERS, QUARTERS))
                    for m in range(CH):
                        for j in range(HPC):
                            for c in range(CH):
                                last = mm(halved(4)[:, m, :], WVm[:, c, m * HPC + j, :], Z[:, c, m * HPC + j, :],
                                          start=(j == 0 and c == 0), stop=(j == HPC - 1 and c == CH - 1))
                    last.then_inc(agg_made, 1)

                def project(t):
                    wait(pe, agg_taken, at(t, 1, 1))
                    for l in range(LH):
                        for c in range(CH):
                            last = mm(halved(4)[:, l, :], AG[:, c, l * P:(l + 1) * P], PW[:, c, :],
                                      start=(c == 0), stop=(c == CH - 1))
                    last.then_inc(proj_made, 1)

                def turn_tokens(a, src, ready, turned):
                    for c in range(CH):
                        for l in range(LH):
                            last = pe.transpose(halved(5)[:, c, l * P:(l + 1) * P], src[:, l, c * P:(c + 1) * P], ident[:, :])
                    last.then_inc(turned, 1)

                def turn_h0(a):
                    wait(pe, h0_ready, at(a, 1, 1))
                    wait(pe, u_var, at(a, 1, 0))
                    turn_tokens(a, H0, h0_ready, h_turned)

                def turn_n(a):
                    wait(pe, n_ready, at(a, 1, 1))
                    wait(pe, h_taken, at(a, 1, 1))
                    turn_tokens(a, NH, n_ready, n_turned)

                def rows_of(a, w, first, src, made):
                    for m in range(CH):
                        for c in range(CH):
                            last = mm(halved(5)[:, m, :], w[:, c, first + m * P:first + (m + 1) * P], src[:, c, :],
                                      start=(c == 0), stop=(c == CH - 1))
                    last.then_inc(made, 1)

                def tokens_of(w, first, src, made):
                    for l in range(LH):
                        for c in range(CH):
                            last = mm(halved(5)[:, l, :], src[:, c, l * P:(l + 1) * P], w[:, c, first:first + C],
                                      start=(c == 0), stop=(c == CH - 1))
                    last.then_inc(made, 1)

                def attn_q(a):
                    wait(pe, n_taken, at(a, 1, 1))
                    rows_of(a, WA, 0, NT, aq_made)

                def attn_k(a):
                    wait(pe, aq_taken, at(a, HEADS, HEADS))
                    rows_of(a, WA, C, NT, ak_made)

                def attn_v(a):
                    wait(pe, ak_taken, at(a, CH, CH))
                    tokens_of(WA, 2 * C, NT, av_made)

                def attn_gate(a):
                    wait(pe, av_taken, at(a, 1, 1))
                    rows_of(a, WG, 0, HT, gate_made)

                def attn_scores(a, h):
                    if h < 2:
                        wait(pe, ao_taken, at(a, CH, h + 1 - CH))
                    else:
                        wait(pe, as_exped, at(a, HEADS * LH, (h - 1) * LH))
                    for i in range(LH):
                        last = mm(halved(6 + h % 2)[:, i, :], QM[:, h, i * P:(i + 1) * P], K[:, h // HPC, :],
                                  start=True, stop=True)
                    last.then_inc(as_made, 1)

                def attn_out(a, m):
                    wait(pe, vs_ready, at(a, CH, m + 1))
                    if m == 0:
                        wait(pe, as_exped, at(a, HEADS * LH, (HEADS - 1) * LH))
                    else:
                        wait(pe, as_exped, at(a, HEADS * LH, HEADS * LH))
                    for j in range(HPC):
                        for i in range(LH):
                            last = mm(banks[6 + m][:, 0:LOC], VS[:, i, m * HPC + j, :], EX[:, m * HPC + j, i, :],
                                      start=(j == 0 and i == 0), stop=(j == HPC - 1 and i == LH - 1))
                    last.then_inc(ao_made, 1)

                def attn_final(a):
                    wait(pe, ao_taken, at(a, CH, CH))
                    wait(pe, gate_exped, at(a, CH, CH))
                    tokens_of(WF, 0, O, fin_made)

                def image(t, a):
                    T, B = t is not None, a is not None
                    if T: turn_feats(t)
                    if B: turn_h0(a)
                    if T: turn_qn(t)
                    if B: turn_n(a)
                    if T: make_q(t)
                    if B: attn_q(a)
                    if T: make_g(t)
                    if B: attn_k(a)
                    for p in range(PAIRS):
                        if T:
                            turn_pair(t, p)
                            if p: score_pair(t, p - 1)
                        if B:
                            if p == 0: attn_v(a)
                            if p == 2: attn_gate(a)
                            if 3 <= p < 3 + HEADS: attn_scores(a, p - 3)
                    if T: score_pair(t, PAIRS - 1)
                    if B: attn_out(a, 0)
                    if T: turn_scores(t)
                    if B: attn_out(a, 1)
                    if T: turn_probs(t)
                    if B: attn_final(a)
                    if T:
                        pool_pixels(t)
                        aggregate(t)
                        project(t)

                image(0, None)
                image(1, 0)
                with pe.Fori(2, NB) as t:
                    image(t, t - 1)
                image(None, NB - 1)

            @block.scalar
            def _(act):
                def copy(out, in_):
                    return act.activation(out, in_, ACT.Copy)

                act.wait_ge(setup_done, 1)

                def take_qn(t):
                    wait(act, qn_turned, at(t, 1, 1))
                    wait(act, q_made, at(t, 1, 0))
                    copy(QN[:, :, :], halved(4)).then_inc(qn_taken, 1)

                def take_q(t):
                    wait(act, q_made, at(t, 1, 1))
                    wait(act, g_made, at(t, HEADS, 0))
                    for m in range(CH):
                        act.activation(Q[:, m, :], halved(4)[:, m, :], ACT.Identity, bias=bq_col[:, m:m + 1],
                                       scale=float(C) ** -0.5).then_inc(q_taken, 1)

                def take_g(t, i):
                    pair, c = i // CH, i % CH
                    wait(act, g_made, at(t, HEADS, i + 1))
                    wait(act, s_made, at(t, QUARTERS, 0))
                    copy(G[:, c, :, 2 * pair:2 * pair + 2].rearrange("p l h -> p h l"),
                         halved(i % 2)).then_inc(g_taken_act, 1)

                def take_xt(t, p):
                    wait(act, xt_made, at(t, PAIRS, p + 1))
                    if p == 0:
                        wait(act, z_made, at(t, 2 * QUARTERS, 0))
                        wait(act, stats_done, at(t, GROUPS, 0))
                    copy(XT[:, 2 * p:2 * p + 2, :], halved(p % 2)).then_inc(xt_taken, 1)

                def exp_scores(t):
                    wait(act, e_shifted, at(t, 1, 1))
                    act.activation(PE_[:, :, :], PE_[:, :, :], ACT.Exp).then_inc(e_exped, 1)

                def take_z(t, i):
                    q, c = i // CH, i % CH
                    wait(act, z_made, at(t, 2 * QUARTERS, i + 1))
                    wait(act, agg_made, at(t, 1, 0))
                    copy(Z[:, c, :, q * GPQ * LPG:(q + 1) * GPQ * LPG],
                         banks[i % 2][:, :].rearrange("p (l h) -> p h l", h=HEADS)).then_inc(z_taken_act, 1)

                def take_agg(t):
                    wait(act, agg_made, at(t, 1, 1))
                    wait(act, proj_made, at(t, 1, 0))
                    copy(AG[:, :, :], halved(4)).then_inc(agg_taken, 1)

                def take_h(a):
                    wait(act, h_turned, at(a, 1, 1))
                    wait(act, gate_made, at(a, 1, 0))
                    copy(HT[:, :, :], halved(5)).then_inc(h_taken, 1)

                def take_n(a):
                    wait(act, n_turned, at(a, 1, 1))
                    wait(act, av_made, at(a, 1, 0))
                    copy(NT[:, :, :], halved(5)).then_inc(n_taken, 1)

                def take_attn_q(a):
                    wait(act, aq_made, at(a, 1, 1))
                    wait(act, as_made, at(a, HEADS, 0))
                    for h in range(HEADS):
                        act.activation(QM[:, h, :], halved(5)[:, h // HPC, :], ACT.Identity, bias=bqm[:, h:h + 1],
                                       scale=qscale[:, h % HPC:h % HPC + 1]).then_inc(aq_taken, 1)

                def take_attn_k(a):
                    wait(act, ak_made, at(a, 1, 1))
                    for m in range(CH):
                        act.activation(K[:, m, :], halved(5)[:, m, :], ACT.Identity,
                                       bias=bk_col[:, m:m + 1]).then_inc(ak_taken, 1)

                def exp_gate(a):
                    wait(act, gate_made, at(a, 1, 1))
                    wait(act, fin_made, at(a, 1, 0))
                    for m in range(CH):
                        act.activation(GT[:, m, :], halved(5)[:, m, :], ACT.Exp, bias=nbg[:, m:m + 1],
                                       scale=-1.0).then_inc(gate_exped, 1)

                def exp_attn(a, h):
                    wait(act, as_max, at(a, HEADS, h + 1))
                    if h == 0:
                        wait(act, ao_made, at(a, CH, 0))
                        wait(act, vs_ready, at(a, CH, 0))
                    for i in range(LH):
                        act.activation(EX[:, h, i, :], halved(6 + h % 2)[:, i, :], ACT.Exp, bias=nmax[:, h, i:i + 1],
                                       accum_out=esum[:, h, i:i + 1]).then_inc(as_exped, 1)

                def image(t, a):
                    T, B = t is not None, a is not None
                    if B: take_h(a)
                    if T: take_qn(t)
                    if B: take_n(a)
                    if T: take_q(t)
                    if B: take_attn_q(a)
                    if T:
                        for i in range(0, HEADS, 2):
                            take_g(t, i)
                    if B: take_attn_k(a)
                    for p in range(PAIRS):
                        if T: take_xt(t, p)
                        if B:
                            if p == 3: exp_gate(a)
                            if 4 <= p < 4 + HEADS: exp_attn(a, p - 4)
                    if T:
                        exp_scores(t)
                        for i in range(0, 2 * QUARTERS, 2):
                            take_z(t, i)
                        take_agg(t)

                image(0, None)
                image(1, 0)
                with act.Fori(2, NB) as t:
                    image(t, t - 1)
                image(None, NB - 1)

            T_LINKS, A_LINKS = 19, 8

            @block.vector
            def _(dve):
                dve.memset(halves[:, :], -0.5).then_inc(su_v, 1)
                dve.memset(ones, 1.0).then_inc(su_v, 1)
                dve.memset(WVm[:, :, :, :], 0.0).then_inc(su_v, 1)
                dve.memset(VS[:, :, :, :], 0.0).then_inc(su_v, 1)
                dve.wait_ge(setup_loads, SETUP_LOADS)
                dve.wait_ge(su_v, 4)
                dve.tensor_tensor(wtmp, raw_wv, row_b.unsqueeze(1).to_broadcast([P, CH, C]), ALU.mult).then_inc(su_v, 1)
                dve.wait_ge(su_v, 5)
                dve.tensor_reduce(bv_col[:, :, 0], wtmp, AX.X, ALU.add).then_inc(su_v, 1)
                dve.wait_ge(su_v, 6)
                for c in range(CH):
                    dve.tensor_scalar(bv_wide[:, c, :], ones, bv_col[:, c, :], None, ALU.mult).then_inc(su_v, 1)
                dve.tensor_tensor(beta_wide, vcol[:, BETA, :].unsqueeze(2).to_broadcast([P, CH, P]),
                                  ones.unsqueeze(1).to_broadcast([P, CH, P]), ALU.mult).then_inc(su_v, 1)
                n = 9
                for raw in (raw_wk, raw_wv):
                    if raw is raw_wv:
                        dve.wait_ge(su_v, n)
                    dve.tensor_tensor(wtmp if raw is raw_wv else raw_wk, raw,
                                      row_w.unsqueeze(1).to_broadcast([P, CH, C]), ALU.mult).then_inc(su_v, 1)
                    dst = wtmp if raw is raw_wv else raw_wk
                    n += 1
                    dve.wait_ge(su_v, n)
                    dve.tensor_reduce(wmean[:, :, 0], dst, AX.X, ALU.add).then_inc(su_v, 1)
                    n += 1
                    dve.wait_ge(su_v, n)
                    dve.scalar_tensor_tensor(dst, wmean.to_broadcast([P, CH, C]), -1.0 / C, dst,
                                             ALU.mult, ALU.add).then_inc(su_v, 1)
                    n += 1
                assert n == 15
                dve.wait_ge(su_v, n)
                for h in range(HEADS):
                    dve.tensor_scalar(WKm[:, h, :], raw_wk[:, h // HPC, :], headmask[:, h % HPC:h % HPC + 1], None,
                                      ALU.mult).then_inc(su_v, 1)
                dve.tensor_scalar(qscale[:, :], headmask[:, :], float(D) ** -0.5, None, ALU.mult).then_inc(su_v, 1)
                dve.tensor_scalar(nbg[:, :], vcol[:, BGATE, :], -1.0, None, ALU.mult).then_inc(su_v, 1)
                for c in range(CH):
                    dve.tensor_scalar(WQ[:, c, :], raw_wq[:, c, :], vcol[:, QW, c:c + 1], None, ALU.mult).then_inc(su_v, 1)
                    dve.tensor_scalar(WA[:, c, :], raw_wqkv[:, c, :], vcol[:, GAMMA, c:c + 1], None, ALU.mult).then_inc(su_v, 1)
                SU_P = 2 * CH + 4 * CH + 2 * CH + CH * CH
                dve.wait_ge(su_p, SU_P)
                dve.tensor_scalar(bq_col[:, :], banks[0][:, 0:CH], float(C) ** -0.5, None, ALU.mult).then_inc(su_v, 1)
                dve.tensor_copy(bk_col[:, :], banks[1][:, CH:2 * CH]).then_inc(su_v, 1)
                dve.tensor_copy(vb_row[:, :], banks[2][:, 0:C]).then_inc(su_v, 1)
                dve.tensor_tensor(pb_row[:, :], banks[3][:, 0:C], pb_raw, ALU.add).then_inc(su_v, 1)
                n += HEADS + 2 + 2 * CH + 4
                dve.wait_ge(su_v, n)
                for m in range(CH):
                    dve.tensor_scalar(bqm[:, m * HPC:(m + 1) * HPC], qscale[:, :], banks[1][:, m:m + 1], None,
                                      ALU.mult).then_inc(su_v, 1)
                for m in range(CH):
                    for j in range(HPC):
                        h = m * HPC + j
                        dve.tensor_copy(WVm[:, :, h, j * D:(j + 1) * D], halved(4)[:, :, h * D:(h + 1) * D]).then_inc(su_v, 1)
                n += CH + HEADS
                dve.wait_ge(su_v, n)
                dve.nop().then_inc(setup_done, 1)

                tstep, astep = Steps(dve, t_chain, T_LINKS), Steps(dve, a_chain, A_LINKS)

                def sum_feats(t):
                    for q in range(QUARTERS):
                        wait(dve, x_loaded[q], at(t, 16, 16))
                    wait(dve, r_turned, at(t, 1, 0))
                    dve.tensor_reduce(R[:, :, :], X[:, :, :].rearrange("p c (l n) -> p c l n", n=N2),
                                      AX.X, ALU.add).then_inc(feats_summed, 1)

                def stats(src, n, mean_var, step, signal):
                    layer_stats(dve, src, n, bnt, mean_var, step, signal)

                def take_r(t):
                    wait(dve, r_turned, at(t, 1, 1))
                    wait(dve, h0_ready, at(t, 1, 0))
                    dve.tensor_scalar(RT[:, :, :], halved(4), 1.0 / N2, None, ALU.mult).then_inc(r_taken, 1)
                    dve.wait_ge(r_taken, at(t, 1, 1))
                    stats(RT, LH, mv, tstep, r_var)

                def norm_q(t):
                    wait(dve, r_rstd, at(t, 1, 1))
                    for l in range(LH):
                        ins = dve.tensor_scalar(QNT[:, l, :], RT[:, l, :], mv[:, l, 0:1], rstd2[:, l:l + 1],
                                                ALU.subtract, ALU.mult)
                    ins.then_inc(qn_ready, 1)

                def take_g(t, i):
                    pair, c = i // CH, i % CH
                    wait(dve, g_made, at(t, HEADS, i + 1))
                    dve.tensor_copy(G[:, c, :, 2 * pair:2 * pair + 2].rearrange("p l h -> p h l"),
                                    halved(i % 2)).then_inc(g_taken_dve, 1)

                def pixel_stats(t, p):
                    wait(dve, xt_taken, at(t, PAIRS, p + 1))
                    for j in range(2):
                        dve.bn_stats(st[:, 2 * p + j, :], XT[:, 2 * p + j, :]).then_inc(stats_done, 1)

                def take_scores(t, q):
                    wait(dve, s_made, at(t, QUARTERS, q + 1))
                    dve.tensor_tensor(SM[:, :, :], banks[2 + q % 2][:, :].rearrange("p (g s) -> p g s", g=GPQ),
                                      pixmask[:, :].unsqueeze(1).to_broadcast([P, GPQ, SH]), ALU.mult).then_inc(s_taken, 1)
                    dve.wait_ge(s_taken, at(t, QUARTERS, q + 1))
                    tstep(dve.tensor_reduce(E[:, q * GPQ:(q + 1) * GPQ, :],
                                            SM[:, :, :].rearrange("p g (l h) -> p g h l", h=HEADS), AX.X, ALU.add))

                def pixel_var(t):
                    dve.wait_ge(stats_done, at(t, GROUPS, GROUPS))
                    tstep(dve.tensor_tensor(vt[:, 0, :], st[:, :, 1], st[:, :, 4], ALU.subtract))
                    tstep(dve.tensor_tensor(vt[:, 0, :], vt[:, 0, :], vt[:, 0, :], ALU.mult))
                    tstep(dve.tensor_tensor(vt[:, 1, :], st[:, :, 2], st[:, :, 5], ALU.add))
                    tstep(dve.scalar_tensor_tensor(vt[:, 1, :], vt[:, 0, :], C / 4.0, vt[:, 1, :], ALU.mult, ALU.add))
                    dve.tensor_scalar(vt[:, 0, :], vt[:, 1, :], 1.0 / C, EPS, ALU.mult, ALU.add).then_inc(pix_var, 1)

                def scale_scores(t):
                    wait(dve, pix_rstd, at(t, 1, 1))
                    dve.tensor_tensor(E[:, :, :], E[:, :, :], RS[:, :].unsqueeze(2).to_broadcast([P, GROUPS, HEADS]),
                                      ALU.mult).then_inc(e_ready, 1)

                def over_pixels(ap):
                    return ap.unsqueeze(2).to_broadcast([P, 2 * LPG, N2])

                def softmax_shift(t):
                    wait(dve, e_turned, at(t, 1, 1))
                    src = banks[4][:, 0:2 * P].rearrange("p (m n) -> p m n", n=N2)
                    tstep(dve.tensor_reduce(mx[:, :], src, AX.X, ALU.max))
                    dve.tensor_tensor(PE_[:, :, :], src, over_pixels(mx[:, :]), ALU.subtract).then_inc(e_shifted, 1)

                def softmax_divide(t):
                    wait(dve, e_exped, at(t, 1, 1))
                    tstep(dve.tensor_reduce(den[:, :], PE_[:, :, :], AX.X, ALU.add))
                    tstep(dve.reciprocal(den[:, :], den[:, :]))
                    dve.tensor_tensor(PE_[:, :, :], PE_[:, :, :], over_pixels(den[:, :]), ALU.mult).then_inc(p_ready, 1)

                def take_probs(t):
                    wait(dve, p_turned, at(t, 1, 1))
                    wait(dve, p_spread, at(t, QUARTERS, 0))
                    dve.tensor_tensor(PR[:, :, :], banks[4][:, 0:GROUPS * HEADS].rearrange("p (g h) -> p g h", h=HEADS),
                                      RS[:, :].unsqueeze(2).to_broadcast([P, GROUPS, HEADS]), ALU.mult).then_inc(p_taken, 1)

                def take_z(t, i):
                    q, c = i // CH, i % CH
                    wait(dve, z_made, at(t, 2 * QUARTERS, i + 1))
                    dve.tensor_copy(Z[:, c, :, q * GPQ * LPG:(q + 1) * GPQ * LPG],
                                    banks[i % 2][:, :].rearrange("p (l h) -> p h l", h=HEADS)).then_inc(z_taken_dve, 1)

                def take_h0(t):
                    wait(dve, proj_made, at(t, 1, 1))
                    wait(dve, rb_ready, at(t, 1, 1))
                    wait(dve, h0_twice, at(t, 1, 0))
                    dve.tensor_tensor(H0[:, :, :], halved(4), RTB[:, :, :], ALU.add).then_inc(h0_ready, 1)
                    dve.wait_ge(h0_ready, at(t, 1, 1))

                def norm_h0(a):
                    wait(dve, h0_rstd, at(a, 1, 1))
                    for l in range(LH):
                        ins = dve.tensor_scalar(NH[:, l, :], H0[:, l, :], amv[:, l, 0:1], arstd[:, l:l + 1],
                                                ALU.subtract, ALU.mult)
                    ins.then_inc(n_ready, 1)

                def take_v(a):
                    wait(dve, av_made, at(a, 1, 1))
                    dve.tensor_tensor(V[:, :, :, :].rearrange("p l h d -> p l (h d)"), halved(5),
                                      vb_row[:, :].unsqueeze(1).to_broadcast([P, LH, C]), ALU.add).then_inc(av_taken, 1)

                def max_attn(a, h):
                    wait(dve, as_made, at(a, HEADS, h + 1))
                    dve.tensor_reduce(nmax[:, h, :], halved(6 + h % 2), AX.X, ALU.max, negate=True).then_inc(as_max, 1)

                def invert_gate(a):
                    wait(dve, gate_exped, at(a, CH, CH))
                    astep(dve.tensor_scalar(GT[:, :, :], GT[:, :, :], 1.0, None, ALU.add))
                    dve.reciprocal(GT[:, :, :], GT[:, :, :]).then_inc(gate_ready, 1)

                def scale_v(a, m):
                    heads = slice(m * HPC, (m + 1) * HPC)
                    wait(dve, as_exped, at(a, HEADS * LH, (m + 1) * HPC * LH))
                    astep(dve.reciprocal(esum[:, heads, :], esum[:, heads, :]))
                    for j in range(HPC):
                        h = m * HPC + j
                        ins = dve.tensor_tensor(VS[:, :, h, j * D:(j + 1) * D], V[:, :, h, :],
                                                esum[:, h, :].unsqueeze(2).to_broadcast([P, LH, D]), ALU.mult)
                    ins.then_inc(vs_ready, 1)

                def gate_out(a, m):
                    wait(dve, ao_made, at(a, CH, m + 1))
                    if m == 0:
                        dve.wait_ge(gate_ready, at(a, 1, 1))
                    dve.tensor_tensor(O[:, m, :], banks[6 + m][:, 0:LOC], GT[:, m, :], ALU.mult).then_inc(ao_taken, 1)

                def add_attn(a):
                    wait(dve, fin_made, at(a, 1, 1))
                    wait(dve, h0_twice, at(a, 1, 1))
                    astep(dve.tensor_tensor(U[:, :, :], halved(5), H2[:, :, :], ALU.add))
                    stats(U, LH, bmv, astep, u_var)

                def norm_u(a):
                    wait(dve, u_rstd, at(a, 1, 1))
                    wait(dve, h1_stored, at(a, 16, 0))
                    for l in range(LH):
                        ins = dve.tensor_scalar(H1[:, l, :], U[:, l, :], bmv[:, l, 0:1], brstd[:, l:l + 1],
                                                ALU.subtract, ALU.mult)
                    ins.then_inc(h1_ready, 1)

                def image(t, a, more=True):
                    T, B = t is not None, a is not None
                    if T: tstep.start(t)
                    if B: astep.start(a)
                    if T: take_r(t)
                    if B: norm_h0(a)
                    if T:
                        norm_q(t)
                        for i in range(1, HEADS, 2):
                            take_g(t, i)
                    ppq = PAIRS // QUARTERS
                    for p in range(PAIRS):
                        if T:
                            pixel_stats(t, p)
                            if p % ppq == 1 and p > ppq:
                                take_scores(t, p // ppq - 1)
                        if B:
                            if p == 1: take_v(a)
                            if 4 <= p < 4 + HEADS: max_attn(a, p - 4)
                            if p == 9: scale_v(a, 0)
                            if p == 5: invert_gate(a)
                    if T: pixel_var(t)
                    if B: scale_v(a, 1)
                    if T:
                        take_scores(t, QUARTERS - 1)
                        scale_scores(t)
                    if B: gate_out(a, 0)
                    if T: softmax_shift(t)
                    if B: gate_out(a, 1)
                    if T:
                        softmax_divide(t)
                        take_probs(t)
                    if B: add_attn(a)
                    if T: take_z(t, 1)
                    if B: norm_u(a)
                    if T:
                        for i in range(3, 2 * QUARTERS, 2):
                            take_z(t, i)
                        if more: sum_feats(t + 1)
                        take_h0(t)
                        stats(H0, LH, amv, tstep, h0_var)
                        tstep.finish()
                    if B: astep.finish()

                sum_feats(0)
                image(0, None)
                image(1, 0)
                with dve.Fori(2, NB - 1) as t:
                    image(t, t - 1)
                image(NB - 1, NB - 2, more=False)
                image(None, NB - 1)

            @block.gpsimd
            def _(pool):
                tstep = Steps(pool, pool_t_chain, 3)
                pool.wait_ge(setup_done, 1)

                def root(out, var, signal):
                    pool.tensor_tensor(out, var, halves[:, 0:out.shape[1]], ALU.pow).then_inc(signal, 1)

                def feats_rstd(t):
                    wait(pool, r_var, at(t, 1, 1))
                    root(rstd2[:, :], mv[:, :, 1], r_rstd)

                def feats_bias(t):
                    wait(pool, h0_ready, at(t, 1, 0))
                    pool.tensor_tensor(RTB[:, :, :], RT[:, :, :], pb_row[:, :].unsqueeze(1).to_broadcast([P, LH, C]),
                                       ALU.add).then_inc(rb_ready, 1)

                def pixel_rstd(t):
                    wait(pool, pix_var, at(t, 1, 1))
                    pool.tensor_tensor(RS[:, :], vt[:, 0, :], halves[:, :], ALU.pow).then_inc(pix_rstd, 1)

                def spread(t, q):
                    if q == 0:
                        wait(pool, p_taken, at(t, 1, 1))
                        wait(pool, z_made, at(t, 2 * QUARTERS, 0))
                    g = slice(q * GPQ, (q + 1) * GPQ)
                    pool.tensor_tensor(A[:, g, :, :], PR[:, g, :].unsqueeze(2).to_broadcast([P, GPQ, LPG, HEADS]),
                                       pixmask[:, :].rearrange("p (l h) -> p l h", h=HEADS).unsqueeze(1).to_broadcast(
                                           [P, GPQ, LPG, HEADS]), ALU.mult).then_inc(p_spread, 1)

                def h0_parts(t):
                    wait(pool, h0_var, at(t, 1, 1))
                    wait(pool, n_ready, at(t, 1, 0))
                    root(arstd[:, :], amv[:, :, 1], h0_rstd)
                    wait(pool, h1_ready, at(t, 1, 0))
                    for l in range(LH):
                        tstep(pool.tensor_tensor(H2[:, l, :], H0[:, l, :], H0[:, l, :], ALU.add))
                    for l in range(LH):
                        ins = pool.tensor_tensor(H2[:, l, :], H2[:, l, :], bf_row[:, :], ALU.add)
                        if l < LH - 1:
                            tstep(ins)
                    ins.then_inc(h0_twice, 1)

                def u_root(a):
                    wait(pool, u_var, at(a, 1, 1))
                    wait(pool, h1_ready, at(a, 1, 0))
                    root(brstd[:, :], bmv[:, :, 1], u_rstd)

                def image(t, a):
                    T, B = t is not None, a is not None
                    if T: tstep.start(t)
                    if T:
                        feats_rstd(t)
                        feats_bias(t)
                        pixel_rstd(t)
                        spread(t, 0)
                        spread(t, 1)
                    if B: u_root(a)
                    if T:
                        for q in range(2, QUARTERS):
                            spread(t, q)
                        h0_parts(t)
                        tstep.finish()

                image(0, None)
                image(1, 0)
                with pool.Fori(2, NB) as t:
                    image(t, t - 1)
                image(None, NB - 1)

        TOK = 512
        TT = TOK // P
        CHUNKS = NB * LOC // TOK
        E6 = EXPERTS
        STAGES = E6 + 2
        w_loads, tok_loaded, out_stored = sem("expert_weights_loaded"), [sem(f"tok_loaded{i}") for i in range(2)], sem("out_stored")
        m_turned, m_taken = sem("m_turned"), sem("m_taken")
        rh_made, rh_taken, logits_made, logits_taken = sem("rh_made"), sem("rh_taken"), sem("logits_made"), sem("logits_taken")
        rt_shifted, rt_exped = sem("router_shifted"), sem("router_exped")
        wt_ready, wt_turned, wt_taken, b3_made = sem("route_ready"), sem("route_turned"), sem("route_taken"), sem("b3_made")
        l1_made, l1_taken, l2_made, l2_taken = sem("l1_made"), sem("l1_taken"), sem("l2_made"), sem("l2_taken")
        l3_made, l3_taken = sem("l3_made"), sem("l3_taken")
        f_var, f_rstd, f_ready = sem("f_var"), sem("f_rstd"), sem("f_ready")
        f_chain = sem("ffn_vector_steps")

        with ExitStack() as two:
            W1, W2, W3 = (sb(two, f"expert_w{n}", E6, CH, C) for n in (1, 2, 3))
            B1, B2 = sb(two, "expert_b1", E6, CH), sb(two, "expert_b2", E6, CH)
            B3 = two.enter_context(nc.sbuf_tensor("expert_b3", [E6, C], F32))
            RW1, RW2 = sb(two, "router_w1", CH, P), sb(two, "router_w2", E6)
            RB1, RB2 = sb(two, "router_b1", 1), sb(two, "router_b2", E6)
            before = sb(two, "expert_before", E6, E6)
            HTOK = sb(two, "tokens", 2, TT, C)
            HC = sb(two, "tokens_turned", CH, TOK)
            RH = sb(two, "router_hidden", TOK)
            LG, PB_, PX = sb(two, "logits", TT, E6), sb(two, "probs", TT, E6), sb(two, "weights_top2", TT, E6)
            l_mx, l_den = sb(two, "logit_max", TT), sb(two, "weight_sum", TT)
            gt, eq, rank = sb(two, "larger", TT, E6, E6), sb(two, "equal_before", TT, E6, E6), sb(two, "rank", TT, E6)
            WTT = two.enter_context(nc.sbuf_tensor("weights_turned", [E6, TT, P], F32))
            A1, A2 = sb(two, "hidden1", CH, TOK), sb(two, "hidden2", CH, TOK)
            ACC = sb(two, "combined", TT, C)
            fst, fmv, frstd = sb(two, "bn_ffn", TT, 8), sb(two, "mean_var_ffn", TT, 2), sb(two, "rstd_ffn", TT)
            OUT = sb(two, "out_tokens", TT, C)

            tok_view = h1_dram.rearrange("(i k p) c -> i p k c", k=TT, p=P)
            out_view = out.rearrange("b l c -> (b l) c").rearrange("(i k p) c -> i p k c", k=TT, p=P)
            WLOADS = 3 * E6 + 10

            block = two.enter_context(nc.Block())

            @block.sync
            def _(sp):
                def load_tokens(i, slot):
                    wait(sp, f_var, at(i, 1, -1))
                    sp.dma_start(HTOK[:, slot, :, :], tok_view[i]).then_inc(tok_loaded[slot], 16)

                sp.wait_ge(h1_stored, 16 * NB)
                load_tokens(0, 0)
                for e in range(E6):
                    for W, w in ((W1, ew1), (W2, ew2), (W3, ew3)):
                        sp.dma_start(W[:, e, :, :], w[e].rearrange("(c p) n -> p c n", p=P)).then_inc(w_loads, 16)
                load_tokens(1, 1)
                with nc.allow_non_contiguous_dma(reason="biases, once"):
                    for dst, src in ((B1[:, :, 0], eb1[:, 0:P].rearrange("e p -> p e")), (B1[:, :, 1], eb1[:, P:C].rearrange("e p -> p e")),
                                     (B2[:, :, 0], eb2[:, 0:P].rearrange("e p -> p e")), (B2[:, :, 1], eb2[:, P:C].rearrange("e p -> p e")),
                                     (RB1[:, :], rb1.rearrange("(p o) -> p o", o=1))):
                        sp.dma_start(dst, src, allow_slow_non_contiguous=True).then_inc(w_loads, 16)
                sp.dma_start(RB2[:, :], rb2.partition_broadcast(P)).then_inc(w_loads, 16)
                sp.dma_start(B3[:, :], eb3).then_inc(w_loads, 16)
                sp.dma_start(RW1[:, :, :], rw1.rearrange("(c p) n -> p c n", p=P)).then_inc(w_loads, 16)
                sp.dma_start(RW2[:, :], rw2).then_inc(w_loads, 16)
                sp.dma_start(before[:, :, :], masks_in[:, SH + HPC:SH + HPC + E6 * E6].rearrange(
                    "p (a b) -> p a b", a=E6)).then_inc(w_loads, 16)

                def store(i):
                    wait(sp, f_ready, at(i, 1, 1))
                    sp.dma_start(out_view[i], OUT[:, :, :]).then_inc(out_stored, 16)

                with sp.Fori(1, CHUNKS // 2) as j:
                    for k in range(2):
                        load_tokens(2 * j + k, k)
                        store(2 * j + k - 2)
                store(CHUNKS - 2)
                store(CHUNKS - 1)
                sp.wait_ge(out_stored, 16 * CHUNKS)

            @block.tensor
            def _(pe):
                mm = pe.matmul
                pe.wait_ge(w_loads, 16 * WLOADS)

                def router(i, half, slot):
                    pe.wait_ge(tok_loaded[slot], at(half, 16, 16))
                    for c in range(CH):
                        wait(pe, m_taken, at(i, CH, c))
                        for k in range(TT):
                            last = pe.transpose(banks[6][:, k * P:(k + 1) * P], HTOK[:, slot, k, c * P:(c + 1) * P], ident[:, :])
                        last.then_inc(m_turned, 1)
                    pe.wait_ge(m_taken, at(i, CH, CH))
                    wait(pe, wt_taken, at(i, 1, 0))
                    for c in range(CH):
                        last = mm(banks[7][:, :], RW1[:, c, :], HC[:, c, :], start=(c == 0), stop=(c == CH - 1))
                    last.then_inc(rh_made, 1)

                def logits(i):
                    pe.wait_ge(rh_taken, at(i, 1, 1))
                    for k in range(TT):
                        last = mm(banks[7][:, k * E6:(k + 1) * E6], RH[:, k * P:(k + 1) * P], RW2[:, :], start=True, stop=True)
                    last.then_inc(logits_made, 1)

                def turn_route(i):
                    pe.wait_ge(wt_ready, at(i, 1, 1))
                    for k in range(TT):
                        last = pe.transpose(banks[7][0:E6, k * P:(k + 1) * P], PX[:, k, :], ident[:, :])
                    last.then_inc(wt_turned, 1)

                def layer(i, e, W, src, first_bank, made):
                    for m in range(CH):
                        for c in range(CH):
                            last = mm(banks[first_bank + m][:, :], W[:, e, c, m * P:(m + 1) * P], src[:, c, :],
                                      start=(c == 0), stop=(c == CH - 1))
                        last.then_inc(made, 1)

                def chunk(i, half, slot):
                    router(i, half, slot)
                    for s in range(STAGES):
                        if s < E6:
                            wait(pe, l1_taken, at(i, E6 * CH, s * CH))
                            layer(i, s, W1, HC, 0, l1_made)
                        if s == 0:
                            logits(i)
                        if 1 <= s <= E6:
                            pe.wait_ge(l1_taken, at(i, E6 * CH, s * CH))
                            wait(pe, l2_taken, at(i, E6 * CH, (s - 1) * CH))
                            layer(i, s - 1, W2, A1, 2, l2_made)
                        if s == 2:
                            turn_route(i)
                            pe.wait_ge(wt_taken, at(i, 1, 1))
                            wait(pe, l3_taken, at(i, E6 + 1, 0))
                            for k in range(TT):
                                last = mm(halved(4 + k // 2)[:, k % 2, :], WTT[:, k, :], B3[:, :], start=True, stop=True)
                            last.then_inc(b3_made, 1)
                        if s >= 2:
                            e = s - 2
                            pe.wait_ge(l2_taken, at(i, E6 * CH, (e + 1) * CH))
                            pe.wait_ge(l3_taken, at(i, E6 + 1, e + 1))
                            for k in range(TT):
                                for c in range(CH):
                                    last = mm(halved(4 + k // 2)[:, k % 2, :], A2[:, c, k * P:(k + 1) * P], W3[:, e, c, :],
                                              start=(c == 0), stop=(c == CH - 1))
                            last.then_inc(l3_made, 1)

                for k in range(2):
                    chunk(k, 0, k)
                with pe.Fori(1, CHUNKS // 2) as j:
                    for k in range(2):
                        chunk(2 * j + k, j, k)

            @block.scalar
            def _(act):
                act.wait_ge(w_loads, 16 * WLOADS)

                def exp(i, n):
                    act.wait_ge(rt_shifted, at(i, 2, n))
                    act.activation(PX[:, :, :], PX[:, :, :], ACT.Exp).then_inc(rt_exped, 1)

                def chunk(i):
                    for c in range(CH):
                        act.wait_ge(m_turned, at(i, CH, c + 1))
                        if c == 0:
                            wait(act, l1_made, at(i, E6 * CH, 0))
                        act.activation(HC[:, c, :], banks[6][:, :], ACT.Copy).then_inc(m_taken, 1)
                    act.wait_ge(rh_made, at(i, 1, 1))
                    wait(act, logits_made, at(i, 1, 0))
                    act.activation(RH[:, :], banks[7][:, :], ACT.Relu, bias=RB1[:, 0:1]).then_inc(rh_taken, 1)
                    for e in range(E6):
                        for m in range(CH):
                            act.wait_ge(l1_made, at(i, E6 * CH, e * CH + m + 1))
                            if m == 0:
                                wait(act, l2_made, at(i, E6 * CH, e * CH))
                            act.activation(A1[:, m, :], banks[m][:, :], ACT.Relu, bias=B1[:, e, m:m + 1]).then_inc(l1_taken, 1)
                        if e < 2:
                            exp(i, e + 1)

                chunk(0)
                with act.Fori(1, CHUNKS) as i:
                    chunk(i)

            @block.vector
            def _(dve):
                step = Steps(dve, f_chain, 19)
                dve.wait_ge(w_loads, 16 * WLOADS)

                def six(ap):
                    return ap.unsqueeze(2).to_broadcast([P, TT, E6])

                def softmax_logits(i):
                    dve.wait_ge(logits_made, at(i, 1, 1))
                    step(dve.tensor_tensor(LG[:, :, :], banks[7][:, 0:TT * E6].rearrange("p (k e) -> p k e", e=E6),
                                           RB2[:, :].unsqueeze(1).to_broadcast([P, TT, E6]), ALU.add))
                    step(dve.tensor_reduce(l_mx[:, :], LG[:, :, :], AX.X, ALU.max))
                    wait(dve, wt_turned, at(i, 1, 0))
                    dve.tensor_tensor(PX[:, :, :], LG[:, :, :], six(l_mx[:, :]), ALU.subtract).then_inc(rt_shifted, 1)
                    dve.wait_ge(rt_exped, at(i, 2, 1))
                    step(dve.tensor_reduce(l_den[:, :], PX[:, :, :], AX.X, ALU.add))
                    step(dve.reciprocal(l_den[:, :], l_den[:, :]))
                    step(dve.tensor_tensor(PB_[:, :, :], PX[:, :, :], six(l_den[:, :]), ALU.mult))

                def choose(i):
                    mine = PB_[:, :, :].unsqueeze(3).to_broadcast([P, TT, E6, E6])
                    other = PB_[:, :, :].unsqueeze(2).to_broadcast([P, TT, E6, E6])
                    first = before[:, :, :].unsqueeze(1).to_broadcast([P, TT, E6, E6])
                    step(dve.tensor_tensor(gt[:, :, :, :], other, mine, ALU.is_gt))
                    step(dve.tensor_tensor(eq[:, :, :, :], other, mine, ALU.is_equal))
                    step(dve.tensor_tensor(eq[:, :, :, :], eq[:, :, :, :], first, ALU.mult))
                    step(dve.tensor_tensor(gt[:, :, :, :], gt[:, :, :, :], eq[:, :, :, :], ALU.add))
                    step(dve.tensor_reduce(rank[:, :, :], gt[:, :, :, :], AX.X, ALU.add))
                    step(dve.tensor_reduce(l_mx[:, :], PB_[:, :, :], AX.X, ALU.max))
                    dve.tensor_tensor(PX[:, :, :], PB_[:, :, :], six(l_mx[:, :]), ALU.subtract).then_inc(rt_shifted, 1)

                def weigh(i):
                    dve.wait_ge(rt_exped, at(i, 2, 2))
                    step(dve.tensor_scalar(rank[:, :, :], rank[:, :, :], 1.5, None, ALU.is_lt))
                    step(dve.tensor_tensor(PX[:, :, :], PX[:, :, :], rank[:, :, :], ALU.mult))
                    step(dve.tensor_reduce(l_den[:, :], PX[:, :, :], AX.X, ALU.add))
                    step(dve.reciprocal(l_den[:, :], l_den[:, :]))
                    dve.tensor_tensor(PX[:, :, :], PX[:, :, :], six(l_den[:, :]), ALU.mult).then_inc(wt_ready, 1)

                def take_l2(i, e):
                    for m in range(CH):
                        dve.wait_ge(l2_made, at(i, E6 * CH, e * CH + m + 1))
                        if m == 0:
                            wait(dve, l3_made, at(i, E6, e))
                        dve.tensor_scalar(A2[:, m, :], banks[2 + m][:, :], B2[:, e, m:m + 1], 0.0,
                                          ALU.add, ALU.max).then_inc(l2_taken, 1)

                def take_b3(i, slot):
                    dve.wait_ge(wt_turned, at(i, 1, 1))
                    dve.tensor_copy(WTT[:, :, :], banks[7][0:E6, :].rearrange("e (k p) -> e k p", p=P)).then_inc(wt_taken, 1)
                    dve.wait_ge(b3_made, at(i, 1, 1))
                    for b in range(TT // 2):
                        last = dve.tensor_tensor(ACC[:, 2 * b:2 * b + 2, :], halved(4 + b), HTOK[:, slot, 2 * b:2 * b + 2, :], ALU.add)
                    last.then_inc(l3_taken, 1)

                def take_l3(i, e):
                    dve.wait_ge(l3_made, at(i, E6, e + 1))
                    dve.wait_ge(l3_taken, at(i, E6 + 1, e + 1))
                    for k in range(TT):
                        last = dve.scalar_tensor_tensor(ACC[:, k, :], halved(4 + k // 2)[:, k % 2, :], PX[:, k, e:e + 1],
                                                        ACC[:, k, :], ALU.mult, ALU.add)
                    last.then_inc(l3_taken, 1)

                def norm(i):
                    dve.wait_ge(l3_taken, at(i, E6 + 1, E6 + 1))
                    layer_stats(dve, ACC, TT, fst, fmv, step, f_var)
                    dve.wait_ge(f_rstd, at(i, 1, 1))
                    wait(dve, out_stored, at(i, 16, 0))
                    for k in range(TT):
                        last = dve.tensor_scalar(OUT[:, k, :], ACC[:, k, :], fmv[:, k, 0:1], frstd[:, k:k + 1],
                                                 ALU.subtract, ALU.mult)
                    last.then_inc(f_ready, 1)

                def chunk(i, slot):
                    step.start(i)
                    softmax_logits(i)
                    choose(i)
                    take_l2(i, 0)
                    weigh(i)
                    take_b3(i, slot)
                    take_l2(i, 1)
                    take_l3(i, 0)
                    for e in range(2, E6):
                        take_l2(i, e)
                        take_l3(i, e - 1)
                    take_l3(i, E6 - 1)
                    norm(i)
                    step.finish()

                for k in range(2):
                    chunk(k, k)
                with dve.Fori(1, CHUNKS // 2) as j:
                    for k in range(2):
                        chunk(2 * j + k, k)

            @block.gpsimd
            def _(pool):
                def chunk(i):
                    pool.wait_ge(f_var, at(i, 1, 1))
                    wait(pool, f_ready, at(i, 1, 0))
                    pool.tensor_tensor(frstd[:, :], fmv[:, :, 1], halves[:, 0:TT], ALU.pow).then_inc(f_rstd, 1)

                chunk(0)
                with pool.Fori(1, CHUNKS) as i:
                    chunk(i)


def kernel(**inputs):
    import numpy as np
    import concourse.bacc as bacc
    from concourse.bass_utils import run_bass_kernel_spmd

    arrays, aps = prepare(inputs, np, bacc)
    nc = aps.pop("nc")
    build(nc, **aps)
    r = run_bass_kernel_spmd(nc, [arrays], core_ids=[0])
    return r.results[0]["out_dram"]


def prepare(inputs, np, bacc):
    def t(name):
        return np.ascontiguousarray(np.asarray(inputs[name]).T)

    def a(name):
        return np.ascontiguousarray(inputs[name])

    x = a("x")
    n, c, h, w = x.shape
    x = np.ascontiguousarray(x.reshape(n, c, h // STRIDE, STRIDE, w // STRIDE, STRIDE).transpose(0, 1, 2, 4, 3, 5)).reshape(
        n, c, -1, STRIDE ** 2)
    p = np.arange(P)
    sh = (np.arange(64) // HEADS)[None, :] == (p // STRIDE ** 2)[:, None]
    hm = np.arange(4)[None, :] == (p // 32)[:, None]
    before = np.broadcast_to((np.arange(EXPERTS)[None, :] < np.arange(EXPERTS)[:, None]).ravel(), (P, EXPERTS ** 2))
    data = {
        "x": x, "wq_t": t("L0_tok_Wq"), "wkv": a("L0_tok_Wkv"), "proj_t": t("L0_tok_proj_w"),
        "wqkv_t": t("L0_attn_W_qkv"), "wgate_t": t("L0_attn_W_gate"), "wfinal_t": t("L0_attn_W_final"),
        "vecs": np.stack([a(n) for n in VECS]), "ident_in": np.eye(P, dtype=np.float32),
        "masks_in": np.concatenate([sh, hm, before], axis=1).astype(np.float32),
        "rw1": a("L0_ffn_router_w1"), "rb1": a("L0_ffn_router_b1"), "rw2": a("L0_ffn_router_w2"), "rb2": a("L0_ffn_router_b2"),
        "ew1": a("L0_ffn_expert_w1"), "eb1": a("L0_ffn_expert_b1"), "ew2": a("L0_ffn_expert_w2"), "eb2": a("L0_ffn_expert_b2"),
        "ew3": a("L0_ffn_expert_w3"), "eb3": a("L0_ffn_expert_b3"),
    }
    nc = bacc.Bacc("TRN2", target_bir_lowering=False, num_devices=1)
    arrays, aps = {}, {"nc": nc}
    for name, value in data.items():
        arrays[f"in_{name}"] = value
        aps[name] = nc.dram_tensor(f"in_{name}", value.shape, mybir.dt.from_np(value.dtype), kind="ExternalInput").ap()
    aps["out"] = nc.dram_tensor("out_dram", (n, (h // STRIDE) ** 2, c), F32, kind="ExternalOutput").ap()
    return arrays, aps
```

```python
from contextlib import ExitStack

import concourse.bass as bass
from concourse import mybir

F32 = mybir.dt.float32
ALU = mybir.AluOpType
ACT = mybir.ActivationFunctionType
AX = mybir.AxisListType

P = 128
STRIDE = 4
HEADS = 8
EPS = 1e-5
EXPERTS = 6
VECS = ["L0_tok_ln_q_w", "L0_tok_ln_q_b", "L0_tok_ln_kv_w", "L0_tok_ln_kv_b", "L0_tok_proj_b",
        "L0_attn_ln_gamma", "L0_attn_ln_beta", "L0_attn_b_gate", "L0_attn_b_final"]
QW, QB, KVW, KVB, PB, GAMMA, BETA, BGATE, BFINAL = range(len(VECS))


def build(nc, x, wq_t, wkv, proj_t, wqkv_t, wgate_t, wfinal_t, vecs, ident_in, masks_in,
          rw1, rb1, rw2, rb2, ew1, eb1, ew2, eb2, ew3, eb3, out):
    NB, C, LOC, N2 = x.shape
    CH = C // P
    PIX = LOC * N2
    LH = LOC // P
    D = C // HEADS
    HPC = P // D
    GROUPS = PIX // P
    LPG = LOC // GROUPS
    QUARTERS = 4
    GPQ = GROUPS // QUARTERS
    PAIRS = GROUPS // 2
    GPH = GROUPS // 2
    LPQ = LOC // QUARTERS
    SH = LPG * HEADS
    assert C == 256 and LOC == 256 and GROUPS == 32 and SH == 64 and NB >= 3

    h1_dram = nc.dram_tensor("h1_scratch", (NB * LOC, C), F32, kind="Internal").ap()

    def at(index, per, n):
        return index * per + n

    def wait(eng, sem, value):
        if not (isinstance(value, int) and value <= 0):
            eng.wait_ge(sem, value)

    class Steps:
        def __init__(self, eng, signal, per):
            self.eng, self.counted, self.per = eng, signal, per

        def start(self, index):
            self.index, self.n = index, 0

        def __call__(self, ins):
            self.n += 1
            ins.then_inc(self.counted, 1)
            self.eng.wait_ge(self.counted, at(self.index, self.per, self.n))

        def finish(self):
            assert self.n == self.per, self.n

    def layer_stats(dve, src, n, tmp, mean_var, step, signal):
        for l in range(n):
            last = dve.bn_stats(tmp[:, l, 0:6], src[:, l, :])
        step(last)
        diff, squares = tmp[:, 0:n, 6], tmp[:, 0:n, 7]
        dve.tensor_tensor(squares, tmp[:, 0:n, 2], tmp[:, 0:n, 5], ALU.add)
        step(dve.tensor_tensor(diff, tmp[:, 0:n, 1], tmp[:, 0:n, 4], ALU.subtract))
        dve.scalar_tensor_tensor(mean_var[:, :, 0], diff, 0.5, tmp[:, 0:n, 4], ALU.mult, ALU.add)
        step(dve.scalar_tensor_tensor(mean_var[:, :, 1], diff, C / 4.0, diff, ALU.mult, ALU.mult))
        step(dve.tensor_tensor(squares, squares, mean_var[:, :, 1], ALU.add))
        dve.tensor_scalar(mean_var[:, :, 1], squares, 1.0 / C, EPS, ALU.mult, ALU.add).then_inc(signal, 1)

    with ExitStack() as whole:
        def sem(name):
            return whole.enter_context(nc.semaphore(name))

        setup_loads = sem("setup_loads")
        x_loaded = [sem(f"x_loaded{q}") for q in range(QUARTERS)]
        h1_stored = sem("h1_stored")
        su_v, su_p, su_a = sem("setup_vector"), sem("setup_tensor"), sem("setup_scalar")
        setup_done = sem("setup_done")
        feats_summed = sem("feats_summed")
        r_turned, r_taken, r_var, r_rstd = sem("r_turned"), sem("r_taken"), sem("r_var"), sem("r_rstd")
        rb_ready = sem("rb_ready")
        qn_ready, qn_turned, qn_taken = sem("qn_ready"), sem("qn_turned"), sem("qn_taken")
        q_made, q_taken = sem("q_made"), sem("q_taken")
        g_made, g_taken = sem("g_made"), sem("g_taken")
        xt_made, xt_taken, stats_done = sem("xt_made"), sem("xt_taken"), sem("stats_done")
        s_made, s_taken = sem("s_made"), sem("s_taken")
        pix_rstd = sem("pix_rstd")
        e_ready, e_turned, e_shifted, e_exped = sem("e_ready"), sem("e_turned"), sem("e_shifted"), sem("e_exped")
        p_ready, p_turned, p_taken, p_spread = sem("p_ready"), sem("p_turned"), sem("p_taken"), sem("p_spread")
        z_made, z_taken = sem("z_made"), sem("z_taken")
        agg_made, agg_taken = sem("agg_made"), sem("agg_taken")
        proj_made, h0_ready = sem("proj_made"), sem("h0_ready")
        t_chain, r_chain = sem("tokenizer_vector_steps"), sem("feats_vector_steps")
        h0_var, h0_rstd, h0_twice = sem("h0_var"), sem("h0_rstd"), sem("h0_twice")
        pool_t_chain = sem("tokenizer_pool_steps")
        h_turned, h_taken = sem("h_turned"), sem("h_taken")
        n_ready, n_turned, n_taken = sem("n_ready"), sem("n_turned"), sem("n_taken")
        aq_made, aq_taken, qm_ready = sem("aq_made"), sem("aq_taken"), sem("q_masked_ready")
        ak_made, ak_taken = sem("ak_made"), sem("ak_taken")
        av_made, av_taken = sem("av_made"), sem("av_taken")
        gate_made, gate_taken = sem("gate_made"), sem("gate_taken")
        as_made, as_max, as_exped = sem("as_made"), sem("as_max"), sem("as_exped")
        vs_ready = sem("vs_ready")
        ao_made, ao_taken = sem("ao_made"), sem("ao_taken")
        fin_made, u_var, u_rstd, h1_ready = sem("fin_made"), sem("u_var"), sem("u_rstd"), sem("h1_ready")
        a_chain = sem("attention_vector_steps")

        banks = [whole.enter_context(nc.psum_tensor(f"bank{i}", [P, 512], F32)) for i in range(8)]

        def sb(stack, name, *shape):
            return stack.enter_context(nc.sbuf_tensor(name, [P, *shape], F32))

        ident = sb(whole, "ident", P)
        halves = sb(whole, "minus_half", 8)

        def halved(bank):
            return banks[bank][:, :].rearrange("p (a b) -> p a b", a=2)

        with ExitStack() as one:
            X = sb(one, "x_image", CH, PIX)
            XT = sb(one, "x_turned", GROUPS, C)
            G = sb(one, "score_weights", CH, LOC, HEADS)
            A = sb(one, "attn_spread", GROUPS, LPG, HEADS)
            Z = sb(one, "pooled_pixels", CH, HEADS, LOC)
            WQ, WKm, WVm = sb(one, "wq", CH, C), sb(one, "wk_masked", HEADS, C), sb(one, "wv_masked", CH, HEADS, P)
            PW, WA = sb(one, "w_proj", CH, C), sb(one, "w_qkv", CH, 3 * C)
            WG, WF = sb(one, "w_gate", CH, C), sb(one, "w_final", CH, C)
            pixmask = sb(one, "pixel_token_mask", SH)
            headmask = sb(one, "head_mask", HPC)
            vcol = sb(one, "vectors_cols", len(VECS), CH)
            pb_row, vb_row, bf_row = sb(one, "proj_b_row", C), sb(one, "v_bias_row", C), sb(one, "b_final_row", C)
            bq_col, aq_bias, bk_col, gb_half = sb(one, "bq_col", CH), sb(one, "aq_bias", CH), sb(one, "bk_col", CH), sb(one, "gate_b_halved", CH)
            c_eps, quarter_c = sb(one, "eps_times_c", GPQ), sb(one, "quarter_of_c", GPQ)
            R = sb(one, "feats", CH, LOC)
            RT, RTB = sb(one, "feats_turned", LH, C), sb(one, "feats_plus_bias", LH, C)
            QNT, QN, Q = sb(one, "qn_tokens", LH, C), sb(one, "qn", CH, LOC), sb(one, "q", CH, LOC)
            bnt, mv, rstd2 = sb(one, "bn_tmp", LH, 8), sb(one, "mean_var", LH, 2), sb(one, "rstd2", LH)
            st, vt, RS = sb(one, "bn_pixels", GROUPS, 6), sb(one, "var_pixels", 2, GROUPS), sb(one, "rstd_pixels", GROUPS)
            SM, E = sb(one, "scores_masked", GPQ, SH), sb(one, "scores", GROUPS, HEADS)
            mx, den = sb(one, "softmax_max", 2, LPG), sb(one, "softmax_sum", 2, LPG)
            PE_, PR = sb(one, "softmax_exp", 2, LPG, N2), sb(one, "attn_scaled", GROUPS, HEADS)
            AG = sb(one, "aggregated", CH, LOC)
            H0, H2 = sb(one, "h0", LH, C), sb(one, "h0_twice_b", LH, C)
            amv, arstd = sb(one, "mean_var_attn", LH, 2), sb(one, "rstd_attn", LH)
            NT, HT = sb(one, "normed_turned", CH, LOC), sb(one, "h0_turned", CH, LOC)
            QM, K = sb(one, "q_masked", HEADS, LOC), sb(one, "k", CH, LOC)
            V, VS = sb(one, "v", LH, HEADS, D), sb(one, "v_scaled_masked", LH, HEADS, P)
            GT = sb(one, "gate", CH, LOC)
            EX = sb(one, "attn_exp", HEADS, LH, LOC)
            nmax, esum = sb(one, "minus_max", HEADS, LH), sb(one, "exp_sum", HEADS, LH)
            O, U = GT, H2
            AQ = AG
            NH = QNT
            H1 = sb(one, "h1", LH, C)
            bmv, brstd = sb(one, "mean_var_out", LH, 2), sb(one, "rstd_out", LH)

            def stage(start, width, chunks=CH):
                return XT[:, :, :].rearrange("p a b -> p (a b)")[:, start:start + chunks * width].rearrange(
                    "p (c w) -> p c w", c=chunks)

            raw_wq, raw_wk, raw_wv = stage(0, C), stage(512, C), stage(1024, C)
            raw_wqkv = stage(1536, 3 * C)
            row_w, row_b = stage(3072, C, 1)[:, 0, :], stage(3328, C, 1)[:, 0, :]
            beta_wide, bv_wide = stage(3584, P), stage(3840, P)
            wtmp = stage(4096, C)
            wmean = stage(4608, 1)
            bv_col = stage(4612, 1)
            ones = stage(4736, P, 1)[:, 0, :]
            pb_raw = stage(4864, C, 1)[:, 0, :]

            x_img = x.rearrange("b (c p) l n -> b p c (l n)", p=P)
            h1_img = h1_dram.rearrange("(b h p) c -> b p h c", h=LH, p=P)
            QP = PIX // QUARTERS

            def halves_of(w):
                return w.rearrange("(c p) n -> p c n", p=P)

            SCORE_SLOTS = (3, 4, 5, 6, 7, 9, 10, 12)

            block = one.enter_context(nc.Block())

            @block.sync
            def _(sp):
                def load_quarter(t, q):
                    wait(sp, s_made, at(t, QUARTERS, q + 1 - QUARTERS))
                    wait(sp, feats_summed, at(t, QUARTERS, q + 1 - QUARTERS))
                    sp.dma_start(X[:, :, q * QP:(q + 1) * QP],
                                 x_img[t, :, :, q * QP:(q + 1) * QP]).then_inc(x_loaded[q], 16)

                def store_h1(a):
                    wait(sp, h1_ready, at(a, 1, 1))
                    sp.dma_start(h1_img[a], H1[:, :, :]).then_inc(h1_stored, 16)

                setup = [
                    (raw_wq, halves_of(wq_t)), (raw_wk, halves_of(wkv[0:C, :])), (raw_wv, halves_of(wkv[C:2 * C, :])),
                    (raw_wqkv, halves_of(wqkv_t)), (PW[:, :, :], halves_of(proj_t)), (WG[:, :, :], halves_of(wgate_t)),
                    (WF[:, :, :], halves_of(wfinal_t)), (ident[:, :], ident_in),
                    (pixmask[:, :], masks_in[:, 0:SH]), (headmask[:, :], masks_in[:, SH:SH + HPC]),
                    (row_w, vecs[KVW, :].partition_broadcast(P)), (row_b, vecs[KVB, :].partition_broadcast(P)),
                    (pb_raw, vecs[PB, :].partition_broadcast(P)), (bf_row[:, :], vecs[BFINAL, :].partition_broadcast(P)),
                ]
                for dst, src in setup:
                    sp.dma_start(dst, src).then_inc(setup_loads, 16)
                with nc.allow_non_contiguous_dma(reason="a few hundred values, once"):
                    for v in range(len(VECS)):
                        sp.dma_start(vcol[:, v, :], vecs[v, :].rearrange("(c p) -> p c", p=P),
                                     allow_slow_non_contiguous=True).then_inc(setup_loads, 16)
                for q in range(QUARTERS):
                    load_quarter(0, q)
                for q in range(QUARTERS):
                    load_quarter(1, q)
                for q in range(QUARTERS):
                    load_quarter(2, q)
                store_h1(0)
                with sp.Fori(3, NB) as t:
                    for q in range(QUARTERS):
                        load_quarter(t, q)
                    store_h1(t - 2)
                store_h1(NB - 2)
                store_h1(NB - 1)
                sp.wait_ge(h1_stored, 16 * NB)

            SETUP_LOADS = 16 * (14 + len(VECS))

            @block.tensor
            def _(pe):
                mm = pe.matmul

                pe.wait_ge(setup_loads, SETUP_LOADS)
                for m in range(CH):
                    for c in range(CH):
                        mm(banks[0][:, m:m + 1], raw_wq[:, c, m * P:(m + 1) * P], vcol[:, QB, c:c + 1],
                           start=(c == 0), stop=(c == CH - 1)).then_inc(su_p, 1)
                for m in range(2 * CH):
                    for c in range(CH):
                        mm(banks[1][:, m:m + 1], raw_wqkv[:, c, m * P:(m + 1) * P], vcol[:, BETA, c:c + 1],
                           start=(c == 0), stop=(c == CH - 1)).then_inc(su_p, 1)
                pe.wait_ge(su_v, 11)
                for c in range(CH):
                    mm(banks[2][:, 0:C], beta_wide[:, c, :], raw_wqkv[:, c, 2 * C:3 * C],
                       start=(c == 0), stop=(c == CH - 1)).then_inc(su_p, 1)
                for c in range(CH):
                    mm(banks[3][:, 0:C], bv_wide[:, c, :], PW[:, c, :],
                       start=(c == 0), stop=(c == CH - 1)).then_inc(su_p, 1)
                pe.wait_ge(su_v, 17)
                for c in range(CH):
                    for m in range(CH):
                        pe.transpose(halved(4)[:, c, m * P:(m + 1) * P], wtmp[:, m, c * P:(c + 1) * P],
                                     ident[:, :]).then_inc(su_p, 1)
                pe.wait_ge(setup_done, 1)

                def turn_feats(t):
                    wait(pe, feats_summed, at(t, QUARTERS, QUARTERS))
                    wait(pe, s_taken, at(t, QUARTERS, 0))
                    for l in range(LH):
                        for c in range(CH):
                            last = pe.transpose(halved(2)[:, l, c * P:(c + 1) * P], R[:, c, l * P:(l + 1) * P], ident[:, :])
                    last.then_inc(r_turned, 1)

                def turn_qn(t):
                    wait(pe, qn_ready, at(t, 1, 1))
                    for c in range(CH):
                        for l in range(LH):
                            last = pe.transpose(halved(3)[:, c, l * P:(l + 1) * P], QNT[:, l, c * P:(c + 1) * P], ident[:, :])
                    last.then_inc(qn_turned, 1)

                def make_q(t):
                    wait(pe, qn_taken, at(t, 1, 1))
                    for m in range(CH):
                        for c in range(CH):
                            last = mm(halved(2)[:, m, :], WQ[:, c, m * P:(m + 1) * P], QN[:, c, :],
                                      start=(c == 0), stop=(c == CH - 1))
                    last.then_inc(q_made, 1)

                def make_g(t, steps):
                    for i in steps:
                        if i == 0:
                            wait(pe, q_taken, at(t, CH, CH))
                        pair, c = i // CH, i % CH
                        if i >= 2:
                            wait(pe, g_taken, at(t, HEADS, i - 1))
                        else:
                            wait(pe, z_taken, at(t, 2 * QUARTERS, i - 1))
                        for j in range(2):
                            h = 2 * pair + j
                            last = mm(halved(i % 2)[:, j, :], WKm[:, h, c * P:(c + 1) * P], Q[:, h // HPC, :],
                                      start=True, stop=True)
                        last.then_inc(g_made, 1)

                def pixels(c, g):
                    return X[:, c, g * P:(g + 1) * P]

                def turn_pair(t, p):
                    if p % (PAIRS // QUARTERS) == 0:
                        q = p // (PAIRS // QUARTERS)
                        wait(pe, x_loaded[q], at(t, 16, 16))
                    if p >= 2:
                        wait(pe, xt_taken, at(t, PAIRS, p - 1))
                    elif p == 0:
                        wait(pe, g_taken, at(t, HEADS, HEADS))
                    for j in range(2):
                        for c in range(CH):
                            last = pe.transpose(halved(p % 2)[:, j, c * P:(c + 1) * P], pixels(c, 2 * p + j), ident[:, :])
                    last.then_inc(xt_made, 1)

                def score_pair(t, p):
                    ppq = PAIRS // QUARTERS
                    q = p // ppq
                    if p % ppq == 0 and q >= 2:
                        wait(pe, s_taken, at(t, QUARTERS, q - 1))
                    for j in range(2):
                        g = 2 * p + j
                        for c in range(CH):
                            last = mm(banks[2 + q % 2][:, (g % GPQ) * SH:(g % GPQ + 1) * SH], pixels(c, g),
                                      G[:, c, g * LPG:(g + 1) * LPG, :], start=(c == 0), stop=(c == CH - 1))
                    if p % ppq == ppq - 1:
                        last.then_inc(s_made, 1)

                def turn_scores(t, u):
                    wait(pe, e_ready, at(t, 2, u + 1))
                    wait(pe, p_taken, at(t, 2, u))
                    pe.transpose(banks[4][:, 0:P], E[:, u * GPH:(u + 1) * GPH, :].rearrange("p g h -> p (g h)"),
                                 ident[:, :]).then_inc(e_turned, 1)

                def turn_probs(t, u):
                    wait(pe, p_ready, at(t, 2, u + 1))
                    pe.transpose(banks[4][:, 0:P], PE_[:, u, :, :].rearrange("p l n -> p (l n)"),
                                 ident[:, :]).then_inc(p_turned, 1)

                def pool_pixels(t, steps):
                    for i in steps:
                        q, c = i // CH, i % CH
                        if c == 0:
                            wait(pe, p_spread, at(t, QUARTERS, q + 1))
                        if i >= 2:
                            wait(pe, z_taken, at(t, 2 * QUARTERS, i - 1))
                        elif i == 0:
                            wait(pe, xt_taken, at(t, PAIRS, PAIRS))
                        for g in range(q * GPQ, (q + 1) * GPQ):
                            last = mm(banks[i % 2][:, (g % GPQ) * SH:(g % GPQ + 1) * SH], XT[:, g, c * P:(c + 1) * P],
                                      A[:, g, :, :], start=True, stop=True)
                        last.then_inc(z_made, 1)

                def aggregate(t):
                    wait(pe, z_taken, at(t, 2 * QUARTERS, 2 * QUARTERS))
                    for m in range(CH):
                        for j in range(HPC):
                            for c in range(CH):
                                last = mm(halved(4)[:, m, :], WVm[:, c, m * HPC + j, :], Z[:, c, m * HPC + j, :],
                                          start=(j == 0 and c == 0), stop=(j == HPC - 1 and c == CH - 1))
                    last.then_inc(agg_made, 1)

                def project(t):
                    wait(pe, agg_taken, at(t, 1, 1))
                    for l in range(LH):
                        for c in range(CH):
                            last = mm(halved(3)[:, l, :], AG[:, c, l * P:(l + 1) * P], PW[:, c, :],
                                      start=(c == 0), stop=(c == CH - 1))
                    last.then_inc(proj_made, 1)

                def turn_tokens(a, src, ready, turned):
                    for c in range(CH):
                        for l in range(LH):
                            last = pe.transpose(halved(5)[:, c, l * P:(l + 1) * P], src[:, l, c * P:(c + 1) * P], ident[:, :])
                    last.then_inc(turned, 1)

                def turn_h0(a):
                    wait(pe, h0_ready, at(a, 1, 1))
                    wait(pe, u_var, at(a, 1, 0))
                    turn_tokens(a, H0, h0_ready, h_turned)

                def turn_n(a):
                    wait(pe, n_ready, at(a, 1, 1))
                    wait(pe, h_taken, at(a, 1, 1))
                    turn_tokens(a, NH, n_ready, n_turned)

                def rows_of(bank, w, first, src, made):
                    for m in range(CH):
                        for c in range(CH):
                            last = mm(halved(bank)[:, m, :], w[:, c, first + m * P:first + (m + 1) * P], src[:, c, :],
                                      start=(c == 0), stop=(c == CH - 1))
                    last.then_inc(made, 1)

                def tokens_of(bank, w, first, src, made):
                    for l in range(LH):
                        for c in range(CH):
                            last = mm(halved(bank)[:, l, :], src[:, c, l * P:(l + 1) * P], w[:, c, first:first + C],
                                      start=(c == 0), stop=(c == CH - 1))
                    last.then_inc(made, 1)

                def attn_q(a):
                    wait(pe, n_taken, at(a, 1, 1))
                    rows_of(5, WA, 0, NT, aq_made)

                def attn_k(a):
                    wait(pe, ao_taken, at(a, CH, 0))
                    rows_of(6, WA, C, NT, ak_made)

                def attn_v(a):
                    tokens_of(7, WA, 2 * C, NT, av_made)

                def attn_gate(a):
                    wait(pe, aq_taken, at(a, CH, CH))
                    rows_of(5, WG, 0, HT, gate_made)

                def attn_scores(a, h):
                    if h == 0:
                        wait(pe, ak_taken, at(a, CH, CH))
                    elif h == 1:
                        wait(pe, av_taken, at(a, 1, 1))
                    else:
                        wait(pe, as_exped, at(a, HEADS * LH, (h - 1) * LH))
                    wait(pe, qm_ready, at(a, HEADS, h + 1))
                    for i in range(LH):
                        last = mm(halved(6 + h % 2)[:, i, :], QM[:, h, i * P:(i + 1) * P], K[:, h // HPC, :],
                                  start=True, stop=True)
                    last.then_inc(as_made, 1)

                def attn_out(a, m):
                    wait(pe, vs_ready, at(a, CH, m + 1))
                    if m == 0:
                        wait(pe, as_exped, at(a, HEADS * LH, (HEADS - 1) * LH))
                    else:
                        wait(pe, as_exped, at(a, HEADS * LH, HEADS * LH))
                    for j in range(HPC):
                        for i in range(LH):
                            last = mm(banks[6 + m][:, 0:LOC], VS[:, i, m * HPC + j, :], EX[:, m * HPC + j, i, :],
                                      start=(j == 0 and i == 0), stop=(j == HPC - 1 and i == LH - 1))
                    last.then_inc(ao_made, 1)

                def attn_final(a):
                    wait(pe, ao_taken, at(a, CH, CH))
                    wait(pe, gate_taken, at(a, CH, CH))
                    tokens_of(5, WF, 0, O, fin_made)

                def image(t, a, more=True):
                    T, B = t is not None, a is not None
                    if T: make_g(t, range(0, 4))
                    if B: turn_h0(a)
                    if T: make_g(t, range(4, 6))
                    if B: turn_n(a)
                    if T: make_g(t, range(6, 8))
                    if B: attn_q(a)
                    for p in range(PAIRS):
                        if T:
                            turn_pair(t, p)
                            if p: score_pair(t, p - 1)
                            if p == 11: turn_scores(t, 0)
                        if B:
                            if p == 0: attn_k(a)
                            if p == 1: attn_v(a)
                            if p == 2: attn_gate(a)
                            if p in SCORE_SLOTS: attn_scores(a, SCORE_SLOTS.index(p))
                    if T:
                        score_pair(t, PAIRS - 1)
                        turn_probs(t, 0)
                    if B: attn_out(a, 0)
                    if T: turn_scores(t, 1)
                    if B: attn_out(a, 1)
                    if T:
                        pool_pixels(t, range(0, 2))
                        turn_probs(t, 1)
                        pool_pixels(t, range(2, 4))
                    if T:
                        pool_pixels(t, range(4, 6))
                        if more: turn_feats(t + 1)
                        pool_pixels(t, range(6, 8))
                    if B: attn_final(a)
                    if T:
                        if more: turn_qn(t + 1)
                        aggregate(t)
                        if more: make_q(t + 1)
                        project(t)

                turn_feats(0)
                turn_qn(0)
                make_q(0)
                image(0, None)
                image(1, 0)
                with pe.Fori(2, NB - 1) as t:
                    image(t, t - 1)
                image(NB - 1, NB - 2, more=False)
                image(None, NB - 1)

            @block.scalar
            def _(act):
                def copy(out, in_):
                    return act.activation(out, in_, ACT.Copy)

                act.wait_ge(setup_done, 1)

                def take_r(t):
                    wait(act, r_turned, at(t, 1, 1))
                    wait(act, rb_ready, at(t, 1, 0))
                    act.activation(RT[:, :, :], halved(2), ACT.Copy, scale=1.0 / N2).then_inc(r_taken, 1)

                def take_qn(t):
                    wait(act, qn_turned, at(t, 1, 1))
                    wait(act, q_made, at(t, 1, 0))
                    copy(QN[:, :, :], halved(3)).then_inc(qn_taken, 1)

                def take_q(t):
                    wait(act, q_made, at(t, 1, 1))
                    wait(act, g_made, at(t, HEADS, 0))
                    for m in range(CH):
                        act.activation(Q[:, m, :], halved(2)[:, m, :], ACT.Identity, bias=bq_col[:, m:m + 1],
                                       scale=1.0).then_inc(q_taken, 1)

                def take_g(t, i):
                    pair, c = i // CH, i % CH
                    wait(act, g_made, at(t, HEADS, i + 1))
                    wait(act, s_made, at(t, QUARTERS, 0))
                    copy(G[:, c, :, 2 * pair:2 * pair + 2].rearrange("p l h -> p h l"),
                         halved(i % 2)).then_inc(g_taken, 1)

                def take_xt(t, p):
                    wait(act, xt_made, at(t, PAIRS, p + 1))
                    if p == 0:
                        wait(act, z_made, at(t, 2 * QUARTERS, 0))
                        wait(act, stats_done, at(t, GROUPS, 0))
                    copy(XT[:, 2 * p:2 * p + 2, :], halved(p % 2)).then_inc(xt_taken, 1)

                def exp_scores(t, u):
                    wait(act, e_shifted, at(t, 2, u + 1))
                    act.activation(PE_[:, u, :, :], PE_[:, u, :, :], ACT.Exp).then_inc(e_exped, 1)

                def take_z(t, i):
                    q, c = i // CH, i % CH
                    wait(act, z_made, at(t, 2 * QUARTERS, i + 1))
                    wait(act, agg_made, at(t, 1, 0))
                    copy(Z[:, c, :, q * GPQ * LPG:(q + 1) * GPQ * LPG],
                         banks[i % 2][:, :].rearrange("p (l h) -> p h l", h=HEADS)).then_inc(z_taken, 1)

                def take_agg(t):
                    wait(act, agg_made, at(t, 1, 1))
                    wait(act, proj_made, at(t, 1, 0))
                    copy(AG[:, :, :], halved(4)).then_inc(agg_taken, 1)

                def take_h(a):
                    wait(act, h_turned, at(a, 1, 1))
                    wait(act, gate_made, at(a, 1, 0))
                    copy(HT[:, :, :], halved(5)).then_inc(h_taken, 1)

                def take_n(a):
                    wait(act, n_turned, at(a, 1, 1))
                    wait(act, av_made, at(a, 1, 0))
                    copy(NT[:, :, :], halved(5)).then_inc(n_taken, 1)

                def take_attn_q(a):
                    wait(act, aq_made, at(a, 1, 1))
                    for m in range(CH):
                        act.activation(AQ[:, m, :], halved(5)[:, m, :], ACT.Identity, bias=aq_bias[:, m:m + 1],
                                       scale=float(D) ** -0.5).then_inc(aq_taken, 1)

                def take_attn_k(a):
                    wait(act, ak_made, at(a, 1, 1))
                    for m in range(CH):
                        act.activation(K[:, m, :], halved(6)[:, m, :], ACT.Identity,
                                       bias=bk_col[:, m:m + 1]).then_inc(ak_taken, 1)

                def take_gate(a):
                    wait(act, gate_made, at(a, 1, 1))
                    wait(act, fin_made, at(a, 1, 0))
                    for m in range(CH):
                        act.activation(GT[:, m, :], halved(5)[:, m, :], ACT.Tanh, bias=gb_half[:, m:m + 1],
                                       scale=0.5).then_inc(gate_taken, 1)

                def exp_attn(a, h):
                    wait(act, as_max, at(a, HEADS, h + 1))
                    if h == 0:
                        wait(act, ao_made, at(a, CH, 0))
                        wait(act, vs_ready, at(a, CH, 0))
                    for i in range(LH):
                        act.activation(EX[:, h, i, :], halved(6 + h % 2)[:, i, :], ACT.Exp, bias=nmax[:, h, i:i + 1],
                                       accum_out=esum[:, h, i:i + 1]).then_inc(as_exped, 1)

                def take_gs(t, steps):
                    for i in steps:
                        take_g(t, i)

                def take_zs(t, steps):
                    for i in steps:
                        take_z(t, i)

                def image(t, a, more=True):
                    T, B = t is not None, a is not None
                    if T: take_gs(t, range(0, 4))
                    if B: take_h(a)
                    if T: take_gs(t, range(4, 6))
                    if B: take_n(a)
                    if T: take_gs(t, range(6, 8))
                    for p in range(PAIRS):
                        if T: take_xt(t, p)
                        if B:
                            if p == 0: take_attn_q(a)
                            if p == 1: take_attn_k(a)
                            if p == 3: take_gate(a)
                            if p - 1 in SCORE_SLOTS: exp_attn(a, SCORE_SLOTS.index(p - 1))
                        if T and p == 12: exp_scores(t, 0)
                    if T:
                        exp_scores(t, 1)
                        take_zs(t, range(0, 6))
                        if more: take_r(t + 1)
                        take_zs(t, range(6, 8))
                        if more: take_qn(t + 1)
                        take_agg(t)
                        if more: take_q(t + 1)

                take_r(0)
                take_qn(0)
                take_q(0)
                image(0, None)
                image(1, 0)
                with act.Fori(2, NB - 1) as t:
                    image(t, t - 1)
                image(NB - 1, NB - 2, more=False)
                image(None, NB - 1)

            T_LINKS, A_LINKS = 14, 7

            @block.vector
            def _(dve):
                dve.memset(halves[:, :], -0.5).then_inc(su_v, 1)
                dve.memset(ones, 1.0).then_inc(su_v, 1)
                dve.memset(c_eps[:, :], C * EPS).then_inc(su_v, 1)
                dve.memset(quarter_c[:, :], C / 4.0).then_inc(su_v, 1)
                dve.memset(WVm[:, :, :, :], 0.0).then_inc(su_v, 1)
                dve.memset(VS[:, :, :, :], 0.0).then_inc(su_v, 1)
                dve.wait_ge(setup_loads, SETUP_LOADS)
                dve.wait_ge(su_v, 6)
                dve.tensor_tensor(wtmp, raw_wv, row_b.unsqueeze(1).to_broadcast([P, CH, C]), ALU.mult).then_inc(su_v, 1)
                dve.wait_ge(su_v, 7)
                dve.tensor_reduce(bv_col[:, :, 0], wtmp, AX.X, ALU.add).then_inc(su_v, 1)
                dve.wait_ge(su_v, 8)
                for c in range(CH):
                    dve.tensor_scalar(bv_wide[:, c, :], ones, bv_col[:, c, :], None, ALU.mult).then_inc(su_v, 1)
                dve.tensor_tensor(beta_wide, vcol[:, BETA, :].unsqueeze(2).to_broadcast([P, CH, P]),
                                  ones.unsqueeze(1).to_broadcast([P, CH, P]), ALU.mult).then_inc(su_v, 1)
                n = 11
                for raw in (raw_wk, raw_wv):
                    if raw is raw_wv:
                        dve.wait_ge(su_v, n)
                    dve.tensor_tensor(wtmp if raw is raw_wv else raw_wk, raw,
                                      row_w.unsqueeze(1).to_broadcast([P, CH, C]), ALU.mult).then_inc(su_v, 1)
                    dst = wtmp if raw is raw_wv else raw_wk
                    n += 1
                    dve.wait_ge(su_v, n)
                    dve.tensor_reduce(wmean[:, :, 0], dst, AX.X, ALU.add).then_inc(su_v, 1)
                    n += 1
                    dve.wait_ge(su_v, n)
                    dve.scalar_tensor_tensor(dst, wmean.to_broadcast([P, CH, C]), -1.0 / C, dst,
                                             ALU.mult, ALU.add).then_inc(su_v, 1)
                    n += 1
                assert n == 17
                dve.wait_ge(su_v, n)
                for h in range(HEADS):
                    dve.tensor_scalar(WKm[:, h, :], raw_wk[:, h // HPC, :], headmask[:, h % HPC:h % HPC + 1], None,
                                      ALU.mult).then_inc(su_v, 1)
                dve.tensor_scalar(gb_half[:, :], vcol[:, BGATE, :], 0.5, None, ALU.mult).then_inc(su_v, 1)
                dve.tensor_scalar(WF[:, :, :], WF[:, :, :], 0.5, None, ALU.mult).then_inc(su_v, 1)
                for c in range(CH):
                    dve.tensor_scalar(WQ[:, c, :], raw_wq[:, c, :], vcol[:, QW, c:c + 1], None, ALU.mult).then_inc(su_v, 1)
                    dve.tensor_scalar(WA[:, c, :], raw_wqkv[:, c, :], vcol[:, GAMMA, c:c + 1], None, ALU.mult).then_inc(su_v, 1)
                SU_P = 2 * CH + 4 * CH + 2 * CH + CH * CH
                dve.wait_ge(su_p, SU_P)
                dve.tensor_copy(bq_col[:, :], banks[0][:, 0:CH]).then_inc(su_v, 1)
                dve.tensor_scalar(aq_bias[:, :], banks[1][:, 0:CH], float(D) ** -0.5, None, ALU.mult).then_inc(su_v, 1)
                dve.tensor_copy(bk_col[:, :], banks[1][:, CH:2 * CH]).then_inc(su_v, 1)
                dve.tensor_copy(vb_row[:, :], banks[2][:, 0:C]).then_inc(su_v, 1)
                dve.tensor_tensor(pb_row[:, :], banks[3][:, 0:C], pb_raw, ALU.add).then_inc(su_v, 1)
                n += HEADS + 2 + 2 * CH + 5
                dve.wait_ge(su_v, n)
                for m in range(CH):
                    for j in range(HPC):
                        h = m * HPC + j
                        dve.tensor_copy(WVm[:, :, h, j * D:(j + 1) * D], halved(4)[:, :, h * D:(h + 1) * D]).then_inc(su_v, 1)
                n += HEADS
                dve.wait_ge(su_v, n)
                dve.nop().then_inc(setup_done, 1)

                tstep, astep = Steps(dve, t_chain, T_LINKS), Steps(dve, a_chain, A_LINKS)
                rstep = Steps(dve, r_chain, 4)

                def sum_feats(t, q, c):
                    wait(dve, x_loaded[q], at(t, 16, 16))
                    wait(dve, r_turned, at(t, 1, 0))
                    ins = dve.tensor_reduce(R[:, c, q * LPQ:(q + 1) * LPQ], X[:, c, q * QP:(q + 1) * QP].rearrange(
                        "p (l n) -> p l n", n=N2), AX.X, ALU.add)
                    if c == CH - 1:
                        ins.then_inc(feats_summed, 1)

                def stats(src, n, mean_var, step, signal):
                    layer_stats(dve, src, n, bnt, mean_var, step, signal)

                def stats_r(t):
                    wait(dve, r_taken, at(t, 1, 1))
                    rstep.start(t)
                    stats(RT, LH, mv, rstep, r_var)
                    rstep.finish()

                def norm_q(t):
                    wait(dve, r_rstd, at(t, 1, 1))
                    for l in range(LH):
                        ins = dve.tensor_scalar(QNT[:, l, :], RT[:, l, :], mv[:, l, 0:1], rstd2[:, l:l + 1],
                                                ALU.subtract, ALU.mult)
                    ins.then_inc(qn_ready, 1)

                def pixel_stats(t, p):
                    wait(dve, xt_taken, at(t, PAIRS, p + 1))
                    for j in range(2):
                        dve.bn_stats(st[:, 2 * p + j, :], XT[:, 2 * p + j, :]).then_inc(stats_done, 1)

                def take_scores(t, q):
                    wait(dve, s_made, at(t, QUARTERS, q + 1))
                    dve.tensor_tensor(SM[:, :, :], banks[2 + q % 2][:, :].rearrange("p (g s) -> p g s", g=GPQ),
                                      pixmask[:, :].unsqueeze(1).to_broadcast([P, GPQ, SH]), ALU.mult).then_inc(s_taken, 1)
                    dve.wait_ge(s_taken, at(t, QUARTERS, q + 1))
                    tstep(dve.tensor_reduce(E[:, q * GPQ:(q + 1) * GPQ, :],
                                            SM[:, :, :].rearrange("p g (l h) -> p g h l", h=HEADS), AX.X, ALU.add))

                def by_head(u):
                    return RS[:, u * GPH:(u + 1) * GPH].unsqueeze(2).to_broadcast([P, GPH, HEADS])

                def scale_scores(t, u):
                    wait(dve, pix_rstd, at(t, QUARTERS, 2 * u + 2))
                    half = E[:, u * GPH:(u + 1) * GPH, :]
                    dve.tensor_tensor(half, half, by_head(u), ALU.mult).then_inc(e_ready, 1)

                def over_pixels(ap):
                    return ap.unsqueeze(2).to_broadcast([P, LPG, N2])

                def softmax_shift(t, u):
                    wait(dve, e_turned, at(t, 2, u + 1))
                    src = banks[4][:, 0:P].rearrange("p (l n) -> p l n", n=N2)
                    tstep(dve.tensor_reduce(mx[:, u, :], src, AX.X, ALU.max))
                    dve.tensor_tensor(PE_[:, u, :, :], src, over_pixels(mx[:, u, :]), ALU.subtract).then_inc(e_shifted, 1)

                def softmax_divide(t, u):
                    wait(dve, e_exped, at(t, 2, u + 1))
                    tstep(dve.tensor_reduce(den[:, u, :], PE_[:, u, :, :], AX.X, ALU.add))
                    tstep(dve.reciprocal(den[:, u, :], den[:, u, :]))
                    dve.tensor_tensor(PE_[:, u, :, :], PE_[:, u, :, :], over_pixels(den[:, u, :]), ALU.mult).then_inc(p_ready, 1)

                def take_probs(t, u):
                    wait(dve, p_turned, at(t, 2, u + 1))
                    wait(dve, p_spread, at(t, QUARTERS, 2 * u + 2 - QUARTERS))
                    dve.scalar_tensor_tensor(PR[:, u * GPH:(u + 1) * GPH, :], banks[4][:, 0:P].rearrange("p (g h) -> p g h", h=HEADS),
                                             float(C) ** 0.5, by_head(u), ALU.mult, ALU.mult).then_inc(p_taken, 1)

                def take_h0(t):
                    wait(dve, proj_made, at(t, 1, 1))
                    wait(dve, rb_ready, at(t, 1, 1))
                    wait(dve, h0_twice, at(t, 1, 0))
                    dve.tensor_tensor(H0[:, :, :], halved(3), RTB[:, :, :], ALU.add).then_inc(h0_ready, 1)
                    dve.wait_ge(h0_ready, at(t, 1, 1))

                def norm_h0(a, t):
                    wait(dve, h0_rstd, at(a, 1, 1))
                    if t is not None:
                        wait(dve, qn_turned, at(t, 1, 1))
                    for l in range(LH):
                        ins = dve.tensor_scalar(NH[:, l, :], H0[:, l, :], amv[:, l, 0:1], arstd[:, l:l + 1],
                                                ALU.subtract, ALU.mult)
                    ins.then_inc(n_ready, 1)

                def take_v(a):
                    wait(dve, av_made, at(a, 1, 1))
                    dve.tensor_tensor(V[:, :, :, :].rearrange("p l h d -> p l (h d)"), halved(7),
                                      vb_row[:, :].unsqueeze(1).to_broadcast([P, LH, C]), ALU.add).then_inc(av_taken, 1)

                def max_attn(a, h):
                    wait(dve, as_made, at(a, HEADS, h + 1))
                    dve.tensor_reduce(nmax[:, h, :], halved(6 + h % 2), AX.X, ALU.max, negate=True).then_inc(as_max, 1)

                def scale_v(a, m):
                    heads = slice(m * HPC, (m + 1) * HPC)
                    wait(dve, as_exped, at(a, HEADS * LH, (m + 1) * HPC * LH))
                    astep(dve.reciprocal(esum[:, heads, :], esum[:, heads, :]))
                    for j in range(HPC):
                        h = m * HPC + j
                        ins = dve.tensor_tensor(VS[:, :, h, j * D:(j + 1) * D], V[:, :, h, :],
                                                esum[:, h, :].unsqueeze(2).to_broadcast([P, LH, D]), ALU.mult)
                    ins.then_inc(vs_ready, 1)

                def gate_out(a, m):
                    wait(dve, ao_made, at(a, CH, m + 1))
                    if m == 0:
                        wait(dve, gate_taken, at(a, CH, CH))
                    dve.scalar_tensor_tensor(O[:, m, :], GT[:, m, :], 1.0, banks[6 + m][:, 0:LOC],
                                             ALU.add, ALU.mult).then_inc(ao_taken, 1)

                def add_attn(a):
                    wait(dve, fin_made, at(a, 1, 1))
                    wait(dve, h0_twice, at(a, 1, 1))
                    astep(dve.tensor_tensor(U[:, :, :], halved(5), H2[:, :, :], ALU.add))
                    stats(U, LH, bmv, astep, u_var)

                def norm_u(a):
                    wait(dve, u_rstd, at(a, 1, 1))
                    wait(dve, h1_stored, at(a, 16, 0))
                    for l in range(LH):
                        ins = dve.tensor_scalar(H1[:, l, :], U[:, l, :], bmv[:, l, 0:1], brstd[:, l:l + 1],
                                                ALU.subtract, ALU.mult)
                    ins.then_inc(h1_ready, 1)

                def image(t, a, more=True):
                    T, B = t is not None, a is not None
                    if T: tstep.start(t)
                    if B: astep.start(a)
                    if B: norm_h0(a, t)
                    for p in range(PAIRS):
                        if T and p == 10: scale_scores(t, 0)
                        if T and p == 12: softmax_shift(t, 0)
                        if T and p == 13: softmax_divide(t, 0)
                        if B and p - 1 in SCORE_SLOTS: max_attn(a, SCORE_SLOTS.index(p - 1))
                        if T:
                            if p in (5, 9, 13): take_scores(t, (p - 5) // 4)
                            pixel_stats(t, p)
                        if B:
                            if p == 2: take_v(a)
                            if p == 11: scale_v(a, 0)
                        if T and more and p in (7,): sum_feats(t + 1, 0, p // 15)
                    if T:
                        take_probs(t, 0)
                        take_scores(t, QUARTERS - 1)
                    if B: scale_v(a, 1)
                    if T:
                        scale_scores(t, 1)
                        if more: sum_feats(t + 1, 0, 1)
                        softmax_shift(t, 1)
                        if more: sum_feats(t + 1, 1, 0)
                        softmax_divide(t, 1)
                        if more: sum_feats(t + 1, 1, 1)
                        take_probs(t, 1)
                        if more: sum_feats(t + 1, 2, 0)
                    if B: gate_out(a, 0)
                    if T and more:
                        sum_feats(t + 1, 2, 1)
                        sum_feats(t + 1, 3, 0)
                        sum_feats(t + 1, 3, 1)
                    if B: gate_out(a, 1)
                    if T and more:
                        stats_r(t + 1)
                        norm_q(t + 1)
                    if B:
                        add_attn(a)
                        norm_u(a)
                    if T:
                        take_h0(t)
                        stats(H0, LH, amv, tstep, h0_var)
                        tstep.finish()
                    if B: astep.finish()

                for q in range(QUARTERS):
                    for c in range(CH):
                        sum_feats(0, q, c)
                stats_r(0)
                norm_q(0)
                image(0, None)
                image(1, 0)
                with dve.Fori(2, NB - 1) as t:
                    image(t, t - 1)
                image(NB - 1, NB - 2, more=False)
                image(None, NB - 1)

            @block.gpsimd
            def _(pool):
                tstep = Steps(pool, pool_t_chain, 3 + 4 * QUARTERS)
                pool.wait_ge(setup_done, 1)

                def root(out, var, signal):
                    pool.tensor_tensor(out, var, halves[:, 0:out.shape[1]], ALU.pow).then_inc(signal, 1)

                def feats_rstd(t):
                    wait(pool, r_var, at(t, 1, 1))
                    root(rstd2[:, :], mv[:, :, 1], r_rstd)

                def feats_bias(t):
                    wait(pool, h0_ready, at(t, 1, 0))
                    pool.tensor_tensor(RTB[:, :, :], RT[:, :, :], pb_row[:, :].unsqueeze(1).to_broadcast([P, LH, C]),
                                       ALU.add).then_inc(rb_ready, 1)

                def pixel_rstd(t, q):
                    groups = slice(q * GPQ, (q + 1) * GPQ)
                    wait(pool, stats_done, at(t, GROUPS, (q + 1) * GPQ))
                    diff, sq = vt[:, 0, groups], vt[:, 1, groups]
                    if q % 2 == 0:
                        wait(pool, p_taken, at(t, 2, q // 2 - 1))
                    pool.tensor_tensor(diff, st[:, groups, 1], st[:, groups, 4], ALU.subtract)
                    tstep(pool.tensor_tensor(sq, st[:, groups, 2], st[:, groups, 5], ALU.add))
                    pool.tensor_tensor(sq, sq, c_eps[:, :], ALU.add)
                    tstep(pool.tensor_tensor(diff, diff, diff, ALU.mult))
                    tstep(pool.tensor_tensor(diff, diff, quarter_c[:, :], ALU.mult))
                    tstep(pool.tensor_tensor(sq, sq, diff, ALU.add))
                    root(RS[:, groups], sq, pix_rstd)

                def spread(t, q):
                    if q % 2 == 0:
                        wait(pool, p_taken, at(t, 2, q // 2 + 1))
                        wait(pool, z_made, at(t, 2 * QUARTERS, 2 * (q + 2) - 2 * QUARTERS))
                    g = slice(q * GPQ, (q + 1) * GPQ)
                    pool.tensor_tensor(A[:, g, :, :], PR[:, g, :].unsqueeze(2).to_broadcast([P, GPQ, LPG, HEADS]),
                                       pixmask[:, :].rearrange("p (l h) -> p l h", h=HEADS).unsqueeze(1).to_broadcast(
                                           [P, GPQ, LPG, HEADS]), ALU.mult).then_inc(p_spread, 1)

                def mask_q(a):
                    wait(pool, aq_taken, at(a, CH, CH))
                    wait(pool, as_made, at(a, HEADS, 0))
                    for h in range(HEADS):
                        pool.tensor_tensor(QM[:, h, :], AQ[:, h // HPC, :], headmask[:, h % HPC:h % HPC + 1].to_broadcast([P, LOC]),
                                           ALU.mult).then_inc(qm_ready, 1)

                def h0_parts(t):
                    wait(pool, h0_var, at(t, 1, 1))
                    wait(pool, n_ready, at(t, 1, 0))
                    root(arstd[:, :], amv[:, :, 1], h0_rstd)
                    wait(pool, h1_ready, at(t, 1, 0))
                    for l in range(LH):
                        tstep(pool.tensor_tensor(H2[:, l, :], H0[:, l, :], H0[:, l, :], ALU.add))
                    for l in range(LH):
                        ins = pool.tensor_tensor(H2[:, l, :], H2[:, l, :], bf_row[:, :], ALU.add)
                        if l < LH - 1:
                            tstep(ins)
                    ins.then_inc(h0_twice, 1)

                def u_root(a):
                    wait(pool, u_var, at(a, 1, 1))
                    wait(pool, h1_ready, at(a, 1, 0))
                    root(brstd[:, :], bmv[:, :, 1], u_rstd)

                def image(t, a, more=True):
                    T, B = t is not None, a is not None
                    if B: mask_q(a)
                    if T:
                        tstep.start(t)
                        feats_bias(t)
                        for q in range(QUARTERS):
                            pixel_rstd(t, q)
                        spread(t, 0)
                        spread(t, 1)
                        spread(t, 2)
                        spread(t, 3)
                        if more: feats_rstd(t + 1)
                    if B: u_root(a)
                    if T:
                        h0_parts(t)
                        tstep.finish()

                feats_rstd(0)
                image(0, None)
                image(1, 0)
                with pool.Fori(2, NB - 1) as t:
                    image(t, t - 1)
                image(NB - 1, NB - 2, more=False)
                image(None, NB - 1)

        TOK = 512
        TT = TOK // P
        CHUNKS = NB * LOC // TOK
        E6 = EXPERTS
        E_L = E6 * CH
        w_loads, expert_loaded = sem("ffn_biases_loaded"), [sem(f"expert{e}_loaded") for e in range(E6)]
        tok_loaded, out_stored = [sem(f"tok_loaded{i}") for i in range(2)], sem("out_stored")
        m_turned, m_taken = sem("m_turned"), sem("m_taken")
        rh_made, rh_taken, logits_made = sem("rh_made"), sem("rh_taken"), sem("logits_made")
        rt_shifted, rt_exped = sem("router_shifted"), sem("router_exped")
        wt_ready, wt_turned, wt_taken, b3_made = sem("route_ready"), sem("route_turned"), sem("route_taken"), sem("b3_made")
        l1_made, l1_taken, l2_made, l2_taken = sem("l1_made"), sem("l1_taken"), sem("l2_made"), sem("l2_taken")
        l3_made, l3_taken = sem("l3_made"), sem("l3_taken")
        f_var, f_rstd, f_ready = sem("f_var"), sem("f_rstd"), sem("f_ready")
        route_chain, weigh_chain, norm_chain = sem("route_steps"), sem("weigh_steps"), sem("norm_steps")

        with ExitStack() as two:
            W1, W2, W3 = (sb(two, f"expert_w{n}", E6, CH, C) for n in (1, 2, 3))
            B1, B2 = sb(two, "expert_b1", E6, CH), sb(two, "expert_b2", E6, CH)
            B3 = two.enter_context(nc.sbuf_tensor("expert_b3", [E6, C], F32))
            RW1, RW2 = sb(two, "router_w1", CH, P), sb(two, "router_w2", E6)
            RB1, RB2 = sb(two, "router_b1", 1), sb(two, "router_b2", E6)
            before = sb(two, "expert_before", E6, E6)
            HTOK = sb(two, "tokens", 2, TT, C)
            HC = sb(two, "tokens_turned", 2, CH, TOK)
            RH = sb(two, "router_hidden", TOK)
            LG, PB_, EL = sb(two, "logits", TT, E6), sb(two, "probs", TT, E6), sb(two, "router_exp", TT, E6)
            PX = sb(two, "weights_top2", 2, TT, E6)
            l_mx, l_den = sb(two, "logit_max", TT), sb(two, "weight_sum", TT)
            gt, eq, rank = sb(two, "larger", TT, E6, E6), sb(two, "equal_before", TT, E6, E6), sb(two, "rank", TT, E6)
            WTT = two.enter_context(nc.sbuf_tensor("weights_turned", [E6, TT, P], F32))
            A1, A2 = sb(two, "hidden1", CH, TOK), sb(two, "hidden2", CH, TOK)
            ACC = sb(two, "combined", TT, C)
            fst, fmv, frstd = sb(two, "bn_ffn", TT, 8), sb(two, "mean_var_ffn", TT, 2), sb(two, "rstd_ffn", TT)
            OUT = sb(two, "out_tokens", TT, C)

            tok_view = h1_dram.rearrange("(i k p) c -> i p k c", k=TT, p=P)
            out_view = out.rearrange("b l c -> (b l) c").rearrange("(i k p) c -> i p k c", k=TT, p=P)
            WLOADS = 10
            PAIRS2 = CHUNKS // 2
            assert PAIRS2 >= 2

            block = two.enter_context(nc.Block())

            @block.sync
            def _(sp):
                def load_tokens(i, slot):
                    wait(sp, f_var, at(i, 1, -1))
                    sp.dma_start(HTOK[:, slot, :, :], tok_view[i]).then_inc(tok_loaded[slot], 16)

                sp.wait_ge(h1_stored, 16 * NB)
                load_tokens(0, 0)
                sp.dma_start(RW1[:, :, :], rw1.rearrange("(c p) n -> p c n", p=P)).then_inc(w_loads, 16)
                sp.dma_start(RW2[:, :], rw2).then_inc(w_loads, 16)
                with nc.allow_non_contiguous_dma(reason="biases, once"):
                    for dst, src in ((B1[:, :, 0], eb1[:, 0:P].rearrange("e p -> p e")), (B1[:, :, 1], eb1[:, P:C].rearrange("e p -> p e")),
                                     (B2[:, :, 0], eb2[:, 0:P].rearrange("e p -> p e")), (B2[:, :, 1], eb2[:, P:C].rearrange("e p -> p e")),
                                     (RB1[:, :], rb1.rearrange("(p o) -> p o", o=1))):
                        sp.dma_start(dst, src, allow_slow_non_contiguous=True).then_inc(w_loads, 16)
                sp.dma_start(RB2[:, :], rb2.partition_broadcast(P)).then_inc(w_loads, 16)
                sp.dma_start(B3[:, :], eb3).then_inc(w_loads, 16)
                sp.dma_start(before[:, :, :], masks_in[:, SH + HPC:SH + HPC + E6 * E6].rearrange(
                    "p (a b) -> p a b", a=E6)).then_inc(w_loads, 16)

                for e in range(E6):
                    for W, w in ((W1, ew1), (W2, ew2), (W3, ew3)):
                        sp.dma_start(W[:, e, :, :], w[e].rearrange("(c p) n -> p c n", p=P)).then_inc(expert_loaded[e], 16)
                load_tokens(1, 1)

                def store(i):
                    wait(sp, f_ready, at(i, 1, 1))
                    sp.dma_start(out_view[i], OUT[:, :, :]).then_inc(out_stored, 16)

                with sp.Fori(1, CHUNKS // 2) as j:
                    for k in range(2):
                        load_tokens(2 * j + k, k)
                        store(2 * j + k - 2)
                store(CHUNKS - 2)
                store(CHUNKS - 1)
                sp.wait_ge(out_stored, 16 * CHUNKS)

            @block.tensor
            def _(pe):
                mm = pe.matmul
                pe.wait_ge(w_loads, 16 * WLOADS)

                def turn_tokens(i, half, slot, c):
                    if c == 0:
                        pe.wait_ge(tok_loaded[slot], at(half, 16, 16))
                    wait(pe, m_taken, at(i, CH, c))
                    for k in range(TT):
                        last = pe.transpose(banks[6][:, k * P:(k + 1) * P], HTOK[:, slot, k, c * P:(c + 1) * P], ident[:, :])
                    last.then_inc(m_turned, 1)

                def router(i, slot):
                    pe.wait_ge(m_taken, at(i, CH, CH))
                    wait(pe, wt_taken, at(i, 1, 0))
                    for c in range(CH):
                        last = mm(banks[7][:, :], RW1[:, c, :], HC[:, slot, c, :], start=(c == 0), stop=(c == CH - 1))
                    last.then_inc(rh_made, 1)

                def logits(i):
                    pe.wait_ge(rh_taken, at(i, 1, 1))
                    for k in range(TT):
                        last = mm(banks[7][:, k * E6:(k + 1) * E6], RH[:, k * P:(k + 1) * P], RW2[:, :], start=True, stop=True)
                    last.then_inc(logits_made, 1)

                def turn_route(i, slot):
                    pe.wait_ge(wt_ready, at(i, 1, 1))
                    for k in range(TT):
                        last = pe.transpose(banks[7][0:E6, k * P:(k + 1) * P], PX[:, slot, k, :], ident[:, :])
                    last.then_inc(wt_turned, 1)

                def open_sum(i):
                    pe.wait_ge(wt_taken, at(i, 1, 1))
                    wait(pe, l3_taken, at(i, E6 + 1, 0))
                    for k in range(TT):
                        last = mm(halved(4 + k // 2)[:, k % 2, :], WTT[:, k, :], B3[:, :], start=True, stop=True)
                    last.then_inc(b3_made, 1)

                def hidden(W, e, src, first_bank, made):
                    for m in range(CH):
                        for c in range(CH):
                            last = mm(banks[first_bank + m][:, :], W[:, e, c, m * P:(m + 1) * P], src[:, c, :],
                                      start=(c == 0), stop=(c == CH - 1))
                        last.then_inc(made, 1)

                def layer1(i, e, slot):
                    wait(pe, l1_taken, at(i, E_L, e * CH))
                    hidden(W1, e, HC[:, slot, :, :], 0, l1_made)

                def layer2(i, e):
                    pe.wait_ge(l1_taken, at(i, E_L, (e + 1) * CH))
                    wait(pe, l2_taken, at(i, E_L, e * CH))
                    hidden(W2, e, A1, 2, l2_made)

                def layer3(i, e):
                    pe.wait_ge(l2_taken, at(i, E_L, (e + 1) * CH))
                    pe.wait_ge(l3_taken, at(i, E6 + 1, e + 1))
                    for k in range(TT):
                        for c in range(CH):
                            last = mm(halved(4 + k // 2)[:, k % 2, :], A2[:, c, k * P:(k + 1) * P], W3[:, e, c, :],
                                      start=(c == 0), stop=(c == CH - 1))
                    last.then_inc(l3_made, 1)

                def chunk(i, half, slot, first=False, final=False):
                    for e in range(E6):
                        if first:
                            pe.wait_ge(expert_loaded[e], 16 * 3)
                        layer1(i, e, slot)
                        if not final:
                            if e == 4: turn_tokens(i + 1, half + slot, 1 - slot, 0)
                            if e == 5: logits(i + 1)
                        if e == 2: open_sum(i)
                        if e >= 1:
                            layer2(i, e - 1)
                        elif not first:
                            layer2(i - 1, E6 - 1)
                        if e == 1: turn_route(i, slot)
                        if e == 4 and not final: turn_tokens(i + 1, half + slot, 1 - slot, 1)
                        if e >= 2:
                            layer3(i, e - 2)
                        elif not first:
                            layer3(i - 1, e + E6 - 2)
                        if e == 4 and not final: router(i + 1, 1 - slot)
                    if final:
                        layer3(i, E6 - 2)
                        layer2(i, E6 - 1)
                        layer3(i, E6 - 1)

                for c in range(CH):
                    turn_tokens(0, 0, 0, c)
                router(0, 0)
                logits(0)
                chunk(0, 0, 0, first=True)
                chunk(1, 0, 1)
                if PAIRS2 > 2:
                    with pe.Fori(1, PAIRS2 - 1) as j:
                        for k in range(2):
                            chunk(2 * j + k, j, k)
                chunk(CHUNKS - 2, PAIRS2 - 1, 0)
                chunk(CHUNKS - 1, PAIRS2 - 1, 1, final=True)

            @block.scalar
            def _(act):
                act.wait_ge(w_loads, 16 * WLOADS)

                def exp(i, n):
                    act.wait_ge(rt_shifted, at(i, 2, n))
                    act.activation(EL[:, :, :], EL[:, :, :], ACT.Exp).then_inc(rt_exped, 1)

                def route(i, slot):
                    for c in range(CH):
                        act.wait_ge(m_turned, at(i, CH, c + 1))
                        act.activation(HC[:, slot, c, :], banks[6][:, :], ACT.Copy).then_inc(m_taken, 1)
                    act.wait_ge(rh_made, at(i, 1, 1))
                    wait(act, logits_made, at(i, 1, 0))
                    act.activation(RH[:, :], banks[7][:, :], ACT.Relu, bias=RB1[:, 0:1]).then_inc(rh_taken, 1)

                def chunk(i, slot, final=False):
                    for e in range(E6):
                        for m in range(CH):
                            act.wait_ge(l1_made, at(i, E_L, e * CH + m + 1))
                            if m == 0:
                                wait(act, l2_made, at(i, E_L, e * CH))
                            act.activation(A1[:, m, :], banks[m][:, :], ACT.Relu, bias=B1[:, e, m:m + 1]).then_inc(l1_taken, 1)
                        if e == 0: exp(i, 2)
                        if e == 4 and not final: route(i + 1, 1 - slot)
                        if e == 5 and not final: exp(i + 1, 1)

                route(0, 0)
                exp(0, 1)
                chunk(0, 0)
                chunk(1, 1)
                if PAIRS2 > 2:
                    with act.Fori(1, PAIRS2 - 1) as j:
                        for k in range(2):
                            chunk(2 * j + k, k)
                chunk(CHUNKS - 2, 0)
                chunk(CHUNKS - 1, 1, final=True)

            @block.vector
            def _(dve):
                rstep, wstep, nstep = Steps(dve, route_chain, 11), Steps(dve, weigh_chain, 4), Steps(dve, norm_chain, 4)
                dve.wait_ge(w_loads, 16 * WLOADS)

                def six(ap):
                    return ap.unsqueeze(2).to_broadcast([P, TT, E6])

                def softmax_logits(i):
                    rstep.start(i)
                    dve.wait_ge(logits_made, at(i, 1, 1))
                    rstep(dve.tensor_tensor(LG[:, :, :], banks[7][:, 0:TT * E6].rearrange("p (k e) -> p k e", e=E6),
                                           RB2[:, :].unsqueeze(1).to_broadcast([P, TT, E6]), ALU.add))
                    rstep(dve.tensor_reduce(l_mx[:, :], LG[:, :, :], AX.X, ALU.max))
                    dve.tensor_tensor(EL[:, :, :], LG[:, :, :], six(l_mx[:, :]), ALU.subtract).then_inc(rt_shifted, 1)
                    dve.wait_ge(rt_exped, at(i, 2, 1))
                    rstep(dve.tensor_reduce(l_den[:, :], EL[:, :, :], AX.X, ALU.add))
                    rstep(dve.reciprocal(l_den[:, :], l_den[:, :]))
                    rstep(dve.tensor_tensor(PB_[:, :, :], EL[:, :, :], six(l_den[:, :]), ALU.mult))

                def choose(i):
                    mine = PB_[:, :, :].unsqueeze(3).to_broadcast([P, TT, E6, E6])
                    other = PB_[:, :, :].unsqueeze(2).to_broadcast([P, TT, E6, E6])
                    first = before[:, :, :].unsqueeze(1).to_broadcast([P, TT, E6, E6])
                    rstep(dve.tensor_tensor(gt[:, :, :, :], other, mine, ALU.is_gt))
                    rstep(dve.tensor_tensor(eq[:, :, :, :], other, mine, ALU.is_equal))
                    rstep(dve.tensor_tensor(eq[:, :, :, :], eq[:, :, :, :], first, ALU.mult))
                    rstep(dve.tensor_tensor(gt[:, :, :, :], gt[:, :, :, :], eq[:, :, :, :], ALU.add))
                    rstep(dve.tensor_reduce(rank[:, :, :], gt[:, :, :, :], AX.X, ALU.add))
                    rstep(dve.tensor_reduce(l_mx[:, :], PB_[:, :, :], AX.X, ALU.max))
                    dve.tensor_tensor(EL[:, :, :], PB_[:, :, :], six(l_mx[:, :]), ALU.subtract).then_inc(rt_shifted, 1)
                    rstep.finish()

                def weigh(i, slot):
                    wstep.start(i)
                    dve.wait_ge(rt_exped, at(i, 2, 2))
                    wstep(dve.tensor_scalar(rank[:, :, :], rank[:, :, :], 1.5, None, ALU.is_lt))
                    wstep(dve.tensor_tensor(EL[:, :, :], EL[:, :, :], rank[:, :, :], ALU.mult))
                    wstep(dve.tensor_reduce(l_den[:, :], EL[:, :, :], AX.X, ALU.add))
                    wstep(dve.reciprocal(l_den[:, :], l_den[:, :]))
                    dve.tensor_tensor(PX[:, slot, :, :], EL[:, :, :], six(l_den[:, :]), ALU.mult).then_inc(wt_ready, 1)
                    wstep.finish()

                def take_l2(i, e):
                    for m in range(CH):
                        dve.wait_ge(l2_made, at(i, E6 * CH, e * CH + m + 1))
                        if m == 0:
                            wait(dve, l3_made, at(i, E6, e))
                        dve.tensor_scalar(A2[:, m, :], banks[2 + m][:, :], B2[:, e, m:m + 1], 0.0,
                                          ALU.add, ALU.max).then_inc(l2_taken, 1)

                def take_route(i):
                    dve.wait_ge(wt_turned, at(i, 1, 1))
                    dve.tensor_copy(WTT[:, :, :], banks[7][0:E6, :].rearrange("e (k p) -> e k p", p=P)).then_inc(wt_taken, 1)

                def take_b3(i, slot):
                    dve.wait_ge(b3_made, at(i, 1, 1))
                    wait(dve, f_ready, at(i, 1, 0))
                    for b in range(TT // 2):
                        last = dve.tensor_tensor(ACC[:, 2 * b:2 * b + 2, :], halved(4 + b), HTOK[:, slot, 2 * b:2 * b + 2, :], ALU.add)
                    last.then_inc(l3_taken, 1)

                def take_l3(i, e, slot):
                    dve.wait_ge(l3_made, at(i, E6, e + 1))
                    dve.wait_ge(l3_taken, at(i, E6 + 1, e + 1))
                    for k in range(TT):
                        last = dve.scalar_tensor_tensor(ACC[:, k, :], halved(4 + k // 2)[:, k % 2, :], PX[:, slot, k, e:e + 1],
                                                        ACC[:, k, :], ALU.mult, ALU.add)
                    last.then_inc(l3_taken, 1)

                def norm(i):
                    nstep.start(i)
                    dve.wait_ge(l3_taken, at(i, E6 + 1, E6 + 1))
                    layer_stats(dve, ACC, TT, fst, fmv, nstep, f_var)
                    nstep.finish()
                    dve.wait_ge(f_rstd, at(i, 1, 1))
                    wait(dve, out_stored, at(i, 16, 0))
                    for k in range(TT):
                        last = dve.tensor_scalar(OUT[:, k, :], ACC[:, k, :], fmv[:, k, 0:1], frstd[:, k:k + 1],
                                                 ALU.subtract, ALU.mult)
                    last.then_inc(f_ready, 1)

                def chunk(i, slot, first=False, final=False):
                    for e in range(E6):
                        if e == 1: take_route(i)
                        if e == 2: take_b3(i, slot)
                        if e >= 1:
                            take_l2(i, e - 1)
                        elif not first:
                            take_l2(i - 1, E6 - 1)
                        if e >= 2:
                            take_l3(i, e - 2, slot)
                        elif not first:
                            take_l3(i - 1, e + E6 - 2, 1 - slot)
                        if e == 0: weigh(i, slot)
                        if e == 1 and not first: norm(i - 1)
                    if not final:
                        softmax_logits(i + 1)
                        choose(i + 1)
                    else:
                        take_l3(i, E6 - 2, slot)
                        take_l2(i, E6 - 1)
                        take_l3(i, E6 - 1, slot)
                        norm(i)

                softmax_logits(0)
                choose(0)
                chunk(0, 0, first=True)
                chunk(1, 1)
                if PAIRS2 > 2:
                    with dve.Fori(1, PAIRS2 - 1) as j:
                        for k in range(2):
                            chunk(2 * j + k, k)
                chunk(CHUNKS - 2, 0)
                chunk(CHUNKS - 1, 1, final=True)

            @block.gpsimd
            def _(pool):
                def chunk(i):
                    pool.wait_ge(f_var, at(i, 1, 1))
                    wait(pool, f_ready, at(i, 1, 0))
                    pool.tensor_tensor(frstd[:, :], fmv[:, :, 1], halves[:, 0:TT], ALU.pow).then_inc(f_rstd, 1)

                chunk(0)
                with pool.Fori(1, CHUNKS) as i:
                    chunk(i)


def kernel(**inputs):
    import numpy as np
    import concourse.bacc as bacc
    from concourse.bass_utils import run_bass_kernel_spmd

    arrays, aps = prepare(inputs, np, bacc)
    nc = aps.pop("nc")
    build(nc, **aps)
    r = run_bass_kernel_spmd(nc, [arrays], core_ids=[0])
    return r.results[0]["out_dram"]


def prepare(inputs, np, bacc):
    def t(name):
        return np.ascontiguousarray(np.asarray(inputs[name]).T)

    def a(name):
        return np.ascontiguousarray(inputs[name])

    x = a("x")
    n, c, h, w = x.shape
    x = np.ascontiguousarray(x.reshape(n, c, h // STRIDE, STRIDE, w // STRIDE, STRIDE).transpose(0, 1, 2, 4, 3, 5)).reshape(
        n, c, -1, STRIDE ** 2)
    p = np.arange(P)
    sh = (np.arange(64) // HEADS)[None, :] == (p // STRIDE ** 2)[:, None]
    hm = np.arange(4)[None, :] == (p // 32)[:, None]
    before = np.broadcast_to((np.arange(EXPERTS)[None, :] < np.arange(EXPERTS)[:, None]).ravel(), (P, EXPERTS ** 2))
    data = {
        "x": x, "wq_t": t("L0_tok_Wq"), "wkv": a("L0_tok_Wkv"), "proj_t": t("L0_tok_proj_w"),
        "wqkv_t": t("L0_attn_W_qkv"), "wgate_t": t("L0_attn_W_gate"), "wfinal_t": t("L0_attn_W_final"),
        "vecs": np.stack([a(n) for n in VECS]), "ident_in": np.eye(P, dtype=np.float32),
        "masks_in": np.concatenate([sh, hm, before], axis=1).astype(np.float32),
        "rw1": a("L0_ffn_router_w1"), "rb1": a("L0_ffn_router_b1"), "rw2": a("L0_ffn_router_w2"), "rb2": a("L0_ffn_router_b2"),
        "ew1": a("L0_ffn_expert_w1"), "eb1": a("L0_ffn_expert_b1"), "ew2": a("L0_ffn_expert_w2"), "eb2": a("L0_ffn_expert_b2"),
        "ew3": a("L0_ffn_expert_w3"), "eb3": a("L0_ffn_expert_b3"),
    }
    nc = bacc.Bacc("TRN2", target_bir_lowering=False, num_devices=1)
    arrays, aps = {}, {"nc": nc}
    for name, value in data.items():
        arrays[f"in_{name}"] = value
        aps[name] = nc.dram_tensor(f"in_{name}", value.shape, mybir.dt.from_np(value.dtype), kind="ExternalInput").ap()
    aps["out"] = nc.dram_tensor("out_dram", (n, (h // STRIDE) ** 2, c), F32, kind="ExternalOutput").ap()
    return arrays, aps
```

```python
from contextlib import ExitStack

import concourse.bass as bass
from concourse import mybir

F32 = mybir.dt.float32
F32R = mybir.dt.float32r
ALU = mybir.AluOpType
ACT = mybir.ActivationFunctionType
AX = mybir.AxisListType

P = 128
STRIDE = 4
HEADS = 8
EPS = 1e-5
EXPERTS = 6
VECS = ["L0_tok_ln_q_w", "L0_tok_ln_q_b", "L0_tok_ln_kv_w", "L0_tok_ln_kv_b", "L0_tok_proj_b",
        "L0_attn_ln_gamma", "L0_attn_ln_beta", "L0_attn_b_gate", "L0_attn_b_final"]
QW, QB, KVW, KVB, PB, GAMMA, BETA, BGATE, BFINAL = range(len(VECS))


def build(nc, x, wq_t, wkv, proj_t, wqkv_t, wgate_t, wfinal_t, vecs, ident_in, masks_in,
          sel_in,
          rw1, rb1, rw2, rb2, ew1, eb1, ew2, eb2, ew3, eb3, out):
    NB, C, LOC, N2 = x.shape
    CH = C // P
    PIX = LOC * N2
    LH = LOC // P
    D = C // HEADS
    HPC = P // D
    GROUPS = PIX // P
    LPG = LOC // GROUPS
    QUARTERS = 4
    GPQ = GROUPS // QUARTERS
    PAIRS = GROUPS // 2
    GPH = GROUPS // 2
    LPQ = LOC // QUARTERS
    SH = LPG * HEADS
    assert C == 256 and LOC == 256 and GROUPS == 32 and SH == 64 and NB >= 3

    h1_dram = nc.dram_tensor("h1_scratch", (NB * LOC, C), F32, kind="Internal").ap()

    def at(index, per, n):
        return index * per + n

    def wait(eng, sem, value):
        if not (isinstance(value, int) and value <= 0):
            eng.wait_ge(sem, value)

    class Steps:
        def __init__(self, eng, signal, per):
            self.eng, self.counted, self.per = eng, signal, per

        def start(self, index):
            self.index, self.n = index, 0

        def __call__(self, ins):
            self.n += 1
            ins.then_inc(self.counted, 1)
            self.eng.wait_ge(self.counted, at(self.index, self.per, self.n))

        def finish(self):
            assert self.n == self.per, self.n

    def layer_stats(dve, src, n, tmp, mean_var, step, signal):
        for l in range(n):
            last = dve.bn_stats(tmp[:, l, 0:6], src[:, l, :])
        step(last)
        diff, squares = tmp[:, 0:n, 6], tmp[:, 0:n, 7]
        dve.tensor_tensor(squares, tmp[:, 0:n, 2], tmp[:, 0:n, 5], ALU.add)
        step(dve.tensor_tensor(diff, tmp[:, 0:n, 1], tmp[:, 0:n, 4], ALU.subtract))
        dve.scalar_tensor_tensor(mean_var[:, :, 0], diff, 0.5, tmp[:, 0:n, 4], ALU.mult, ALU.add)
        step(dve.scalar_tensor_tensor(mean_var[:, :, 1], diff, C / 4.0, diff, ALU.mult, ALU.mult))
        step(dve.tensor_tensor(squares, squares, mean_var[:, :, 1], ALU.add))
        dve.tensor_scalar(mean_var[:, :, 1], squares, 1.0 / C, EPS, ALU.mult, ALU.add).then_inc(signal, 1)

    with ExitStack() as whole:
        def sem(name):
            return whole.enter_context(nc.semaphore(name))

        setup_loads = sem("setup_loads")
        x_loaded = [sem(f"x_loaded{q}") for q in range(QUARTERS)]
        h1_stored = sem("h1_stored")
        su_v, su_p = sem("setup_vector"), sem("setup_tensor")
        setup_done = sem("setup_done")
        feats_summed = sem("feats_summed")
        r_turned, r_taken, r_var, r_rstd = sem("r_turned"), sem("r_taken"), sem("r_var"), sem("r_rstd")
        rb_ready = sem("rb_ready")
        qn_ready, qn_turned, qn_taken = sem("qn_ready"), sem("qn_turned"), sem("qn_taken")
        q_made, q_taken, q_high, q_split = sem("q_made"), sem("q_taken"), sem("q_high"), sem("q_split")
        qs_made, qs_taken_act, qs_taken_dve = sem("q_stack_made"), sem("q_stack_taken_act"), sem("q_stack_taken_dve")
        g_made, g_taken_act, g_taken_dve = sem("g_made"), sem("g_taken_act"), sem("g_taken_dve")
        xt_made, xt_taken, stats_done = sem("xt_made"), sem("xt_taken"), sem("stats_done")
        s_made, s_taken = sem("s_made"), sem("s_taken")
        pix_rstd = sem("pix_rstd")
        e_ready, e_turned, e_shifted, e_exped = sem("e_ready"), sem("e_turned"), sem("e_shifted"), sem("e_exped")
        p_ready, p_turned, p_taken, p_spread = sem("p_ready"), sem("p_turned"), sem("p_taken"), sem("p_spread")
        z_made, z_taken = sem("z_made"), sem("z_taken")
        agg_made, agg_taken = sem("agg_made"), sem("agg_taken")
        proj_made, h0_ready = sem("proj_made"), sem("h0_ready")
        t_chain, r_chain = sem("tokenizer_vector_steps"), sem("feats_vector_steps")
        h0_var, h0_rstd, h0_twice = sem("h0_var"), sem("h0_rstd"), sem("h0_twice")
        pool_t_chain = sem("tokenizer_pool_steps")
        h_turned, h_taken = sem("h_turned"), sem("h_taken")
        n_ready, n_turned, n_taken = sem("n_ready"), sem("n_turned"), sem("n_taken")
        aq_made, aq_taken, qm_ready = sem("aq_made"), sem("aq_taken"), sem("q_masked_ready")
        ak_made, ak_taken = sem("ak_made"), sem("ak_taken")
        av_made, av_taken = sem("av_made"), sem("av_taken")
        gate_made, gate_taken = sem("gate_made"), sem("gate_taken")
        as_made, as_max, as_exped = sem("as_made"), sem("as_max"), sem("as_exped")
        vs_ready = sem("vs_ready")
        ao_made, ao_taken = sem("ao_made"), sem("ao_taken")
        fin_made, u_var, u_rstd, h1_ready = sem("fin_made"), sem("u_var"), sem("u_rstd"), sem("h1_ready")
        a_chain = sem("attention_vector_steps")

        banks = [whole.enter_context(nc.psum_tensor(f"bank{i}", [P, 512], F32)) for i in range(8)]

        def sb(stack, name, *shape, dtype=F32):
            return stack.enter_context(nc.sbuf_tensor(name, [P, *shape], dtype))

        ident = sb(whole, "ident", P)
        halves = sb(whole, "minus_half", 8)

        def halved(bank):
            return banks[bank][:, :].rearrange("p (a b) -> p a b", a=2)

        with ExitStack() as one:
            X = sb(one, "x_image", CH, PIX)
            XT = sb(one, "x_turned", GROUPS, C)
            GZ = sb(one, "score_weights_or_pooled", CH, LOC * HEADS)
            G = GZ[:, :, :].rearrange("p c (l h) -> p c l h", h=HEADS)
            A = sb(one, "attn_spread", GROUPS, LPG, HEADS)
            Z = GZ[:, :, :].rearrange("p c (h l) -> p c h l", h=HEADS)
            WQ, WKs, WVm = sb(one, "wq", CH, C), sb(one, "wk_stacked", HEADS, C, dtype=F32R), sb(one, "wv_masked", CH, HEADS, P)
            PW, WA = sb(one, "w_proj", CH, C), sb(one, "w_qkv", CH, 3 * C)
            WG, WF = sb(one, "w_gate", CH, C), sb(one, "w_final", CH, C)
            pixmask = sb(one, "pixel_token_mask", SH)
            headmask = sb(one, "head_mask", HPC)
            vcol = sb(one, "vectors_cols", len(VECS), CH)
            pb_row, vb_row, bf_row = sb(one, "proj_b_row", C), sb(one, "v_bias_row", C), sb(one, "b_final_row", C)
            bq_col, aq_bias, bk_col, gb_half = sb(one, "bq_col", CH), sb(one, "aq_bias", CH), sb(one, "bk_col", CH), sb(one, "gate_b_halved", CH)
            c_eps, quarter_c = sb(one, "eps_times_c", GPQ), sb(one, "quarter_of_c", GPQ)
            R = sb(one, "feats", CH, LOC)
            RT, RTB = sb(one, "feats_turned", LH, C), sb(one, "feats_plus_bias", LH, C)
            QS, SEL = sb(one, "q_stacked", HEADS, LOC, dtype=F32R), sb(one, "stack_rows", HPC, 2, P, dtype=F32R)
            QH, QL = sb(one, "q_high", CH, LOC, dtype=F32R), sb(one, "q_low", CH, LOC, dtype=F32R)
            QNT, QN, Q = sb(one, "qn_tokens", LH, C), sb(one, "qn", CH, LOC), sb(one, "q", CH, LOC)
            bnt, mv, rstd2 = sb(one, "bn_tmp", LH, 8), sb(one, "mean_var", LH, 2), sb(one, "rstd2", LH)
            st, vt, RS = sb(one, "bn_pixels", GROUPS, 6), sb(one, "var_pixels", 2, GROUPS), sb(one, "rstd_pixels", GROUPS)
            SM, E = sb(one, "scores_masked", GPQ, SH), sb(one, "scores", GROUPS, HEADS)
            mx, den = sb(one, "softmax_max", 2, LPG), sb(one, "softmax_sum", 2, LPG)
            PE_, PR = sb(one, "softmax_exp", 2, LPG, N2), sb(one, "attn_scaled", GROUPS, HEADS)
            AG = sb(one, "aggregated", CH, LOC)
            H0, H2 = sb(one, "h0", LH, C), sb(one, "h0_twice_b", LH, C)
            amv, arstd = sb(one, "mean_var_attn", LH, 2), sb(one, "rstd_attn", LH)
            NT, HT = sb(one, "normed_turned", CH, LOC), sb(one, "h0_turned", CH, LOC)
            QM, K = sb(one, "q_masked", HEADS, LOC), sb(one, "k", CH, LOC)
            V, VS = sb(one, "v", LH, HEADS, D), sb(one, "v_scaled_masked", LH, HEADS, P)
            GT = sb(one, "gate", CH, LOC)
            EX = sb(one, "attn_exp", HEADS, LH, LOC)
            nmax, esum = sb(one, "minus_max", HEADS, LH), sb(one, "exp_sum", HEADS, LH)
            O, U = GT, H2
            AQ = AG
            NH = QNT
            H1 = sb(one, "h1", LH, C)
            bmv, brstd = sb(one, "mean_var_out", LH, 2), sb(one, "rstd_out", LH)

            def stage(start, width, chunks=CH):
                return XT[:, :, :].rearrange("p a b -> p (a b)")[:, start:start + chunks * width].rearrange(
                    "p (c w) -> p c w", c=chunks)

            raw_wq, raw_wk, raw_wv = stage(0, C), stage(512, C), stage(1024, C)
            raw_wqkv = stage(1536, 3 * C)
            row_w, row_b = stage(3072, C, 1)[:, 0, :], stage(3328, C, 1)[:, 0, :]
            beta_wide, bv_wide = stage(3584, P), stage(3840, P)
            wtmp = stage(4096, C)
            wmean = stage(4608, 1)
            bv_col = stage(4612, 1)
            ones = stage(4736, P, 1)[:, 0, :]
            pb_raw = stage(4864, C, 1)[:, 0, :]
            sel_q, sel_k = (stage(5120 + n * HPC * 2 * P, 2 * P, HPC).rearrange("p h (s m) -> p h s m", s=2) for n in range(2))
            wk_high, wk_low = stage(7168, C), stage(7680, C)

            x_img = x.rearrange("b (c p) l n -> b p c (l n)", p=P)
            h1_img = h1_dram.rearrange("(b h p) c -> b p h c", h=LH, p=P)
            QP = PIX // QUARTERS

            def halves_of(w):
                return w.rearrange("(c p) n -> p c n", p=P)

            def wk_stack_psum(h):
                return halved(5 + h // 2)[:, h % 2, :] if h < 6 else halved(h - 4)[:, 1, :]

            SCORE_SLOTS = (3, 4, 5, 6, 7, 9, 10, 12)

            G_DVE = (5, 7)
            G_BANKS = (0, 1, 6)

            block = one.enter_context(nc.Block())

            @block.sync
            def _(sp):
                def load_quarter(t, q):
                    wait(sp, s_made, at(t, QUARTERS, q + 1 - QUARTERS))
                    wait(sp, feats_summed, at(t, QUARTERS, q + 1 - QUARTERS))
                    sp.dma_start(X[:, :, q * QP:(q + 1) * QP],
                                 x_img[t, :, :, q * QP:(q + 1) * QP]).then_inc(x_loaded[q], 16)

                def store_h1(a):
                    wait(sp, h1_ready, at(a, 1, 1))
                    sp.dma_start(h1_img[a], H1[:, :, :]).then_inc(h1_stored, 16)

                setup = [
                    (raw_wq, halves_of(wq_t)), (raw_wk, halves_of(wkv[0:C, :])), (raw_wv, halves_of(wkv[C:2 * C, :])),
                    (raw_wqkv, halves_of(wqkv_t)), (PW[:, :, :], halves_of(proj_t)), (WG[:, :, :], halves_of(wgate_t)),
                    (WF[:, :, :], halves_of(wfinal_t)), (ident[:, :], ident_in),
                    (sel_q, sel_in[:, 0]), (sel_k, sel_in[:, 1]),
                    (pixmask[:, :], masks_in[:, 0:SH]), (headmask[:, :], masks_in[:, SH:SH + HPC]),
                    (row_w, vecs[KVW, :].partition_broadcast(P)), (row_b, vecs[KVB, :].partition_broadcast(P)),
                    (pb_raw, vecs[PB, :].partition_broadcast(P)), (bf_row[:, :], vecs[BFINAL, :].partition_broadcast(P)),
                ]
                for dst, src in setup:
                    sp.dma_start(dst, src).then_inc(setup_loads, 16)
                with nc.allow_non_contiguous_dma(reason="a few hundred values, once"):
                    for v in range(len(VECS)):
                        sp.dma_start(vcol[:, v, :], vecs[v, :].rearrange("(c p) -> p c", p=P),
                                     allow_slow_non_contiguous=True).then_inc(setup_loads, 16)
                for q in range(QUARTERS):
                    load_quarter(0, q)
                for q in range(QUARTERS):
                    load_quarter(1, q)
                for q in range(QUARTERS):
                    load_quarter(2, q)
                store_h1(0)
                with sp.Fori(3, NB) as t:
                    for q in range(QUARTERS):
                        load_quarter(t, q)
                    store_h1(t - 2)
                store_h1(NB - 2)
                store_h1(NB - 1)
                sp.wait_ge(h1_stored, 16 * NB)

            SETUP_LOADS = 16 * (16 + len(VECS))

            @block.tensor
            def _(pe):
                mm = pe.matmul

                pe.wait_ge(setup_loads, SETUP_LOADS)
                for m in range(CH):
                    for c in range(CH):
                        mm(banks[0][:, m:m + 1], raw_wq[:, c, m * P:(m + 1) * P], vcol[:, QB, c:c + 1],
                           start=(c == 0), stop=(c == CH - 1)).then_inc(su_p, 1)
                for m in range(2 * CH):
                    for c in range(CH):
                        mm(banks[1][:, m:m + 1], raw_wqkv[:, c, m * P:(m + 1) * P], vcol[:, BETA, c:c + 1],
                           start=(c == 0), stop=(c == CH - 1)).then_inc(su_p, 1)
                pe.wait_ge(su_v, 11)
                for c in range(CH):
                    mm(banks[2][:, 0:C], beta_wide[:, c, :], raw_wqkv[:, c, 2 * C:3 * C],
                       start=(c == 0), stop=(c == CH - 1)).then_inc(su_p, 1)
                for c in range(CH):
                    mm(banks[3][:, 0:C], bv_wide[:, c, :], PW[:, c, :],
                       start=(c == 0), stop=(c == CH - 1)).then_inc(su_p, 1)
                pe.wait_ge(su_v, 20)
                for h in range(HEADS):
                    for part, w in enumerate((wk_high, wk_low)):
                        mm(wk_stack_psum(h), sel_k[:, h % HPC, part, :], w[:, h // HPC, :],
                           start=(part == 0), stop=(part == 1)).then_inc(su_p, 1)
                for c in range(CH):
                    for m in range(CH):
                        pe.transpose(halved(4)[:, c, m * P:(m + 1) * P], wtmp[:, m, c * P:(c + 1) * P],
                                     ident[:, :]).then_inc(su_p, 1)
                pe.wait_ge(setup_done, 1)

                def turn_feats(t):
                    wait(pe, feats_summed, at(t, QUARTERS, QUARTERS))
                    wait(pe, s_taken, at(t, QUARTERS, 0))
                    for l in range(LH):
                        for c in range(CH):
                            last = pe.transpose(halved(2)[:, l, c * P:(c + 1) * P], R[:, c, l * P:(l + 1) * P], ident[:, :])
                    last.then_inc(r_turned, 1)

                def turn_qn(t):
                    wait(pe, qn_ready, at(t, 1, 1))
                    for c in range(CH):
                        for l in range(LH):
                            last = pe.transpose(halved(3)[:, c, l * P:(l + 1) * P], QNT[:, l, c * P:(c + 1) * P], ident[:, :])
                    last.then_inc(qn_turned, 1)

                def make_q(t):
                    wait(pe, qn_taken, at(t, 1, 1))
                    for m in range(CH):
                        for c in range(CH):
                            last = mm(halved(2)[:, m, :], WQ[:, c, m * P:(m + 1) * P], QN[:, c, :],
                                      start=(c == 0), stop=(c == CH - 1))
                    last.then_inc(q_made, 1)

                def stack_q(t, steps):
                    for i in steps:
                        if i < 2:
                            wait(pe, q_split, at(t, 1, 1))
                        else:
                            wait(pe, (qs_taken_act, qs_taken_dve)[i % 2], at(t, 2, i // 2))
                        for j in range(2):
                            h = 2 * i + j
                            for part, q in enumerate((QH, QL)):
                                last = mm(halved(2 + i % 2)[:, j, :], SEL[:, h % HPC, part, :], q[:, h // HPC, :],
                                          start=(part == 0), stop=(part == 1))
                        last.then_inc(qs_made, 1)

                def g_taken(t, i):
                    if i in G_DVE:
                        wait(pe, g_taken_dve, at(t, len(G_DVE), G_DVE.index(i) + 1))
                    else:
                        before = sum(j < i for j in G_DVE)
                        wait(pe, g_taken_act, at(t, HEADS - len(G_DVE), i - before + 1))

                def make_g(t, steps):
                    for i in steps:
                        pair, c = i // CH, i % CH
                        if c == 0:
                            wait(pe, (qs_taken_act, qs_taken_dve)[pair % 2], at(t, 2, pair // 2 + 1))
                        if i >= 3:
                            g_taken(t, i - 3)
                        elif i == 2:
                            wait(pe, ao_taken, at(t - 1, CH, 0))
                        else:
                            wait(pe, z_taken, at(t, 2 * QUARTERS, i - 1))
                        for j in range(2):
                            h = 2 * pair + j
                            last = mm(halved(G_BANKS[i % 3])[:, j, :], WKs[:, h, c * P:(c + 1) * P], QS[:, h, :],
                                      start=True, stop=True)
                        last.then_inc(g_made, 1)

                def pixels(c, g):
                    return X[:, c, g * P:(g + 1) * P]

                def turn_pair(t, p):
                    if p % (PAIRS // QUARTERS) == 0:
                        q = p // (PAIRS // QUARTERS)
                        wait(pe, x_loaded[q], at(t, 16, 16))
                    if p >= 2:
                        wait(pe, xt_taken, at(t, PAIRS, p - 1))
                    elif p == 0:
                        g_taken(t, HEADS - 2)
                        g_taken(t, HEADS - 1)
                    for j in range(2):
                        for c in range(CH):
                            last = pe.transpose(halved(p % 2)[:, j, c * P:(c + 1) * P], pixels(c, 2 * p + j), ident[:, :])
                    last.then_inc(xt_made, 1)

                def score_pair(t, p):
                    ppq = PAIRS // QUARTERS
                    q = p // ppq
                    if p % ppq == 0 and q >= 2:
                        wait(pe, s_taken, at(t, QUARTERS, q - 1))
                    for j in range(2):
                        g = 2 * p + j
                        for c in range(CH):
                            last = mm(banks[2 + q % 2][:, (g % GPQ) * SH:(g % GPQ + 1) * SH], pixels(c, g),
                                      G[:, c, g * LPG:(g + 1) * LPG, :], start=(c == 0), stop=(c == CH - 1))
                    if p % ppq == ppq - 1:
                        last.then_inc(s_made, 1)

                def turn_scores(t, u):
                    wait(pe, e_ready, at(t, 2, u + 1))
                    wait(pe, p_taken, at(t, 2, u))
                    pe.transpose(banks[4][:, 0:P], E[:, u * GPH:(u + 1) * GPH, :].rearrange("p g h -> p (g h)"),
                                 ident[:, :]).then_inc(e_turned, 1)

                def turn_probs(t, u):
                    wait(pe, p_ready, at(t, 2, u + 1))
                    pe.transpose(banks[4][:, 0:P], PE_[:, u, :, :].rearrange("p l n -> p (l n)"),
                                 ident[:, :]).then_inc(p_turned, 1)

                def pool_pixels(t, steps):
                    for i in steps:
                        q, c = i // CH, i % CH
                        if c == 0:
                            wait(pe, p_spread, at(t, QUARTERS, q + 1))
                        if i >= 2:
                            wait(pe, z_taken, at(t, 2 * QUARTERS, i - 1))
                        elif i == 0:
                            wait(pe, xt_taken, at(t, PAIRS, PAIRS))
                        for g in range(q * GPQ, (q + 1) * GPQ):
                            last = mm(banks[i % 2][:, (g % GPQ) * SH:(g % GPQ + 1) * SH], XT[:, g, c * P:(c + 1) * P],
                                      A[:, g, :, :], start=True, stop=True)
                        last.then_inc(z_made, 1)

                def aggregate(t, m):
                    if m == 0:
                        wait(pe, z_taken, at(t, 2 * QUARTERS, 2 * QUARTERS))
                    for j in range(HPC):
                        for c in range(CH):
                            last = mm(halved(4)[:, m, :], WVm[:, c, m * HPC + j, :], Z[:, c, m * HPC + j, :],
                                      start=(j == 0 and c == 0), stop=(j == HPC - 1 and c == CH - 1))
                    last.then_inc(agg_made, 1)

                def project(t):
                    wait(pe, agg_taken, at(t, 1, 1))
                    for l in range(LH):
                        for c in range(CH):
                            last = mm(halved(4)[:, l, :], AG[:, c, l * P:(l + 1) * P], PW[:, c, :],
                                      start=(c == 0), stop=(c == CH - 1))
                    last.then_inc(proj_made, 1)

                def turn_tokens(bank, src, turned):
                    for c in range(CH):
                        for l in range(LH):
                            last = pe.transpose(halved(bank)[:, c, l * P:(l + 1) * P], src[:, l, c * P:(c + 1) * P], ident[:, :])
                    last.then_inc(turned, 1)

                def turn_h0(a):
                    wait(pe, h0_ready, at(a, 1, 1))
                    wait(pe, u_var, at(a, 1, 0))
                    turn_tokens(5, H0, h_turned)

                def turn_n(a):
                    wait(pe, n_ready, at(a, 1, 1))
                    wait(pe, ao_taken, at(a, CH, 0))
                    turn_tokens(7, NH, n_turned)

                def rows_of(bank, w, first, src, made):
                    for m in range(CH):
                        for c in range(CH):
                            last = mm(halved(bank)[:, m, :], w[:, c, first + m * P:first + (m + 1) * P], src[:, c, :],
                                      start=(c == 0), stop=(c == CH - 1))
                    last.then_inc(made, 1)

                def tokens_of(bank, w, first, src, made):
                    for l in range(LH):
                        for c in range(CH):
                            last = mm(halved(bank)[:, l, :], src[:, c, l * P:(l + 1) * P], w[:, c, first:first + C],
                                      start=(c == 0), stop=(c == CH - 1))
                    last.then_inc(made, 1)

                def attn_q(a):
                    wait(pe, n_taken, at(a, 1, 1))
                    wait(pe, gate_taken, at(a, CH, CH))
                    rows_of(5, WA, 0, NT, aq_made)

                def attn_k(a):
                    rows_of(6, WA, C, NT, ak_made)

                def attn_v(a):
                    tokens_of(7, WA, 2 * C, NT, av_made)

                def attn_gate(a):
                    wait(pe, h_taken, at(a, 1, 1))
                    rows_of(5, WG, 0, HT, gate_made)

                def attn_scores(a, h):
                    if h == 0:
                        wait(pe, ak_taken, at(a, CH, CH))
                    elif h == 1:
                        wait(pe, av_taken, at(a, 1, 1))
                    else:
                        wait(pe, as_exped, at(a, HEADS * LH, (h - 1) * LH))
                    wait(pe, qm_ready, at(a, HEADS, h + 1))
                    for i in range(LH):
                        last = mm(halved(6 + h % 2)[:, i, :], QM[:, h, i * P:(i + 1) * P], K[:, h // HPC, :],
                                  start=True, stop=True)
                    last.then_inc(as_made, 1)

                def attn_out(a, m):
                    wait(pe, vs_ready, at(a, CH, m + 1))
                    if m == 0:
                        wait(pe, as_exped, at(a, HEADS * LH, (HEADS - 1) * LH))
                    else:
                        wait(pe, as_exped, at(a, HEADS * LH, HEADS * LH))
                    for j in range(HPC):
                        for i in range(LH):
                            last = mm(banks[6 + m][:, 0:LOC], VS[:, i, m * HPC + j, :], EX[:, m * HPC + j, i, :],
                                      start=(j == 0 and i == 0), stop=(j == HPC - 1 and i == LH - 1))
                    last.then_inc(ao_made, 1)

                def attn_final(a):
                    wait(pe, ao_taken, at(a, CH, CH))
                    wait(pe, gate_taken, at(a, CH, CH))
                    tokens_of(5, WF, 0, O, fin_made)

                def image(t, a, more=True):
                    T, B = t is not None, a is not None
                    if T: make_g(t, range(0, 2))
                    if B: turn_h0(a)
                    if T: make_g(t, range(2, 5))
                    if B: attn_gate(a)
                    if T: make_g(t, range(5, 6))
                    if B: turn_n(a)
                    if T: make_g(t, range(6, 8))
                    if B: attn_q(a)
                    for p in range(PAIRS):
                        if T:
                            turn_pair(t, p)
                            if p: score_pair(t, p - 1)
                            if p == 11: turn_scores(t, 0)
                        if B:
                            if p == 0:
                                if T: g_taken(t, 5)
                                attn_k(a)
                            if p == 1: attn_v(a)
                            if p in SCORE_SLOTS: attn_scores(a, SCORE_SLOTS.index(p))
                    if T:
                        score_pair(t, PAIRS - 1)
                        turn_probs(t, 0)
                    if B: attn_out(a, 0)
                    if T: turn_scores(t, 1)
                    if B: attn_out(a, 1)
                    if T:
                        pool_pixels(t, range(0, 2))
                        turn_probs(t, 1)
                        pool_pixels(t, range(2, 4))
                    if T:
                        pool_pixels(t, range(4, 6))
                        if more: turn_feats(t + 1)
                        pool_pixels(t, range(6, 8))
                    if B: attn_final(a)
                    if T:
                        if more: turn_qn(t + 1)
                        aggregate(t, 0)
                        if more: make_q(t + 1)
                        aggregate(t, 1)
                        if more: stack_q(t + 1, range(0, 2))
                        project(t)
                        if more: stack_q(t + 1, range(2, 4))

                turn_feats(0)
                turn_qn(0)
                make_q(0)
                stack_q(0, range(0, 4))
                image(0, None)
                image(1, 0)
                with pe.Fori(2, NB - 1) as t:
                    image(t, t - 1)
                image(NB - 1, NB - 2, more=False)
                image(None, NB - 1)

            @block.scalar
            def _(act):
                def copy(out, in_):
                    return act.activation(out, in_, ACT.Copy)

                act.wait_ge(setup_done, 1)

                def take_r(t):
                    wait(act, r_turned, at(t, 1, 1))
                    wait(act, rb_ready, at(t, 1, 0))
                    act.activation(RT[:, :, :], halved(2), ACT.Copy, scale=1.0 / N2).then_inc(r_taken, 1)

                def take_qn(t):
                    wait(act, qn_turned, at(t, 1, 1))
                    wait(act, q_made, at(t, 1, 0))
                    copy(QN[:, :, :], halved(3)).then_inc(qn_taken, 1)

                def take_q(t):
                    wait(act, q_made, at(t, 1, 1))
                    wait(act, q_split, at(t, 1, 0))
                    for m in range(CH):
                        act.activation(Q[:, m, :], halved(2)[:, m, :], ACT.Identity, bias=bq_col[:, m:m + 1],
                                       scale=1.0).then_inc(q_taken, 1)
                    wait(act, q_taken, at(t, CH, CH))
                    wait(act, qs_made, at(t, HPC, 0))
                    copy(QH[:, :, :], Q[:, :, :]).then_inc(q_high, 1)

                def take_qs(t, i):
                    wait(act, qs_made, at(t, HPC, i + 1))
                    wait(act, g_made, at(t, HEADS, 0))
                    copy(QS[:, 2 * i:2 * i + 2, :], halved(2)).then_inc(qs_taken_act, 1)

                def take_g(t, i):
                    pair, c = i // CH, i % CH
                    wait(act, g_made, at(t, HEADS, i + 1))
                    wait(act, s_made, at(t, QUARTERS, 0))
                    copy(G[:, c, :, 2 * pair:2 * pair + 2].rearrange("p l h -> p h l"),
                         halved(G_BANKS[i % 3])).then_inc(g_taken_act, 1)

                def take_xt(t, p):
                    wait(act, xt_made, at(t, PAIRS, p + 1))
                    if p == 0:
                        wait(act, z_made, at(t, 2 * QUARTERS, 0))
                        wait(act, stats_done, at(t, GROUPS, 0))
                    copy(XT[:, 2 * p:2 * p + 2, :], halved(p % 2)).then_inc(xt_taken, 1)

                def exp_scores(t, u):
                    wait(act, e_shifted, at(t, 2, u + 1))
                    act.activation(PE_[:, u, :, :], PE_[:, u, :, :], ACT.Exp).then_inc(e_exped, 1)

                def take_z(t, i):
                    q, c = i // CH, i % CH
                    wait(act, z_made, at(t, 2 * QUARTERS, i + 1))
                    wait(act, agg_made, at(t, CH, 0))
                    copy(Z[:, c, :, q * GPQ * LPG:(q + 1) * GPQ * LPG],
                         banks[i % 2][:, :].rearrange("p (l h) -> p h l", h=HEADS)).then_inc(z_taken, 1)

                def take_agg(t):
                    wait(act, agg_made, at(t, CH, CH))
                    wait(act, proj_made, at(t, 1, 0))
                    copy(AG[:, :, :], halved(4)).then_inc(agg_taken, 1)

                def take_h(a):
                    wait(act, h_turned, at(a, 1, 1))
                    wait(act, gate_made, at(a, 1, 0))
                    copy(HT[:, :, :], halved(5)).then_inc(h_taken, 1)

                def take_n(a):
                    wait(act, n_turned, at(a, 1, 1))
                    wait(act, av_made, at(a, 1, 0))
                    copy(NT[:, :, :], halved(7)).then_inc(n_taken, 1)

                def take_attn_q(a):
                    wait(act, aq_made, at(a, 1, 1))
                    for m in range(CH):
                        act.activation(AQ[:, m, :], halved(5)[:, m, :], ACT.Identity, bias=aq_bias[:, m:m + 1],
                                       scale=float(D) ** -0.5).then_inc(aq_taken, 1)

                def take_attn_k(a):
                    wait(act, ak_made, at(a, 1, 1))
                    for m in range(CH):
                        act.activation(K[:, m, :], halved(6)[:, m, :], ACT.Identity,
                                       bias=bk_col[:, m:m + 1]).then_inc(ak_taken, 1)

                def take_gate(a):
                    wait(act, gate_made, at(a, 1, 1))
                    wait(act, fin_made, at(a, 1, 0))
                    for m in range(CH):
                        act.activation(GT[:, m, :], halved(5)[:, m, :], ACT.Tanh, bias=gb_half[:, m:m + 1],
                                       scale=0.5).then_inc(gate_taken, 1)

                def exp_attn(a, h):
                    wait(act, as_max, at(a, HEADS, h + 1))
                    if h == 0:
                        wait(act, ao_made, at(a, CH, 0))
                        wait(act, vs_ready, at(a, CH, 0))
                    for i in range(LH):
                        act.activation(EX[:, h, i, :], halved(6 + h % 2)[:, i, :], ACT.Exp, bias=nmax[:, h, i:i + 1],
                                       accum_out=esum[:, h, i:i + 1]).then_inc(as_exped, 1)

                def take_gs(t, steps):
                    for i in steps:
                        if i not in G_DVE:
                            take_g(t, i)

                def take_zs(t, steps):
                    for i in steps:
                        take_z(t, i)

                def image(t, a, more=True):
                    T, B = t is not None, a is not None
                    if T: take_gs(t, range(0, 2))
                    if B: take_h(a)
                    if T: take_gs(t, range(2, 4))
                    if T: take_gs(t, range(4, 6))
                    if B: take_gate(a)
                    if B: take_n(a)
                    if T: take_gs(t, range(6, 8))
                    for p in range(PAIRS):
                        if T: take_xt(t, p)
                        if B:
                            if p == 0: take_attn_q(a)
                            if p == 1: take_attn_k(a)
                            if p - 1 in SCORE_SLOTS: exp_attn(a, SCORE_SLOTS.index(p - 1))
                        if T and p == 12: exp_scores(t, 0)
                    if T:
                        exp_scores(t, 1)
                        take_zs(t, range(0, 6))
                        if more: take_r(t + 1)
                        take_zs(t, range(6, 8))
                        if more:
                            take_qn(t + 1)
                            take_q(t + 1)
                        take_agg(t)
                        if more:
                            take_qs(t + 1, 0)
                            take_qs(t + 1, 2)

                take_r(0)
                take_qn(0)
                take_q(0)
                take_qs(0, 0)
                take_qs(0, 2)
                image(0, None)
                image(1, 0)
                with act.Fori(2, NB - 1) as t:
                    image(t, t - 1)
                image(NB - 1, NB - 2, more=False)
                image(None, NB - 1)

            T_LINKS, A_LINKS = 14, 7

            @block.vector
            def _(dve):
                dve.memset(halves[:, :], -0.5).then_inc(su_v, 1)
                dve.memset(ones, 1.0).then_inc(su_v, 1)
                dve.memset(c_eps[:, :], C * EPS).then_inc(su_v, 1)
                dve.memset(quarter_c[:, :], C / 4.0).then_inc(su_v, 1)
                dve.memset(WVm[:, :, :, :], 0.0).then_inc(su_v, 1)
                dve.memset(VS[:, :, :, :], 0.0).then_inc(su_v, 1)
                dve.wait_ge(setup_loads, SETUP_LOADS)
                dve.wait_ge(su_v, 6)
                dve.tensor_tensor(wtmp, raw_wv, row_b.unsqueeze(1).to_broadcast([P, CH, C]), ALU.mult).then_inc(su_v, 1)
                dve.wait_ge(su_v, 7)
                dve.tensor_reduce(bv_col[:, :, 0], wtmp, AX.X, ALU.add).then_inc(su_v, 1)
                dve.wait_ge(su_v, 8)
                for c in range(CH):
                    dve.tensor_scalar(bv_wide[:, c, :], ones, bv_col[:, c, :], None, ALU.mult).then_inc(su_v, 1)
                dve.tensor_tensor(beta_wide, vcol[:, BETA, :].unsqueeze(2).to_broadcast([P, CH, P]),
                                  ones.unsqueeze(1).to_broadcast([P, CH, P]), ALU.mult).then_inc(su_v, 1)
                n = 11
                for raw in (raw_wk, raw_wv):
                    if raw is raw_wv:
                        dve.wait_ge(su_v, n)
                    dve.tensor_tensor(wtmp if raw is raw_wv else raw_wk, raw,
                                      row_w.unsqueeze(1).to_broadcast([P, CH, C]), ALU.mult).then_inc(su_v, 1)
                    dst = wtmp if raw is raw_wv else raw_wk
                    n += 1
                    dve.wait_ge(su_v, n)
                    dve.tensor_reduce(wmean[:, :, 0], dst, AX.X, ALU.add).then_inc(su_v, 1)
                    n += 1
                    dve.wait_ge(su_v, n)
                    dve.scalar_tensor_tensor(dst, wmean.to_broadcast([P, CH, C]), -1.0 / C, dst,
                                             ALU.mult, ALU.add).then_inc(su_v, 1)
                    n += 1
                assert n == 17
                dve.wait_ge(su_v, n)
                dve.tensor_copy(QH[:, :, :], raw_wk).then_inc(su_v, 1)
                dve.wait_ge(su_v, n + 1)
                dve.tensor_copy(wk_high, QH[:, :, :]).then_inc(su_v, 1)
                dve.wait_ge(su_v, n + 2)
                dve.tensor_tensor(wk_low, raw_wk, wk_high, ALU.subtract).then_inc(su_v, 1)
                n += 3
                dve.tensor_copy(SEL[:, :, :, :], sel_q).then_inc(su_v, 1)
                dve.tensor_scalar(gb_half[:, :], vcol[:, BGATE, :], 0.5, None, ALU.mult).then_inc(su_v, 1)
                dve.tensor_scalar(WF[:, :, :], WF[:, :, :], 0.5, None, ALU.mult).then_inc(su_v, 1)
                for c in range(CH):
                    dve.tensor_scalar(WQ[:, c, :], raw_wq[:, c, :], vcol[:, QW, c:c + 1], None, ALU.mult).then_inc(su_v, 1)
                    dve.tensor_scalar(WA[:, c, :], raw_wqkv[:, c, :], vcol[:, GAMMA, c:c + 1], None, ALU.mult).then_inc(su_v, 1)
                SU_P = 2 * CH + 4 * CH + 2 * CH + 2 * HEADS + CH * CH
                dve.wait_ge(su_p, SU_P)
                dve.tensor_copy(bq_col[:, :], banks[0][:, 0:CH]).then_inc(su_v, 1)
                dve.tensor_scalar(aq_bias[:, :], banks[1][:, 0:CH], float(D) ** -0.5, None, ALU.mult).then_inc(su_v, 1)
                dve.tensor_copy(bk_col[:, :], banks[1][:, CH:2 * CH]).then_inc(su_v, 1)
                dve.tensor_copy(vb_row[:, :], banks[2][:, 0:C]).then_inc(su_v, 1)
                dve.tensor_tensor(pb_row[:, :], banks[3][:, 0:C], pb_raw, ALU.add).then_inc(su_v, 1)
                for h in range(HEADS):
                    dve.tensor_copy(WKs[:, h, :], wk_stack_psum(h)).then_inc(su_v, 1)
                n += HEADS + 3 + 2 * CH + 5
                dve.wait_ge(su_v, n)
                for m in range(CH):
                    for j in range(HPC):
                        h = m * HPC + j
                        dve.tensor_copy(WVm[:, :, h, j * D:(j + 1) * D], halved(4)[:, :, h * D:(h + 1) * D]).then_inc(su_v, 1)
                n += HEADS
                dve.wait_ge(su_v, n)
                dve.nop().then_inc(setup_done, 1)

                tstep, astep = Steps(dve, t_chain, T_LINKS), Steps(dve, a_chain, A_LINKS)
                rstep = Steps(dve, r_chain, 4)

                def sum_feats(t, q, c):
                    wait(dve, x_loaded[q], at(t, 16, 16))
                    wait(dve, r_turned, at(t, 1, 0))
                    ins = dve.tensor_reduce(R[:, c, q * LPQ:(q + 1) * LPQ], X[:, c, q * QP:(q + 1) * QP].rearrange(
                        "p (l n) -> p l n", n=N2), AX.X, ALU.add)
                    if c == CH - 1:
                        ins.then_inc(feats_summed, 1)

                def stats(src, n, mean_var, step, signal):
                    layer_stats(dve, src, n, bnt, mean_var, step, signal)

                def stats_r(t):
                    wait(dve, r_taken, at(t, 1, 1))
                    rstep.start(t)
                    stats(RT, LH, mv, rstep, r_var)
                    rstep.finish()

                def norm_q(t):
                    wait(dve, r_rstd, at(t, 1, 1))
                    for l in range(LH):
                        ins = dve.tensor_scalar(QNT[:, l, :], RT[:, l, :], mv[:, l, 0:1], rstd2[:, l:l + 1],
                                                ALU.subtract, ALU.mult)
                    ins.then_inc(qn_ready, 1)

                def q_low(t):
                    wait(dve, q_high, at(t, 1, 1))
                    dve.tensor_tensor(QL[:, :, :], Q[:, :, :], QH[:, :, :], ALU.subtract).then_inc(q_split, 1)

                def take_qs(t, i):
                    wait(dve, qs_made, at(t, HPC, i + 1))
                    dve.tensor_copy(QS[:, 2 * i:2 * i + 2, :], halved(3)).then_inc(qs_taken_dve, 1)

                def take_g(t, i):
                    pair, c = i // CH, i % CH
                    wait(dve, g_made, at(t, HEADS, i + 1))
                    dve.tensor_copy(G[:, c, :, 2 * pair:2 * pair + 2].rearrange("p l h -> p h l"),
                                    halved(G_BANKS[i % 3])).then_inc(g_taken_dve, 1)

                def pixel_stats(t, p):
                    wait(dve, xt_taken, at(t, PAIRS, p + 1))
                    for j in range(2):
                        dve.bn_stats(st[:, 2 * p + j, :], XT[:, 2 * p + j, :]).then_inc(stats_done, 1)

                def take_scores(t, q):
                    wait(dve, s_made, at(t, QUARTERS, q + 1))
                    dve.tensor_tensor(SM[:, :, :], banks[2 + q % 2][:, :].rearrange("p (g s) -> p g s", g=GPQ),
                                      pixmask[:, :].unsqueeze(1).to_broadcast([P, GPQ, SH]), ALU.mult).then_inc(s_taken, 1)
                    dve.wait_ge(s_taken, at(t, QUARTERS, q + 1))
                    tstep(dve.tensor_reduce(E[:, q * GPQ:(q + 1) * GPQ, :],
                                            SM[:, :, :].rearrange("p g (l h) -> p g h l", h=HEADS), AX.X, ALU.add))

                def by_head(u):
                    return RS[:, u * GPH:(u + 1) * GPH].unsqueeze(2).to_broadcast([P, GPH, HEADS])

                def scale_scores(t, u):
                    wait(dve, pix_rstd, at(t, QUARTERS, 2 * u + 2))
                    half = E[:, u * GPH:(u + 1) * GPH, :]
                    dve.tensor_tensor(half, half, by_head(u), ALU.mult).then_inc(e_ready, 1)

                def over_pixels(ap):
                    return ap.unsqueeze(2).to_broadcast([P, LPG, N2])

                def softmax_shift(t, u):
                    wait(dve, e_turned, at(t, 2, u + 1))
                    src = banks[4][:, 0:P].rearrange("p (l n) -> p l n", n=N2)
                    tstep(dve.tensor_reduce(mx[:, u, :], src, AX.X, ALU.max))
                    dve.tensor_tensor(PE_[:, u, :, :], src, over_pixels(mx[:, u, :]), ALU.subtract).then_inc(e_shifted, 1)

                def softmax_divide(t, u):
                    wait(dve, e_exped, at(t, 2, u + 1))
                    tstep(dve.tensor_reduce(den[:, u, :], PE_[:, u, :, :], AX.X, ALU.add))
                    tstep(dve.reciprocal(den[:, u, :], den[:, u, :]))
                    dve.tensor_tensor(PE_[:, u, :, :], PE_[:, u, :, :], over_pixels(den[:, u, :]), ALU.mult).then_inc(p_ready, 1)

                def take_probs(t, u):
                    wait(dve, p_turned, at(t, 2, u + 1))
                    wait(dve, p_spread, at(t, QUARTERS, 2 * u + 2 - QUARTERS))
                    dve.scalar_tensor_tensor(PR[:, u * GPH:(u + 1) * GPH, :], banks[4][:, 0:P].rearrange("p (g h) -> p g h", h=HEADS),
                                             float(C) ** 0.5, by_head(u), ALU.mult, ALU.mult).then_inc(p_taken, 1)

                def take_h0(t):
                    wait(dve, proj_made, at(t, 1, 1))
                    wait(dve, rb_ready, at(t, 1, 1))
                    wait(dve, h0_twice, at(t, 1, 0))
                    dve.tensor_tensor(H0[:, :, :], halved(4), RTB[:, :, :], ALU.add).then_inc(h0_ready, 1)
                    dve.wait_ge(h0_ready, at(t, 1, 1))

                def norm_h0(a, t):
                    wait(dve, h0_rstd, at(a, 1, 1))
                    if t is not None:
                        wait(dve, qn_turned, at(t, 1, 1))
                    for l in range(LH):
                        ins = dve.tensor_scalar(NH[:, l, :], H0[:, l, :], amv[:, l, 0:1], arstd[:, l:l + 1],
                                                ALU.subtract, ALU.mult)
                    ins.then_inc(n_ready, 1)

                def take_v(a):
                    wait(dve, av_made, at(a, 1, 1))
                    dve.tensor_tensor(V[:, :, :, :].rearrange("p l h d -> p l (h d)"), halved(7),
                                      vb_row[:, :].unsqueeze(1).to_broadcast([P, LH, C]), ALU.add).then_inc(av_taken, 1)

                def max_attn(a, h):
                    wait(dve, as_made, at(a, HEADS, h + 1))
                    dve.tensor_reduce(nmax[:, h, :], halved(6 + h % 2), AX.X, ALU.max, negate=True).then_inc(as_max, 1)

                def scale_v(a, m):
                    heads = slice(m * HPC, (m + 1) * HPC)
                    wait(dve, as_exped, at(a, HEADS * LH, (m + 1) * HPC * LH))
                    astep(dve.reciprocal(esum[:, heads, :], esum[:, heads, :]))
                    for j in range(HPC):
                        h = m * HPC + j
                        ins = dve.tensor_tensor(VS[:, :, h, j * D:(j + 1) * D], V[:, :, h, :],
                                                esum[:, h, :].unsqueeze(2).to_broadcast([P, LH, D]), ALU.mult)
                    ins.then_inc(vs_ready, 1)

                def gate_out(a, m):
                    wait(dve, ao_made, at(a, CH, m + 1))
                    if m == 0:
                        wait(dve, gate_taken, at(a, CH, CH))
                    dve.scalar_tensor_tensor(O[:, m, :], GT[:, m, :], 1.0, banks[6 + m][:, 0:LOC],
                                             ALU.add, ALU.mult).then_inc(ao_taken, 1)

                def add_attn(a):
                    wait(dve, fin_made, at(a, 1, 1))
                    wait(dve, h0_twice, at(a, 1, 1))
                    astep(dve.tensor_tensor(U[:, :, :], halved(5), H2[:, :, :], ALU.add))
                    stats(U, LH, bmv, astep, u_var)

                def norm_u(a):
                    wait(dve, u_rstd, at(a, 1, 1))
                    wait(dve, h1_stored, at(a, 16, 0))
                    for l in range(LH):
                        ins = dve.tensor_scalar(H1[:, l, :], U[:, l, :], bmv[:, l, 0:1], brstd[:, l:l + 1],
                                                ALU.subtract, ALU.mult)
                    ins.then_inc(h1_ready, 1)

                def image(t, a, more=True):
                    T, B = t is not None, a is not None
                    if T: tstep.start(t)
                    if B: astep.start(a)
                    if B: norm_h0(a, t)
                    if T:
                        for i in G_DVE:
                            take_g(t, i)
                    for p in range(PAIRS):
                        if T and p == 10: scale_scores(t, 0)
                        if T and p == 12: softmax_shift(t, 0)
                        if T and p == 13: softmax_divide(t, 0)
                        if B and p - 1 in SCORE_SLOTS: max_attn(a, SCORE_SLOTS.index(p - 1))
                        if T:
                            if p in (5, 9, 13): take_scores(t, (p - 5) // 4)
                            pixel_stats(t, p)
                        if B:
                            if p == 2: take_v(a)
                            if p == 11: scale_v(a, 0)
                        if T and more and p in (7,): sum_feats(t + 1, 0, p // 15)
                    if T:
                        take_probs(t, 0)
                        take_scores(t, QUARTERS - 1)
                    if B: scale_v(a, 1)
                    if T:
                        scale_scores(t, 1)
                        if more: sum_feats(t + 1, 0, 1)
                        softmax_shift(t, 1)
                        if more: sum_feats(t + 1, 1, 0)
                        softmax_divide(t, 1)
                        if more: sum_feats(t + 1, 1, 1)
                        take_probs(t, 1)
                        if more: sum_feats(t + 1, 2, 0)
                    if B: gate_out(a, 0)
                    if T and more:
                        sum_feats(t + 1, 2, 1)
                        sum_feats(t + 1, 3, 0)
                        sum_feats(t + 1, 3, 1)
                    if B: gate_out(a, 1)
                    if T and more:
                        stats_r(t + 1)
                        norm_q(t + 1)
                    if B:
                        add_attn(a)
                        norm_u(a)
                    if T:
                        if more:
                            q_low(t + 1)
                            take_qs(t + 1, 1)
                        take_h0(t)
                        stats(H0, LH, amv, tstep, h0_var)
                        if more: take_qs(t + 1, 3)
                        tstep.finish()
                    if B: astep.finish()

                for q in range(QUARTERS):
                    for c in range(CH):
                        sum_feats(0, q, c)
                stats_r(0)
                norm_q(0)
                q_low(0)
                take_qs(0, 1)
                take_qs(0, 3)
                image(0, None)
                image(1, 0)
                with dve.Fori(2, NB - 1) as t:
                    image(t, t - 1)
                image(NB - 1, NB - 2, more=False)
                image(None, NB - 1)

            @block.gpsimd
            def _(pool):
                tstep = Steps(pool, pool_t_chain, 3 + 4 * QUARTERS)
                pool.wait_ge(setup_done, 1)

                def root(out, var, signal):
                    pool.tensor_tensor(out, var, halves[:, 0:out.shape[1]], ALU.pow).then_inc(signal, 1)

                def feats_rstd(t):
                    wait(pool, r_var, at(t, 1, 1))
                    root(rstd2[:, :], mv[:, :, 1], r_rstd)

                def feats_bias(t):
                    wait(pool, h0_ready, at(t, 1, 0))
                    pool.tensor_tensor(RTB[:, :, :], RT[:, :, :], pb_row[:, :].unsqueeze(1).to_broadcast([P, LH, C]),
                                       ALU.add).then_inc(rb_ready, 1)

                def pixel_rstd(t, q):
                    groups = slice(q * GPQ, (q + 1) * GPQ)
                    wait(pool, stats_done, at(t, GROUPS, (q + 1) * GPQ))
                    diff, sq = vt[:, 0, groups], vt[:, 1, groups]
                    if q % 2 == 0:
                        wait(pool, p_taken, at(t, 2, q // 2 - 1))
                    pool.tensor_tensor(diff, st[:, groups, 1], st[:, groups, 4], ALU.subtract)
                    tstep(pool.tensor_tensor(sq, st[:, groups, 2], st[:, groups, 5], ALU.add))
                    pool.tensor_tensor(sq, sq, c_eps[:, :], ALU.add)
                    tstep(pool.tensor_tensor(diff, diff, diff, ALU.mult))
                    tstep(pool.tensor_tensor(diff, diff, quarter_c[:, :], ALU.mult))
                    tstep(pool.tensor_tensor(sq, sq, diff, ALU.add))
                    root(RS[:, groups], sq, pix_rstd)

                def spread(t, q):
                    if q % 2 == 0:
                        wait(pool, p_taken, at(t, 2, q // 2 + 1))
                        wait(pool, z_made, at(t, 2 * QUARTERS, 2 * (q + 2) - 2 * QUARTERS))
                    g = slice(q * GPQ, (q + 1) * GPQ)
                    pool.tensor_tensor(A[:, g, :, :], PR[:, g, :].unsqueeze(2).to_broadcast([P, GPQ, LPG, HEADS]),
                                       pixmask[:, :].rearrange("p (l h) -> p l h", h=HEADS).unsqueeze(1).to_broadcast(
                                           [P, GPQ, LPG, HEADS]), ALU.mult).then_inc(p_spread, 1)

                def mask_q(a):
                    wait(pool, aq_taken, at(a, CH, CH))
                    wait(pool, as_made, at(a, HEADS, 0))
                    for h in range(HEADS):
                        pool.tensor_tensor(QM[:, h, :], AQ[:, h // HPC, :], headmask[:, h % HPC:h % HPC + 1].to_broadcast([P, LOC]),
                                           ALU.mult).then_inc(qm_ready, 1)

                def h0_parts(t):
                    wait(pool, h0_var, at(t, 1, 1))
                    wait(pool, n_ready, at(t, 1, 0))
                    root(arstd[:, :], amv[:, :, 1], h0_rstd)
                    wait(pool, h1_ready, at(t, 1, 0))
                    for l in range(LH):
                        tstep(pool.tensor_tensor(H2[:, l, :], H0[:, l, :], H0[:, l, :], ALU.add))
                    for l in range(LH):
                        ins = pool.tensor_tensor(H2[:, l, :], H2[:, l, :], bf_row[:, :], ALU.add)
                        if l < LH - 1:
                            tstep(ins)
                    ins.then_inc(h0_twice, 1)

                def u_root(a):
                    wait(pool, u_var, at(a, 1, 1))
                    wait(pool, h1_ready, at(a, 1, 0))
                    root(brstd[:, :], bmv[:, :, 1], u_rstd)

                def image(t, a, more=True):
                    T, B = t is not None, a is not None
                    if B: mask_q(a)
                    if T:
                        tstep.start(t)
                        feats_bias(t)
                        for q in range(QUARTERS):
                            pixel_rstd(t, q)
                        spread(t, 0)
                        spread(t, 1)
                        spread(t, 2)
                        spread(t, 3)
                        if more: feats_rstd(t + 1)
                    if B: u_root(a)
                    if T:
                        h0_parts(t)
                        tstep.finish()

                feats_rstd(0)
                image(0, None)
                image(1, 0)
                with pool.Fori(2, NB - 1) as t:
                    image(t, t - 1)
                image(NB - 1, NB - 2, more=False)
                image(None, NB - 1)

        TOK = 512
        TT = TOK // P
        CHUNKS = NB * LOC // TOK
        E6 = EXPERTS
        E_L = E6 * CH
        w_loads, expert_loaded = sem("ffn_biases_loaded"), [sem(f"expert{e}_loaded") for e in range(E6)]
        tok_free = sem("tok_free")
        tok_loaded, out_stored = [sem(f"tok_loaded{i}") for i in range(2)], sem("out_stored")
        w_high, w_split = sem("weights_high"), sem("weights_split")
        m_turned, m_taken, m_high, m_split = sem("m_turned"), sem("m_taken"), sem("m_high"), sem("m_split")
        rh_made, rh_taken, logits_made = sem("rh_made"), sem("rh_taken"), sem("logits_made")
        rt_shifted, rt_exped = sem("router_shifted"), sem("router_exped")
        wt_ready, wt_turned, wt_taken, b3_made = sem("route_ready"), sem("route_turned"), sem("route_taken"), sem("b3_made")
        l1_made, l1_taken, l2_made, l2_taken = sem("l1_made"), sem("l1_taken"), sem("l2_made"), sem("l2_taken")
        a1_high, a1_split, a2_high, a2_split = sem("hidden1_high"), sem("hidden1_split"), sem("hidden2_high"), sem("hidden2_split")
        l3_made, l3_taken = sem("l3_made"), sem("l3_taken")
        f_var, f_rstd, f_ready = sem("f_var"), sem("f_rstd"), sem("f_ready")
        route_chain, weigh_chain, norm_chain = sem("route_steps"), sem("weigh_steps"), sem("norm_steps")

        with ExitStack() as two:
            class Split:
                def __init__(self, name, *shape):
                    self.high = sb(two, name + "_high", *shape, dtype=F32R)
                    self.low = sb(two, name + "_low", *shape, dtype=F32R)

            W = sb(two, "expert_weights", E6, 3, CH, C)
            WS = Split("expert_weights", E6, 3, CH, C)
            B1, B2 = sb(two, "expert_b1", E6, CH), sb(two, "expert_b2", E6, CH)
            B3 = two.enter_context(nc.sbuf_tensor("expert_b3", [E6, C], F32))
            RW1, RW2 = sb(two, "router_w1", CH, P), sb(two, "router_w2", E6)
            RB1, RB2 = sb(two, "router_b1", 1), sb(two, "router_b2", E6)
            before = sb(two, "expert_before", E6, E6)
            HTOK = sb(two, "tokens", 2, TT, C)
            HC, HS = sb(two, "tokens_turned", CH, TOK), Split("tokens_turned", 2, CH, TOK)
            RH = sb(two, "router_hidden", TOK)
            LG, PB_, EL = sb(two, "logits", TT, E6), sb(two, "probs", TT, E6), sb(two, "router_exp", TT, E6)
            PX = sb(two, "weights_top2", 2, TT, E6)
            l_mx, l_den = sb(two, "logit_max", TT), sb(two, "weight_sum", TT)
            gt, eq, rank = sb(two, "larger", TT, E6, E6), sb(two, "equal_before", TT, E6, E6), sb(two, "rank", TT, E6)
            WTT = two.enter_context(nc.sbuf_tensor("weights_turned", [E6, TT, P], F32))
            A1, A1S = sb(two, "hidden1", CH, TOK), Split("hidden1", CH, TOK)
            A2, A2S = sb(two, "hidden2", CH, TOK), Split("hidden2", CH, TOK)
            ACC = sb(two, "combined", 2, TT, C)
            fst, fmv, frstd = sb(two, "bn_ffn", TT, 8), sb(two, "mean_var_ffn", TT, 2), sb(two, "rstd_ffn", TT)
            OUT = sb(two, "out_tokens", TT, C)

            tok_view = h1_dram.rearrange("(i k p) c -> i p k c", k=TT, p=P)
            out_view = out.rearrange("b l c -> (b l) c").rearrange("(i k p) c -> i p k c", k=TT, p=P)
            WLOADS = 10
            PAIRS2 = CHUNKS // 2
            assert PAIRS2 >= 2

            block = two.enter_context(nc.Block())

            @block.sync
            def _(sp):
                def load_tokens(i, slot):
                    wait(sp, tok_free, at(i, 1, -1))
                    sp.dma_start(HTOK[:, slot, :, :], tok_view[i]).then_inc(tok_loaded[slot], 16)

                sp.wait_ge(h1_stored, 16 * NB)
                load_tokens(0, 0)
                sp.dma_start(RW1[:, :, :], rw1.rearrange("(c p) n -> p c n", p=P)).then_inc(w_loads, 16)
                sp.dma_start(RW2[:, :], rw2).then_inc(w_loads, 16)
                with nc.allow_non_contiguous_dma(reason="biases, once"):
                    for dst, src in ((B1[:, :, 0], eb1[:, 0:P].rearrange("e p -> p e")), (B1[:, :, 1], eb1[:, P:C].rearrange("e p -> p e")),
                                     (B2[:, :, 0], eb2[:, 0:P].rearrange("e p -> p e")), (B2[:, :, 1], eb2[:, P:C].rearrange("e p -> p e")),
                                     (RB1[:, :], rb1.rearrange("(p o) -> p o", o=1))):
                        sp.dma_start(dst, src, allow_slow_non_contiguous=True).then_inc(w_loads, 16)
                sp.dma_start(RB2[:, :], rb2.partition_broadcast(P)).then_inc(w_loads, 16)
                sp.dma_start(B3[:, :], eb3).then_inc(w_loads, 16)
                sp.dma_start(before[:, :, :], masks_in[:, SH + HPC:SH + HPC + E6 * E6].rearrange(
                    "p (a b) -> p a b", a=E6)).then_inc(w_loads, 16)

                for e in range(E6):
                    for n, w in enumerate((ew1, ew2, ew3)):
                        sp.dma_start(W[:, e, n, :, :], w[e].rearrange("(c p) n -> p c n", p=P)).then_inc(expert_loaded[e], 16)
                load_tokens(1, 1)

                def store(i):
                    wait(sp, f_ready, at(i, 1, 1))
                    sp.dma_start(out_view[i], OUT[:, :, :]).then_inc(out_stored, 16)

                with sp.Fori(1, CHUNKS // 2) as j:
                    for k in range(2):
                        load_tokens(2 * j + k, k)
                        store(2 * j + k - 2)
                store(CHUNKS - 2)
                store(CHUNKS - 1)
                sp.wait_ge(out_stored, 16 * CHUNKS)

            @block.tensor
            def _(pe):
                mm = pe.matmul
                pe.wait_ge(w_loads, 16 * WLOADS)

                def turn_tokens(i, half, slot, c):
                    if c == 0:
                        pe.wait_ge(tok_loaded[slot], at(half, 16, 16))
                    wait(pe, m_taken, at(i, CH, c))
                    for k in range(TT):
                        last = pe.transpose(banks[6][:, k * P:(k + 1) * P], HTOK[:, slot, k, c * P:(c + 1) * P], ident[:, :])
                    last.then_inc(m_turned, 1)

                def router(i, slot):
                    pe.wait_ge(m_taken, at(i, CH, CH))
                    wait(pe, wt_taken, at(i, 1, 0))
                    for c in range(CH):
                        last = mm(banks[7][:, :], RW1[:, c, :], HC[:, c, :], start=(c == 0), stop=(c == CH - 1))
                    last.then_inc(rh_made, 1)

                def logits(i):
                    pe.wait_ge(rh_taken, at(i, 1, 1))
                    for k in range(TT):
                        last = mm(banks[7][:, k * E6:(k + 1) * E6], RH[:, k * P:(k + 1) * P], RW2[:, :], start=True, stop=True)
                    last.then_inc(logits_made, 1)

                def turn_route(i, slot):
                    pe.wait_ge(wt_ready, at(i, 1, 1))
                    for k in range(TT):
                        last = pe.transpose(banks[7][0:E6, k * P:(k + 1) * P], PX[:, slot, k, :], ident[:, :])
                    last.then_inc(wt_turned, 1)

                def open_sum(i):
                    pe.wait_ge(wt_taken, at(i, 1, 1))
                    wait(pe, l3_taken, at(i, E6 + 1, 0))
                    for k in range(TT):
                        last = mm(halved(4 + k // 2)[:, k % 2, :], WTT[:, k, :], B3[:, :], start=True, stop=True)
                    last.then_inc(b3_made, 1)

                def product(out, a, a_at, b, b_at, start, stop):
                    mm(out, a.high[a_at], b.high[b_at], start=start, stop=False)
                    mm(out, a.high[a_at], b.low[b_at], start=False, stop=False)
                    return mm(out, a.low[a_at], b.high[b_at], start=False, stop=stop)

                def hidden(e, n, src, src_at, first_bank, made):
                    for m in range(CH):
                        for c in range(CH):
                            last = product(banks[first_bank + m][:, :], WS, (slice(None), e, n, c, slice(m * P, (m + 1) * P)),
                                           src, src_at(c), c == 0, c == CH - 1)
                        last.then_inc(made, 1)

                def layer1(i, e, slot):
                    if e == 0:
                        pe.wait_ge(m_split, at(i, CH, CH))
                    wait(pe, l1_taken, at(i, E_L, e * CH))
                    hidden(e, 0, HS, lambda c: (slice(None), slot, c, slice(None)), 0, l1_made)

                def layer2(i, e):
                    pe.wait_ge(a1_split, at(i, E_L, (e + 1) * CH))
                    wait(pe, l2_taken, at(i, E_L, e * CH))
                    hidden(e, 1, A1S, lambda c: (slice(None), c, slice(None)), 2, l2_made)

                def layer3(i, e):
                    pe.wait_ge(a2_split, at(i, E_L, (e + 1) * CH))
                    pe.wait_ge(l3_taken, at(i, E6 + 1, e + 1))
                    for k in range(TT):
                        for c in range(CH):
                            last = product(halved(4 + k // 2)[:, k % 2, :], A2S, (slice(None), c, slice(k * P, (k + 1) * P)),
                                           WS, (slice(None), e, 2, c, slice(None)), c == 0, c == CH - 1)
                    last.then_inc(l3_made, 1)

                def chunk(i, half, slot, first=False, final=False):
                    for e in range(E6):
                        if first:
                            pe.wait_ge(w_split, 3 * (e + 1))
                        layer1(i, e, slot)
                        if not final:
                            if e == 3: turn_tokens(i + 1, half + slot, 1 - slot, 0)
                            if e == 4: router(i + 1, 1 - slot)
                        if e == 2: open_sum(i)
                        if e >= 1:
                            layer2(i, e - 1)
                        elif not first:
                            layer2(i - 1, E6 - 1)
                        if e == 1: turn_route(i, slot)
                        if e >= 2:
                            layer3(i, e - 2)
                        elif not first:
                            layer3(i - 1, e + E6 - 2)
                        if e == 3 and not final: turn_tokens(i + 1, half + slot, 1 - slot, 1)
                        if e == 4 and not final: logits(i + 1)
                    if final:
                        layer3(i, E6 - 2)
                        layer2(i, E6 - 1)
                        layer3(i, E6 - 1)

                for c in range(CH):
                    turn_tokens(0, 0, 0, c)
                router(0, 0)
                logits(0)
                chunk(0, 0, 0, first=True)
                chunk(1, 0, 1)
                if PAIRS2 > 2:
                    with pe.Fori(1, PAIRS2 - 1) as j:
                        for k in range(2):
                            chunk(2 * j + k, j, k)
                chunk(CHUNKS - 2, PAIRS2 - 1, 0)
                chunk(CHUNKS - 1, PAIRS2 - 1, 1, final=True)

            @block.scalar
            def _(act):
                act.wait_ge(w_loads, 16 * WLOADS)

                def exp(i, n):
                    act.wait_ge(rt_shifted, at(i, 2, n))
                    act.activation(EL[:, :, :], EL[:, :, :], ACT.Exp).then_inc(rt_exped, 1)

                def weights_high(e):
                    act.wait_ge(expert_loaded[e], 16 * 3)
                    for n in range(3):
                        act.activation(WS.high[:, e, n, :, :], W[:, e, n, :, :], ACT.Copy).then_inc(w_high, 1)

                def take_turned(i, c):
                    if c == 0:
                        wait(act, rh_made, at(i, 1, 0))
                        wait(act, m_split, at(i, CH, 0))
                    act.wait_ge(m_turned, at(i, CH, c + 1))
                    act.activation(HC[:, c, :], banks[6][:, :], ACT.Copy).then_inc(m_taken, 1)

                def tokens_high(i, slot):
                    for c in range(CH):
                        act.wait_ge(m_taken, at(i, CH, c + 1))
                        act.activation(HS.high[:, slot, c, :], HC[:, c, :], ACT.Copy).then_inc(m_high, 1)

                def take_rh(i):
                    act.wait_ge(rh_made, at(i, 1, 1))
                    wait(act, logits_made, at(i, 1, 0))
                    act.activation(RH[:, :], banks[7][:, :], ACT.Relu, bias=RB1[:, 0:1]).then_inc(rh_taken, 1)

                def hidden1(i, e):
                    wait(act, a1_split, at(i, E_L, e * CH))
                    for m in range(CH):
                        act.wait_ge(l1_made, at(i, E_L, e * CH + m + 1))
                        act.activation(A1[:, m, :], banks[m][:, :], ACT.Relu, bias=B1[:, e, m:m + 1]).then_inc(l1_taken, 1)
                    wait(act, l2_made, at(i, E_L, e * CH))
                    for m in range(CH):
                        act.wait_ge(l1_taken, at(i, E_L, e * CH + m + 1))
                        act.activation(A1S.high[:, m, :], A1[:, m, :], ACT.Copy).then_inc(a1_high, 1)

                def hidden2_high(i, e):
                    wait(act, l3_made, at(i, E6, e))
                    for m in range(CH):
                        act.wait_ge(l2_taken, at(i, E_L, e * CH + m + 1))
                        act.activation(A2S.high[:, m, :], A2[:, m, :], ACT.Copy).then_inc(a2_high, 1)

                def chunk(i, slot, first=False, final=False):
                    for e in range(E6):
                        hidden1(i, e)
                        if e == 3 and not final: take_turned(i + 1, 0)
                        if e == 4 and not final: take_rh(i + 1)
                        if e == 0: exp(i, 2)
                        if e >= 1:
                            hidden2_high(i, e - 1)
                        elif not first:
                            hidden2_high(i - 1, E6 - 1)
                        if e == 3 and not final:
                            take_turned(i + 1, 1)
                            tokens_high(i + 1, 1 - slot)
                        if e == 5 and not final: exp(i + 1, 1)
                        if first and e + 2 < E6: weights_high(e + 2)
                    if final: hidden2_high(i, E6 - 1)

                take_turned(0, 0)
                take_turned(0, 1)
                tokens_high(0, 0)
                take_rh(0)
                exp(0, 1)
                weights_high(0)
                weights_high(1)
                chunk(0, 0, first=True)
                chunk(1, 1)
                if PAIRS2 > 2:
                    with act.Fori(1, PAIRS2 - 1) as j:
                        for k in range(2):
                            chunk(2 * j + k, k)
                chunk(CHUNKS - 2, 0)
                chunk(CHUNKS - 1, 1, final=True)

            @block.vector
            def _(dve):
                rstep, wstep, nstep = Steps(dve, route_chain, 11), Steps(dve, weigh_chain, 4), Steps(dve, norm_chain, 4)
                dve.wait_ge(w_loads, 16 * WLOADS)

                def six(ap):
                    return ap.unsqueeze(2).to_broadcast([P, TT, E6])

                def softmax_logits(i):
                    rstep.start(i)
                    dve.wait_ge(logits_made, at(i, 1, 1))
                    rstep(dve.tensor_tensor(LG[:, :, :], banks[7][:, 0:TT * E6].rearrange("p (k e) -> p k e", e=E6),
                                           RB2[:, :].unsqueeze(1).to_broadcast([P, TT, E6]), ALU.add))
                    rstep(dve.tensor_reduce(l_mx[:, :], LG[:, :, :], AX.X, ALU.max))
                    dve.tensor_tensor(EL[:, :, :], LG[:, :, :], six(l_mx[:, :]), ALU.subtract).then_inc(rt_shifted, 1)
                    dve.wait_ge(rt_exped, at(i, 2, 1))
                    rstep(dve.tensor_reduce(l_den[:, :], EL[:, :, :], AX.X, ALU.add))
                    rstep(dve.reciprocal(l_den[:, :], l_den[:, :]))
                    rstep(dve.tensor_tensor(PB_[:, :, :], EL[:, :, :], six(l_den[:, :]), ALU.mult))

                def choose(i):
                    mine = PB_[:, :, :].unsqueeze(3).to_broadcast([P, TT, E6, E6])
                    other = PB_[:, :, :].unsqueeze(2).to_broadcast([P, TT, E6, E6])
                    first = before[:, :, :].unsqueeze(1).to_broadcast([P, TT, E6, E6])
                    rstep(dve.tensor_tensor(gt[:, :, :, :], other, mine, ALU.is_gt))
                    rstep(dve.tensor_tensor(eq[:, :, :, :], other, mine, ALU.is_equal))
                    rstep(dve.tensor_tensor(eq[:, :, :, :], eq[:, :, :, :], first, ALU.mult))
                    rstep(dve.tensor_tensor(gt[:, :, :, :], gt[:, :, :, :], eq[:, :, :, :], ALU.add))
                    rstep(dve.tensor_reduce(rank[:, :, :], gt[:, :, :, :], AX.X, ALU.add))
                    rstep(dve.tensor_reduce(l_mx[:, :], PB_[:, :, :], AX.X, ALU.max))
                    dve.tensor_tensor(EL[:, :, :], PB_[:, :, :], six(l_mx[:, :]), ALU.subtract).then_inc(rt_shifted, 1)
                    rstep.finish()

                def weigh(i, slot):
                    wstep.start(i)
                    dve.wait_ge(rt_exped, at(i, 2, 2))
                    wstep(dve.tensor_scalar(rank[:, :, :], rank[:, :, :], 1.5, None, ALU.is_lt))
                    wstep(dve.tensor_tensor(EL[:, :, :], EL[:, :, :], rank[:, :, :], ALU.mult))
                    wstep(dve.tensor_reduce(l_den[:, :], EL[:, :, :], AX.X, ALU.add))
                    wstep(dve.reciprocal(l_den[:, :], l_den[:, :]))
                    dve.tensor_tensor(PX[:, slot, :, :], EL[:, :, :], six(l_den[:, :]), ALU.mult).then_inc(wt_ready, 1)
                    wstep.finish()

                def take_l2(i, e):
                    wait(dve, a2_split, at(i, E_L, e * CH))
                    for m in range(CH):
                        dve.wait_ge(l2_made, at(i, E_L, e * CH + m + 1))
                        dve.tensor_scalar(A2[:, m, :], banks[2 + m][:, :], B2[:, e, m:m + 1], 0.0,
                                          ALU.add, ALU.max).then_inc(l2_taken, 1)

                def hidden2_low(i, e):
                    for m in range(CH):
                        dve.wait_ge(a2_high, at(i, E_L, e * CH + m + 1))
                        dve.tensor_tensor(A2S.low[:, m, :], A2[:, m, :], A2S.high[:, m, :], ALU.subtract).then_inc(a2_split, 1)

                def weights_low(e):
                    for n in range(3):
                        dve.wait_ge(w_high, 3 * e + n + 1)
                        dve.tensor_tensor(WS.low[:, e, n, :, :], W[:, e, n, :, :], WS.high[:, e, n, :, :],
                                          ALU.subtract).then_inc(w_split, 1)

                def take_route(i):
                    dve.wait_ge(wt_turned, at(i, 1, 1))
                    dve.tensor_copy(WTT[:, :, :], banks[7][0:E6, :].rearrange("e (k p) -> e k p", p=P)).then_inc(wt_taken, 1)

                def take_b3(i, slot):
                    dve.wait_ge(b3_made, at(i, 1, 1))
                    wait(dve, f_ready, at(i, 1, -1))
                    for b in range(TT // 2):
                        last = dve.tensor_tensor(ACC[:, slot, 2 * b:2 * b + 2, :], halved(4 + b), HTOK[:, slot, 2 * b:2 * b + 2, :], ALU.add)
                    last.then_inc(l3_taken, 1)

                def take_l3(i, e, slot):
                    dve.wait_ge(l3_made, at(i, E6, e + 1))
                    dve.wait_ge(l3_taken, at(i, E6 + 1, e + 1))
                    for k in range(TT):
                        last = dve.scalar_tensor_tensor(ACC[:, slot, k, :], halved(4 + k // 2)[:, k % 2, :], PX[:, slot, k, e:e + 1],
                                                        ACC[:, slot, k, :], ALU.mult, ALU.add)
                        if e == 0 and k == 0:
                            last.then_inc(tok_free, 1)
                    last.then_inc(l3_taken, 1)

                def norm(i, slot):
                    nstep.start(i)
                    dve.wait_ge(l3_taken, at(i, E6 + 1, E6 + 1))
                    layer_stats(dve, ACC[:, slot, :, :], TT, fst, fmv, nstep, f_var)
                    nstep.finish()
                    dve.wait_ge(f_rstd, at(i, 1, 1))
                    wait(dve, out_stored, at(i, 16, 0))
                    for k in range(TT):
                        last = dve.tensor_scalar(OUT[:, k, :], ACC[:, slot, k, :], fmv[:, k, 0:1], frstd[:, k:k + 1],
                                                 ALU.subtract, ALU.mult)
                    last.then_inc(f_ready, 1)

                def chunk(i, slot, first=False, final=False):
                    for e in range(E6):
                        if e == 1: take_route(i)
                        if e == 2: take_b3(i, slot)
                        if e >= 1:
                            take_l2(i, e - 1)
                        elif not first:
                            take_l2(i - 1, E6 - 1)
                        if e >= 2:
                            take_l3(i, e - 2, slot)
                        elif not first:
                            take_l3(i - 1, e + E6 - 2, 1 - slot)
                        if e == 0: weigh(i, slot)
                        if e >= 1:
                            hidden2_low(i, e - 1)
                        elif not first:
                            hidden2_low(i - 1, E6 - 1)
                        if e == 2 and not first: norm(i - 1, 1 - slot)
                        if first and e + 2 < E6: weights_low(e + 2)
                    if not final:
                        softmax_logits(i + 1)
                        choose(i + 1)
                    else:
                        take_l3(i, E6 - 2, slot)
                        take_l2(i, E6 - 1)
                        hidden2_low(i, E6 - 1)
                        take_l3(i, E6 - 1, slot)
                        norm(i, slot)

                softmax_logits(0)
                choose(0)
                weights_low(0)
                weights_low(1)
                chunk(0, 0, first=True)
                chunk(1, 1)
                if PAIRS2 > 2:
                    with dve.Fori(1, PAIRS2 - 1) as j:
                        for k in range(2):
                            chunk(2 * j + k, k)
                chunk(CHUNKS - 2, 0)
                chunk(CHUNKS - 1, 1, final=True)

            @block.gpsimd
            def _(pool):
                def low(split, at_, whole_, high, value, signal):
                    pool.wait_ge(high, value)
                    pool.tensor_tensor(split.low[at_], whole_, split.high[at_], ALU.subtract).then_inc(signal, 1)

                def tokens_low(i, slot):
                    for c in range(CH):
                        low(HS, (slice(None), slot, c, slice(None)), HC[:, c, :], m_high, at(i, CH, c + 1), m_split)

                def hidden1_low(i, e):
                    for m in range(CH):
                        low(A1S, (slice(None), m, slice(None)), A1[:, m, :], a1_high, at(i, E_L, e * CH + m + 1), a1_split)

                def rstd(i):
                    pool.wait_ge(f_var, at(i, 1, 1))
                    wait(pool, f_ready, at(i, 1, 0))
                    pool.tensor_tensor(frstd[:, :], fmv[:, :, 1], halves[:, 0:TT], ALU.pow).then_inc(f_rstd, 1)

                def chunk(i, slot, first=False, final=False):
                    for e in range(E6):
                        hidden1_low(i, e)
                        if e == 2 and not first: rstd(i - 1)
                        if e == 3 and not final: tokens_low(i + 1, 1 - slot)
                    if final: rstd(i)

                tokens_low(0, 0)
                chunk(0, 0, first=True)
                chunk(1, 1)
                if PAIRS2 > 2:
                    with pool.Fori(1, PAIRS2 - 1) as j:
                        for k in range(2):
                            chunk(2 * j + k, k)
                chunk(CHUNKS - 2, 0)
                chunk(CHUNKS - 1, 1, final=True)


def kernel(**inputs):
    import numpy as np
    import concourse.bacc as bacc
    from concourse.bass_utils import run_bass_kernel_spmd

    arrays, aps = prepare(inputs, np, bacc)
    nc = aps.pop("nc")
    build(nc, **aps)
    r = run_bass_kernel_spmd(nc, [arrays], core_ids=[0])
    return r.results[0]["out_dram"]


def prepare(inputs, np, bacc):
    def t(name):
        return np.ascontiguousarray(np.asarray(inputs[name]).T)

    def a(name):
        return np.ascontiguousarray(inputs[name])

    x = a("x")
    n, c, h, w = x.shape
    x = np.ascontiguousarray(x.reshape(n, c, h // STRIDE, STRIDE, w // STRIDE, STRIDE).transpose(0, 1, 2, 4, 3, 5)).reshape(
        n, c, -1, STRIDE ** 2)
    p = np.arange(P)
    sh = (np.arange(64) // HEADS)[None, :] == (p // STRIDE ** 2)[:, None]
    hm = np.arange(4)[None, :] == (p // 32)[:, None]
    before = np.broadcast_to((np.arange(EXPERTS)[None, :] < np.arange(EXPERTS)[:, None]).ravel(), (P, EXPERTS ** 2))
    head = np.arange(4)[None, :, None, None]
    is_channel = (p[:, None, None, None] == 32 * head + p % 32)
    quarter = p // 32
    parts = [np.stack([quarter < 2, quarter >= 2]), np.stack([quarter % 2 == 0, quarter % 2 == 1])]
    sel = np.stack([is_channel & part[None, None] for part in parts], axis=1)
    data = {
        "x": x, "wq_t": t("L0_tok_Wq"), "wkv": a("L0_tok_Wkv"), "proj_t": t("L0_tok_proj_w"),
        "wqkv_t": t("L0_attn_W_qkv"), "wgate_t": t("L0_attn_W_gate"), "wfinal_t": t("L0_attn_W_final"),
        "vecs": np.stack([a(n) for n in VECS]), "ident_in": np.eye(P, dtype=np.float32),
        "masks_in": np.concatenate([sh, hm, before], axis=1).astype(np.float32),
        "sel_in": sel.astype(np.float32),
        "rw1": a("L0_ffn_router_w1"), "rb1": a("L0_ffn_router_b1"), "rw2": a("L0_ffn_router_w2"), "rb2": a("L0_ffn_router_b2"),
        "ew1": a("L0_ffn_expert_w1"), "eb1": a("L0_ffn_expert_b1"), "ew2": a("L0_ffn_expert_w2"), "eb2": a("L0_ffn_expert_b2"),
        "ew3": a("L0_ffn_expert_w3"), "eb3": a("L0_ffn_expert_b3"),
    }
    nc = bacc.Bacc("TRN2", target_bir_lowering=False, num_devices=1)
    arrays, aps = {}, {"nc": nc}
    for name, value in data.items():
        arrays[f"in_{name}"] = value
        aps[name] = nc.dram_tensor(f"in_{name}", value.shape, mybir.dt.from_np(value.dtype), kind="ExternalInput").ap()
    aps["out"] = nc.dram_tensor("out_dram", (n, (h // STRIDE) ** 2, c), F32, kind="ExternalOutput").ap()
    return arrays, aps
```
